# Optimizing a Trainium2 kernel written in Bass

```python
import numpy as np
import jax
import jax.numpy as jnp

def _softmax(x, axis=-1):
    return jax.nn.softmax(x, axis=axis)

def _gelu(x):
    return jax.nn.gelu(x, approximate=True)

def _silu(x):
    return jax.nn.silu(x)

def _sigmoid(x):
    return jax.nn.sigmoid(x)

def _layernorm(x, axis=-1, eps=1e-05):
    m = jnp.mean(x, axis=axis, keepdims=True)
    v = jnp.var(x, axis=axis, keepdims=True)
    return (x - m) / jnp.sqrt(v + eps)

def _scatter_add(tgt, idx, src, axis=0):
    return tgt.at[idx].add(src)

def _segment_sum(src, seg, n):
    return jax.ops.segment_sum(src, seg, n)
kernel_name = 'mk_xattn_ffn_d2_seqx_r4_ea508a'

def setup_inputs(seed: int=0):
    np.random.seed(seed)
    _w = jnp.asarray

    def _rec_inputs():
        import jax
        import jax.numpy as jnp
        _rk = jax.random.key(seed)
        x = -0.000125 + 0.9999 * jax.random.normal(jax.random.fold_in(_rk, 1), (8, 256, 512), jnp.float32)
        _lenS = 256 - jax.random.randint(jax.random.fold_in(_rk, 7), (8,), 0, max(1, 256 // 4) + 1, jnp.int32)
        _lenS2 = 256 - jax.random.randint(jax.random.fold_in(_rk, 8), (8,), 0, max(1, 256 // 4) + 1, jnp.int32)
        _ctx_2048P = jax.random.normal(jax.random.fold_in(_rk, 11), (8, 16, 512), jnp.float32)
        _ctx_2048c = jax.random.dirichlet(jax.random.fold_in(_rk, 511), 0.3 * jnp.ones((16,), jnp.float32), (8, 256))
        _ctx_2048t = jnp.einsum('bsk,bkd->bsd', _ctx_2048c, _ctx_2048P)
        _ctx_2048t = _ctx_2048t * jax.lax.rsqrt(jnp.mean(jnp.square(_ctx_2048t)) + 1e-12) * 0.953939
        ctx_2048 = 1.72703e-05 + 1.00003 * (_ctx_2048t + 0.3 * jax.random.normal(jax.random.fold_in(_rk, 611), (8, 256, 512), jnp.float32))
        _validS = jnp.arange(256)[None, :] < _lenS[:, None]
        _validS2 = jnp.arange(256)[None, :] < _lenS2[:, None]
        _causal = jnp.tril(jnp.ones((256, 256), dtype=bool))
        mask_BxS2_bk0 = jnp.logical_not(jnp.broadcast_to(_validS2[:, :], (8, 256)))
        return (x, ctx_2048, mask_BxS2_bk0)
    x, ctx_2048, mask_BxS2_bk0 = _rec_inputs()

    def _L0_xattn_setup():
        import jax, jax.numpy as jnp
        import numpy as np
        DIM = 512
        NH = 16
        HD = DIM // NH
        EPS = 1e-06
        IMG_LEN = 257

        def rms_norm(x, w, eps=EPS):
            xf = x.astype(jnp.float32)
            y = xf * jax.lax.rsqrt(jnp.mean(xf * xf, axis=-1, keepdims=True) + eps)
            return y.astype(x.dtype) * w

        def linear(x, w, b):
            return jnp.einsum('blc,oc->blo', x, w) + b

        def attention(q, k, v):
            scale = 1.0 / jnp.sqrt(jnp.asarray(HD, q.dtype))
            scores = jnp.einsum('bqhd,bkhd->bhqk', q, k) * scale
            probs = jax.nn.softmax(scores, axis=-1)
            return jnp.einsum('bhqk,bkhd->bqhd', probs, v)
        key = jax.random.key(seed)
        ks = jax.random.split(key, 12)
        B, L = (2, 2048)
        s = 0.02
        inp = {'x': jax.random.normal(ks[0], (B, L, DIM), jnp.float32), 'context': jax.random.normal(ks[1], (B, 769, DIM), jnp.float32), 'q_w': jax.random.normal(ks[2], (DIM, DIM), jnp.float32) * s, 'q_b': jnp.zeros((DIM,), jnp.float32), 'k_w': jax.random.normal(ks[3], (DIM, DIM), jnp.float32) * s, 'k_b': jnp.zeros((DIM,), jnp.float32), 'v_w': jax.random.normal(ks[4], (DIM, DIM), jnp.float32) * s, 'v_b': jnp.zeros((DIM,), jnp.float32), 'k_img_w': jax.random.normal(ks[5], (DIM, DIM), jnp.float32) * s, 'k_img_b': jnp.zeros((DIM,), jnp.float32), 'v_img_w': jax.random.normal(ks[6], (DIM, DIM), jnp.float32) * s, 'v_img_b': jnp.zeros((DIM,), jnp.float32), 'o_w': jax.random.normal(ks[7], (DIM, DIM), jnp.float32) * s, 'o_b': jnp.zeros((DIM,), jnp.float32), 'norm_q_w': jnp.ones((DIM,), jnp.float32), 'norm_k_w': jnp.ones((DIM,), jnp.float32), 'norm_k_img_w': jnp.ones((DIM,), jnp.float32)}
        return inp
    _L0_xattn_all = _L0_xattn_setup()
    _L0_xattn_in = {k: v for k, v in _L0_xattn_all.items() if k in ('q_w', 'q_b', 'k_w', 'k_b', 'v_w', 'v_b', 'k_img_w', 'k_img_b', 'v_img_w', 'v_img_b', 'o_w', 'o_b', 'norm_q_w', 'norm_k_w', 'norm_k_img_w')}
    del _L0_xattn_all

    def _L0_ffn_setup():
        import jax, jax.numpy as jnp
        import numpy as np
        B, S, H = (2, 512, 512)
        E, K, I = (64, 8, 192)

        def _moe_forward(hidden_states, gate_weight, w_gate, w_up, w_down):
            b, s, h = hidden_states.shape
            x = hidden_states.reshape(-1, h)
            logits = x.astype(jnp.float32) @ gate_weight.astype(jnp.float32).T
            scores = jax.nn.softmax(logits, axis=-1)
            topk_w, topk_idx = jax.lax.top_k(scores, K)
            topk_w = topk_w / jnp.sum(topk_w, axis=-1, keepdims=True)
            flat_ids = topk_idx.reshape(-1)
            expanded = jnp.repeat(x, K, axis=0)
            order = jnp.argsort(flat_ids)
            sorted_tokens = expanded[order]
            group_sizes = jnp.zeros((E,), jnp.int32).at[flat_ids].add(1)
            g = jax.lax.ragged_dot(sorted_tokens, w_gate, group_sizes)
            u = jax.lax.ragged_dot(sorted_tokens, w_up, group_sizes)
            out = jax.lax.ragged_dot(jax.nn.silu(g) * u, w_down, group_sizes)
            inv = jnp.argsort(order)
            outs = out[inv].reshape(-1, K, h)
            y = jnp.sum(outs * topk_w[:, :, None], axis=1)
            return y.reshape(b, s, h)
        key = jax.random.key(seed)
        k0, k1, k2, k3, k4 = jax.random.split(key, 5)
        hidden_states = jax.random.normal(k0, (B, S, H), dtype=jnp.float32)
        gate_weight = jax.random.normal(k1, (E, H), dtype=jnp.float32) * 0.02
        w_gate = jax.random.normal(k2, (E, H, I), dtype=jnp.float32) * 0.02
        w_up = jax.random.normal(k3, (E, H, I), dtype=jnp.float32) * 0.02
        w_down = jax.random.normal(k4, (E, I, H), dtype=jnp.float32) * 0.02
        return {'hidden_states': hidden_states, 'gate_weight': gate_weight, 'w_gate': w_gate, 'w_up': w_up, 'w_down': w_down}
    _L0_ffn_all = _L0_ffn_setup()
    _L0_ffn_in = {k: v for k, v in _L0_ffn_all.items() if k in ('gate_weight', 'w_gate', 'w_up', 'w_down')}
    del _L0_ffn_all

    def _L1_xattn_setup():
        import jax, jax.numpy as jnp
        import numpy as np
        key = jax.random.key(seed)
        k1, k2, k3 = jax.random.split(key, 3)
        B, S, D, M = (8, 512, 512, 128)
        hidden_states = jax.random.normal(k1, (B, S, D), dtype=jnp.float32)
        memory_tokens = jax.random.normal(k2, (B, M, D), dtype=jnp.float32)
        memory_mask = jax.random.randint(k3, (B, M), 0, 2).astype(jnp.bool_)
        return {'hidden_states': hidden_states, 'memory_tokens': memory_tokens, 'memory_mask': memory_mask}
    _L1_xattn_all = _L1_xattn_setup()
    _L1_xattn_in = {k: v for k, v in _L1_xattn_all.items() if k in ()}
    del _L1_xattn_all

    def _L1_ffn_setup():
        import jax, jax.numpy as jnp
        import numpy as np
        HIDDEN = 512
        INTER = 1408
        B, S = (2, 512)

        def _ternary(key, shape):
            return jax.random.randint(key, shape, -1, 2).astype(jnp.float32)
        key = jax.random.key(seed)
        ks = jax.random.split(key, 7)
        x = jax.random.normal(ks[0], (B, S, HIDDEN), dtype=jnp.float32)
        gate_w = _ternary(ks[1], (INTER, HIDDEN))
        up_w = _ternary(ks[2], (INTER, HIDDEN))
        down_w = _ternary(ks[3], (HIDDEN, INTER))
        gate_s = jax.random.uniform(ks[4], (INTER,), minval=0.01, maxval=0.1, dtype=jnp.float32)
        up_s = jax.random.uniform(ks[5], (INTER,), minval=0.01, maxval=0.1, dtype=jnp.float32)
        down_s = jax.random.uniform(ks[6], (HIDDEN,), minval=0.01, maxval=0.1, dtype=jnp.float32)
        return {'x': x, 'gate_w': gate_w, 'up_w': up_w, 'down_w': down_w, 'gate_s': gate_s, 'up_s': up_s, 'down_s': down_s}
    _L1_ffn_all = _L1_ffn_setup()
    _L1_ffn_in = {k: v for k, v in _L1_ffn_all.items() if k in ('gate_w', 'up_w', 'down_w', 'gate_s', 'up_s', 'down_s')}
    del _L1_ffn_all
    return {'x': x, 'ctx_2048': ctx_2048, 'mask_BxS2_bk0': mask_BxS2_bk0, 'L0_xattn_q_w': _L0_xattn_in['q_w'], 'L0_xattn_q_b': _L0_xattn_in['q_b'], 'L0_xattn_k_w': _L0_xattn_in['k_w'], 'L0_xattn_k_b': _L0_xattn_in['k_b'], 'L0_xattn_v_w': _L0_xattn_in['v_w'], 'L0_xattn_v_b': _L0_xattn_in['v_b'], 'L0_xattn_k_img_w': _L0_xattn_in['k_img_w'], 'L0_xattn_k_img_b': _L0_xattn_in['k_img_b'], 'L0_xattn_v_img_w': _L0_xattn_in['v_img_w'], 'L0_xattn_v_img_b': _L0_xattn_in['v_img_b'], 'L0_xattn_o_w': _L0_xattn_in['o_w'], 'L0_xattn_o_b': _L0_xattn_in['o_b'], 'L0_xattn_norm_q_w': _L0_xattn_in['norm_q_w'], 'L0_xattn_norm_k_w': _L0_xattn_in['norm_k_w'], 'L0_xattn_norm_k_img_w': _L0_xattn_in['norm_k_img_w'], 'L0_ffn_gate_weight': _L0_ffn_in['gate_weight'], 'L0_ffn_w_gate': _L0_ffn_in['w_gate'], 'L0_ffn_w_up': _L0_ffn_in['w_up'], 'L0_ffn_w_down': _L0_ffn_in['w_down'], 'L1_ffn_gate_w': _L1_ffn_in['gate_w'], 'L1_ffn_up_w': _L1_ffn_in['up_w'], 'L1_ffn_down_w': _L1_ffn_in['down_w'], 'L1_ffn_gate_s': _L1_ffn_in['gate_s'], 'L1_ffn_up_s': _L1_ffn_in['up_s'], 'L1_ffn_down_s': _L1_ffn_in['down_s']}

def reference(x, ctx_2048, mask_BxS2_bk0, L0_xattn_q_w, L0_xattn_q_b, L0_xattn_k_w, L0_xattn_k_b, L0_xattn_v_w, L0_xattn_v_b, L0_xattn_k_img_w, L0_xattn_k_img_b, L0_xattn_v_img_w, L0_xattn_v_img_b, L0_xattn_o_w, L0_xattn_o_b, L0_xattn_norm_q_w, L0_xattn_norm_k_w, L0_xattn_norm_k_img_w, L0_ffn_gate_weight, L0_ffn_w_gate, L0_ffn_w_up, L0_ffn_w_down, L1_ffn_gate_w, L1_ffn_up_w, L1_ffn_down_w, L1_ffn_gate_s, L1_ffn_up_s, L1_ffn_down_s):
    import jax
    import jax.numpy as jnp

    def _L0_xattn_ref(x, context, q_w, q_b, k_w, k_b, v_w, v_b, k_img_w, k_img_b, v_img_w, v_img_b, o_w, o_b, norm_q_w, norm_k_w, norm_k_img_w):
        import jax, jax.numpy as jnp
        import numpy as np
        DIM = 512
        NH = 16
        HD = DIM // NH
        EPS = 1e-06
        IMG_LEN = 257

        def rms_norm(x, w, eps=EPS):
            xf = x.astype(jnp.float32)
            y = xf * jax.lax.rsqrt(jnp.mean(xf * xf, axis=-1, keepdims=True) + eps)
            return y.astype(x.dtype) * w

        def linear(x, w, b):
            return jnp.einsum('blc,oc->blo', x, w) + b

        def attention(q, k, v):
            scale = 1.0 / jnp.sqrt(jnp.asarray(HD, q.dtype))
            scores = jnp.einsum('bqhd,bkhd->bhqk', q, k) * scale
            probs = jax.nn.softmax(scores, axis=-1)
            return jnp.einsum('bhqk,bkhd->bqhd', probs, v)
        B, L, _ = x.shape
        ctx_img = context[:, :IMG_LEN]
        ctx_txt = context[:, IMG_LEN:]
        q = rms_norm(linear(x, q_w, q_b), norm_q_w).reshape(B, L, NH, HD)
        k = rms_norm(linear(ctx_txt, k_w, k_b), norm_k_w).reshape(B, -1, NH, HD)
        v = linear(ctx_txt, v_w, v_b).reshape(B, -1, NH, HD)
        k_img = rms_norm(linear(ctx_img, k_img_w, k_img_b), norm_k_img_w).reshape(B, -1, NH, HD)
        v_img = linear(ctx_img, v_img_w, v_img_b).reshape(B, -1, NH, HD)
        img_x = attention(q, k_img, v_img)
        txt_x = attention(q, k, v)
        out = (txt_x + img_x).reshape(B, L, DIM)
        return linear(out, o_w, o_b)

    def _L0_ffn_ref(hidden_states, gate_weight, w_gate, w_up, w_down):
        import jax, jax.numpy as jnp
        import numpy as np
        B, S, H = (2, 512, 512)
        E, K, I = (64, 8, 192)

        def _moe_forward(hidden_states, gate_weight, w_gate, w_up, w_down):
            b, s, h = hidden_states.shape
            x = hidden_states.reshape(-1, h)
            logits = x.astype(jnp.float32) @ gate_weight.astype(jnp.float32).T
            scores = jax.nn.softmax(logits, axis=-1)
            topk_w, topk_idx = jax.lax.top_k(scores, K)
            topk_w = topk_w / jnp.sum(topk_w, axis=-1, keepdims=True)
            flat_ids = topk_idx.reshape(-1)
            expanded = jnp.repeat(x, K, axis=0)
            order = jnp.argsort(flat_ids)
            sorted_tokens = expanded[order]
            group_sizes = jnp.zeros((E,), jnp.int32).at[flat_ids].add(1)
            g = jax.lax.ragged_dot(sorted_tokens, w_gate, group_sizes)
            u = jax.lax.ragged_dot(sorted_tokens, w_up, group_sizes)
            out = jax.lax.ragged_dot(jax.nn.silu(g) * u, w_down, group_sizes)
            inv = jnp.argsort(order)
            outs = out[inv].reshape(-1, K, h)
            y = jnp.sum(outs * topk_w[:, :, None], axis=1)
            return y.reshape(b, s, h)
        return _moe_forward(hidden_states, gate_weight, w_gate, w_up, w_down)

    def _L1_xattn_ref(hidden_states, memory_tokens, memory_mask):
        import jax, jax.numpy as jnp
        import numpy as np
        B, S, D = hidden_states.shape
        scale = 1.0 / jnp.sqrt(jnp.asarray(D, hidden_states.dtype))
        scores = jnp.einsum('bsd,bmd->bsm', hidden_states, memory_tokens) * scale
        neg_inf = jnp.asarray(-1e+30, scores.dtype)
        scores = jnp.where(memory_mask[:, None, :], scores, neg_inf)
        attn = jax.nn.softmax(scores, axis=-1)
        readout = jnp.einsum('bsm,bmd->bsd', attn, memory_tokens)
        valid_b = jnp.any(memory_mask, axis=-1)
        out = jnp.where(valid_b[:, None, None], readout, jnp.zeros_like(readout))
        return out

    def _L1_ffn_ref(x, gate_w, up_w, down_w, gate_s, up_s, down_s):
        import jax, jax.numpy as jnp
        import numpy as np
        HIDDEN = 512
        INTER = 1408
        B, S = (2, 512)

        def _ternary(key, shape):
            return jax.random.randint(key, shape, -1, 2).astype(jnp.float32)
        b, s, h = x.shape
        xf = x.reshape(b * s, h)
        g = jnp.einsum('th,ih->ti', xf, gate_w) * gate_s
        u = jnp.einsum('th,ih->ti', xf, up_w) * up_s
        hdn = jax.nn.silu(g) * u
        out = jnp.einsum('ti,hi->th', hdn, down_w) * down_s
        return out.reshape(b, s, -1)
    x = x + _L0_xattn_ref(_layernorm(x, axis=-1), ctx_2048, L0_xattn_q_w, L0_xattn_q_b, L0_xattn_k_w, L0_xattn_k_b, L0_xattn_v_w, L0_xattn_v_b, L0_xattn_k_img_w, L0_xattn_k_img_b, L0_xattn_v_img_w, L0_xattn_v_img_b, L0_xattn_o_w, L0_xattn_o_b, L0_xattn_norm_q_w, L0_xattn_norm_k_w, L0_xattn_norm_k_img_w)
    x = x + _L0_ffn_ref(_layernorm(x, axis=-1), L0_ffn_gate_weight, L0_ffn_w_gate, L0_ffn_w_up, L0_ffn_w_down)
    x = x + _L1_xattn_ref(_layernorm(x, axis=-1), ctx_2048, mask_BxS2_bk0)
    x = x + _L1_ffn_ref(_layernorm(x, axis=-1), L1_ffn_gate_w, L1_ffn_up_w, L1_ffn_down_w, L1_ffn_gate_s, L1_ffn_up_s, L1_ffn_down_s)
    return x

_drawn_inputs = setup_inputs


def setup_inputs(seed=0):
    import zlib

    import numpy as np

    out = dict(_drawn_inputs(seed))
    spreads = {'L0_xattn_q_b': (0.0, 0.8),
     'L0_xattn_k_b': (0.0, 0.1),
     'L0_xattn_v_b': (0.0, 0.1),
     'L0_xattn_k_img_b': (0.0, 0.8),
     'L0_xattn_v_img_b': (0.0, 0.1),
     'L0_xattn_o_b': (0.0, 0.1),
     'L0_xattn_norm_q_w': (1.0, 0.6),
     'L0_xattn_norm_k_w': (1.0, 0.2),
     'L0_xattn_norm_k_img_w': (1.0, 0.6)}
    factors = {'L0_ffn_gate_weight': 4.615,
     'L0_ffn_w_gate': 4.261,
     'L0_ffn_w_up': 4.177,
     'L0_ffn_w_down': 4.16}
    for name, (base, spread) in spreads.items():
        noise = np.random.default_rng([zlib.crc32(name.encode()), seed]).standard_normal(out[name].shape)
        drawn = base * np.exp(spread * noise) if base else spread * noise
        out[name] = jnp.asarray(drawn.astype(out[name].dtype))
    for name, factor in factors.items():
        out[name] = (out[name] * factor).astype(out[name].dtype)
    return out
```

```python
from contextlib import ExitStack

import numpy as np
import concourse.bass as bass
from concourse import mybir

F32 = mybir.dt.float32
F16 = mybir.dt.float16
I32 = mybir.dt.int32
U32 = mybir.dt.uint32
U8 = mybir.dt.uint8
ALU = mybir.AluOpType
ACT = mybir.ActivationFunctionType
AX = mybir.AxisListType

P = 128
B, S, D = 8, 256, 512
T = B * S
NT = T // P
TPB = S // P
DC = D // P
NH, HD = 16, 32
HG = P // HD
E, K, I = 64, 8, 192
NBLK = T * K // P + E
IH = I // 2
NWB = 4
F, FC = 1408, 1408 // P
LN_EPS, RMS_EPS = 1e-5, 1e-6
SLOT_TOP = 65536.0


class Steps:

    def __init__(self, nc, ctx, name, names, lag=4):
        self.sem, self.names, self.lag, self.at = ctx.enter_context(nc.semaphore(name)), names, lag, 0

    def start(self, eng):
        eng.sem_inc(self.sem, self.lag * len(self.names))

    def done(self, ins, name):
        assert self.names[self.at] == name, (self.names[self.at], name)
        self.at = (self.at + 1) % len(self.names)
        ins.then_inc(self.sem, 1)

    def value(self, unit, name):
        return (unit + self.lag) * len(self.names) + self.names.index(name) + 1

    def wait(self, eng, unit, name):
        eng.wait_ge(self.sem, self.value(unit, name))


def apart(eng, sem):
    eng.sem_inc(sem, 1)


class Chain:

    def __init__(self, nc, ctx, name, eng=None):
        self.sem, self.n, self.eng = ctx.enter_context(nc.semaphore(name)), 0, eng

    def __call__(self, ins):
        self.n += 1
        ins.then_inc(self.sem, 1)
        self.eng.wait_ge(self.sem, self.n)


def project(nc, x_in, ctxT_in, wT_in, rows_in, X, qT, kT, V, ident):
    with ExitStack() as ctx:
        sb = lambda name, shape, dt=F32: ctx.enter_context(nc.sbuf_tensor(name, shape, dt))
        ps = lambda name, shape, dt=F32: ctx.enter_context(nc.psum_tensor(name, shape, dt))
        sem = lambda name: ctx.enter_context(nc.semaphore(name))
        W = sb("proj_w", [P, 3, DC, D])
        rows = sb("proj_rows", [P, 5, D])
        ctxT = sb("ctxT", [P, 2, DC, P])
        stats, mv = sb("ln1_stats", [P, NT, 6]), sb("ln1_mv", [P, NT, 2])
        lnp = sb("ln1_scale_shift", [P, NT, 2])
        rstd, shift = lnp[:, :, 0], lnp[:, :, 1]
        xn, xnT = sb("xn", [P, 2, D]), sb("xnT", [P, 2, DC, P])
        xc, lnc = sb("xc", [P, D]), sb("ln1_col", [P, 2])
        kb, qb, kn, qn, sq = sb("kb", [P, D]), sb("qb", [P, D]), sb("kn", [P, D]), sb("qn", [P, D]), sb("sq", [P, D])
        kms, qms, krs, qrs = sb("kms", [P, 2]), sb("qms", [P, 2]), sb("krs", [P, 1]), sb("qrs", [P, 1])
        pxT, pk, pq, pv, pkT, pqT = [ps(n, [P, D]) for n in ("pxT", "pk", "pq", "pv", "pkT", "pqT")]
        s_x, s_w, s_rows, s_id = sem("p_x"), [sem(f"p_w{i}") for i in range(3)], sem("p_rows"), sem("p_id")
        s_c = [sem(f"p_c{i}") for i in range(2)]
        s_apart = sem("p_apart")
        eps, s_eps = sb("rms_eps", [P, 1]), sem("p_eps")
        s_mv, s_sd, s_ln = sem("p_mv"), sem("p_sd"), sem("p_ln")
        pe = Steps(nc, ctx, "p_pe", ["xT", "k", "q", "v", "kT", "qT"])
        dve = Steps(nc, ctx, "p_dve", ["xT", "kb", "qb", "kr", "kn", "qr", "qn", "vb"])
        act = Steps(nc, ctx, "p_act", ["ksq", "ksd", "qsq", "qsd", "kT", "qT"])
        pool = Steps(nc, ctx, "p_pool", ["xc", "lnc", "xn"])
        block = ctx.enter_context(nc.Block())

        @block.sync
        def _(eng):
            for n in range(4):
                eng.dma_start(X[:, 4 * n:4 * n + 4, :],
                              x_in.rearrange("(n t p) d -> n p t d", p=P, t=4)[n]).then_inc(s_x, 16)
            eng.dma_start(W[:, 1, :, :], wT_in[1]).then_inc(s_w[1], 16)
            with eng.Fori(0, NT // 2) as i:
                for par in range(2):
                    t = i * 2 + par
                    pe.wait(eng, t - 2, "v")
                    eng.dma_start(ctxT[:, par, :, :], ctxT_in[t, :, :, :]).then_inc(s_c[par], 16)

        @block.scalar
        def _(eng):
            act.start(eng)
            eng.dma_start(W[:, 0, :, :], wT_in[0]).then_inc(s_w[0], 16)
            eng.dma_start(rows[:, :, :], rows_in[0:5, :].unsqueeze(0).to_broadcast([P, 5, D])).then_inc(s_rows, 16)
            eng.dma_start(W[:, 2, :, :], wT_in[2]).then_inc(s_w[2], 16)
            eng.wait_ge(s_mv, 1)
            eng.activation(rstd, mv[:, :, 1], ACT.Sqrt).then_inc(s_sd, 1)
            eng.wait_ge(s_eps, 1)
            with eng.Fori(0, NT) as t:
                for x, psum, sbuf in (("k", kb, kms), ("q", qb, qms)):
                    dve.wait(eng, t, x + "b")
                    if x == "k":
                        dve.wait(eng, t - 1, "kr")
                        dve.wait(eng, t - 1, "qr")
                    act.done(eng.activation(sq[:, :], psum[:, :], ACT.Square, accum_out=sbuf[:, 0:1]), x + "sq")
                    act.wait(eng, t, x + "sq")
                    act.done(eng.activation(sbuf[:, 1:2], sbuf[:, 0:1], ACT.Sqrt, bias=eps[:, 0:1], scale=1.0 / D), x + "sd")
                for x, psum, dst in (("k", pkT, kT), ("q", pqT, qT)):
                    pe.wait(eng, t, x + "T")
                    act.done(eng.activation(dst[:, :, bass.ts(t, P)], psum[:, :].rearrange("p (c n) -> p c n", c=DC),
                                            ACT.Copy), x + "T")

        @block.gpsimd
        def _(eng):
            pool.start(eng)
            eng.memset(ident[:, :], 0.0).then_inc(s_id, 1)
            eng.wait_ge(s_id, 1)
            eng.affine_select(out=ident[:, :], in_=ident[:, :], compare_op=ALU.not_equal, fill=1.0, base=0,
                              pattern=[[-1, P]], channel_multiplier=1).then_inc(s_id, 1)
            eng.wait_ge(s_ln, 1)
            with eng.Fori(0, NT // 2) as i:
                for par in range(2):
                    t = i * 2 + par
                    pool.wait(eng, t - 1, "xn")
                    pool.done(eng.tensor_copy(xc[:, :], X[:, t, :]), "xc")
                    pool.done(eng.tensor_copy(lnc[:, :], lnp[:, t, :]), "lnc")
                    pool.wait(eng, t, "lnc")
                    pe.wait(eng, t - 2, "xT")
                    apart(eng, s_apart)
                    pool.done(eng.tensor_scalar(xn[:, par, :], xc[:, :], lnc[:, 0:1], lnc[:, 1:2], ALU.mult, ALU.add), "xn")

        @block.tensor
        def _(eng):
            pe.start(eng)
            eng.wait_ge(s_id, 2)
            for s in s_w:
                eng.wait_ge(s, 16)
            with eng.Fori(0, NT // 2) as i:
                for par in range(2):
                    t = i * 2 + par
                    pool.wait(eng, t, "xn")
                    dve.wait(eng, t - 1, "xT")
                    for c in range(DC):
                        m = eng.transpose(pxT[:, bass.ts(c, P)], xn[:, par, bass.ts(c, P)], ident[:, :])
                    pe.done(m, "xT")
                    eng.wait_ge(s_c[par], 16 * (i + 1))
                    for x, psum, lhs, w, free in (("k", pk, ctxT, 1, "kb"), ("q", pq, xnT, 0, "qb"), ("v", pv, ctxT, 2, "vb")):
                        if x == "q":
                            dve.wait(eng, t, "xT")
                        dve.wait(eng, t - 1, free)
                        for c in range(DC):
                            m = eng.matmul(psum[:, :], lhs[:, par, c, :], W[:, w, c, :], start=c == 0, stop=c == DC - 1)
                        pe.done(m, x)
                    for x, psum, src in (("k", pkT, kn), ("q", pqT, qn)):
                        dve.wait(eng, t, x + "n")
                        act.wait(eng, t - 1, x + "T")
                        for c in range(DC):
                            m = eng.transpose(psum[:, bass.ts(c, P)], src[:, bass.ts(c, P)], ident[:, :])
                        pe.done(m, x + "T")

        @block.vector
        def _(eng):
            dve.start(eng)
            link = Chain(nc, ctx, "p_link", eng)
            eng.wait_ge(s_x, 64)
            for t in range(NT):
                last = eng.bn_stats(stats[:, t, :], X[:, t, :])
            link(last)
            for t in range(NT):
                last = eng.bn_aggr(mv[:, t, :], stats[:, t, :])
            link(last)
            link(eng.tensor_scalar_add(mv[:, :, 1], mv[:, :, 1], LN_EPS))
            eng.sem_inc(s_mv, 1)
            eng.wait_ge(s_sd, 1)
            link(eng.reciprocal(rstd, rstd))
            eng.scalar_tensor_tensor(shift, mv[:, :, 0], -1.0, rstd, ALU.mult, ALU.mult).then_inc(s_ln, 1)
            eng.wait_ge(s_rows, 16)
            link(eng.tensor_scalar_mul(rows[:, 3, :], rows[:, 3, :], -HD ** -0.5))
            link(eng.memset(eps[:, :], RMS_EPS))
            eng.sem_inc(s_eps, 1)
            with eng.Fori(0, NT // 2) as i:
                for par in range(2):
                    t = i * 2 + par
                    pe.wait(eng, t, "xT")
                    pe.wait(eng, t - 2, "q")
                    dve.done(eng.tensor_copy(xnT[:, par, :, :], pxT[:, :].rearrange("p (c n) -> p c n", c=DC)), "xT")
                    for x, psum, dst, bias in (("k", pk, kb, 2), ("q", pq, qb, 0)):
                        pe.wait(eng, t, x)
                        act.wait(eng, t - 1, x + "sq")
                        dve.done(eng.tensor_tensor(dst[:, :], psum[:, :], rows[:, bias, :], ALU.add), x + "b")
                    for x, src, root, inv, dst, w in (("k", kb, kms, krs, kn, 3), ("q", qb, qms, qrs, qn, 1)):
                        act.wait(eng, t, x + "sd")
                        dve.done(eng.reciprocal(inv[:, :], root[:, 1:2]), x + "r")
                        dve.wait(eng, t, x + "r")
                        pe.wait(eng, t - 1, x + "T")
                        dve.done(eng.scalar_tensor_tensor(dst[:, :], src[:, :], inv[:, 0:1], rows[:, w, :],
                                                          ALU.mult, ALU.mult), x + "n")
                    pe.wait(eng, t, "v")
                    dve.done(eng.tensor_tensor(V[:, t, :], pv[:, :], rows[:, 4, :], ALU.add), "vb")


def attend(nc, qT, kT, V, ident):
    GH = range(HG)
    with ExitStack() as ctx:
        sb = lambda name, shape, dt=F32: ctx.enter_context(nc.sbuf_tensor(name, shape, dt))
        ps = lambda name, shape, dt=F32: ctx.enter_context(nc.psum_tensor(name, shape, dt))
        qg, kg, vg = sb("qg", [P, 2, S]), sb("kg", [P, 2, S]), sb("vg", [P, 2, TPB, P])
        low, tot, inv = sb("low", [P, 2, HG, TPB]), sb("tot", [P, 2, HG, TPB]), sb("inv", [P, 2, HG, TPB])
        prob = sb("prob", [P, 2, HG, TPB, S])
        probT = sb("probT", [P, 2, HG, TPB, S])
        pS = [ps(f"pS{j}", [P, TPB, S]) for j in GH]
        pT = [ps(f"pT{j}", [P, TPB, S]) for j in range(2)]
        pO = [ps(f"pO{j}", [P, S]) for j in range(2)]
        peS = Steps(nc, ctx, "a_peS", [f"S{j}" for j in GH])
        peT = Steps(nc, ctx, "a_peT", [f"T{j}" for j in GH] + ["O"])
        dveM = Steps(nc, ctx, "a_dveM", [f"M{j}" for j in GH])
        dveR = Steps(nc, ctx, "a_dveR", [f"R{j}" for j in GH])
        dveT = Steps(nc, ctx, "a_dveT", [f"T{j}" for j in GH])
        actE = Steps(nc, ctx, "a_actE", [f"E{j}" for j in GH])
        actO = Steps(nc, ctx, "a_actO", ["O"])
        poolC = Steps(nc, ctx, "a_poolC", ["q", "k", "v"])
        poolN = Steps(nc, ctx, "a_poolN", [f"N{j}" for j in GH])
        NU = B * DC
        block = ctx.enter_context(nc.Block())

        def units(eng, one):
            with eng.Fori(0, B - 1) as b:
                for g in range(DC):
                    one(b, g, lambda n: True)
            for g in range(DC):
                one(B - 1, g, lambda n, g=g: g + n < DC)

        def scores(eng, u, par):
            poolC.wait(eng, u, "k")
            for j in GH:
                actE.wait(eng, u - 1, f"E{j}")
                for h in range(TPB):
                    m = eng.matmul(pS[j][:, h, :], qg[bass.ts(j, HD), par, bass.ts(h, P)],
                                   kg[bass.ts(j, HD), par, :], start=True, stop=True)
                peS.done(m, f"S{j}")

        @block.tensor
        def _(eng):
            peS.start(eng)
            peT.start(eng)
            scores(eng, 0, 0)

            def one(b, g, later):
                u, par = b * DC + g, g % 2
                if later(1):
                    scores(eng, u + 1, 1 - par)
                for j in GH:
                    poolN.wait(eng, u, f"N{j}")
                    if j < 2:
                        dveT.wait(eng, u - 1, f"T{j + 2}")
                    else:
                        dveT.wait(eng, u, f"T{j - 2}")
                    for kt in range(TPB):
                        for h in range(TPB):
                            m = eng.transpose(pT[j % 2][:, kt, bass.ts(h, P)], prob[:, par, j, h, bass.ts(kt, P)], ident[:, :])
                    peT.done(m, f"T{j}")
                poolC.wait(eng, u, "v")
                actO.wait(eng, u - 2, "O")
                for j in GH:
                    dveT.wait(eng, u, f"T{j}")
                    for kt in range(TPB):
                        m = eng.matmul(pO[par][bass.ts(j, HD), :], vg[:, par, kt, bass.ts(j, HD)],
                                       probT[:, par, j, kt, :], start=kt == 0, stop=kt == TPB - 1)
                peT.done(m, "O")

            units(eng, one)

        @block.vector
        def _(eng):
            dveM.start(eng)
            dveR.start(eng)
            dveT.start(eng)

            def lows(u, par, j):
                peS.wait(eng, u, f"S{j}")
                actE.wait(eng, u - 2, f"E{j}")
                dveM.done(eng.tensor_reduce(low[:, par, j, :], pS[j][:, :, :], axis=AX.X, op=ALU.min), f"M{j}")

            for j in GH:
                lows(0, 0, j)

            def one(b, g, later):
                u, par = b * DC + g, g % 2
                for j in GH:
                    actE.wait(eng, u, f"E{j}")
                    poolN.wait(eng, u - 2, f"N{j}")
                    dveR.done(eng.reciprocal(inv[:, par, j, :], tot[:, par, j, :]), f"R{j}")
                    if later(1):
                        lows(u + 1, 1 - par, j)
                for j in GH:
                    peT.wait(eng, u, f"T{j}")
                    peT.wait(eng, u - 2, "O")
                    dveT.done(eng.tensor_copy(probT[:, par, j, :, :], pT[j % 2][:, :, :]), f"T{j}")

            units(eng, one)

        @block.scalar
        def _(eng):
            actE.start(eng)
            actO.start(eng)

            def exps(u, par):
                for j in GH:
                    dveM.wait(eng, u, f"M{j}")
                    peT.wait(eng, u - 2, f"T{j}")
                    dveR.wait(eng, u - 2, f"R{j}")
                    for h in range(TPB):
                        a = eng.activation(prob[:, par, j, h, :], pS[j][:, h, :], ACT.Exp, bias=low[:, par, j, h:h + 1],
                                           scale=-1.0, accum_out=tot[:, par, j, h:h + 1])
                    actE.done(a, f"E{j}")

            exps(0, 0)

            def one(b, g, later):
                u, par = b * DC + g, g % 2
                if later(1):
                    exps(u + 1, 1 - par)
                peT.wait(eng, u, "O")
                actO.done(eng.activation(qT[:, g, bass.ts(b, S)], pO[par][:, :], ACT.Copy), "O")

            units(eng, one)

        @block.gpsimd
        def _(eng):
            poolC.start(eng)
            poolN.start(eng)

            def copies(b, g):
                u, par = b * DC + g, g % 2
                peS.wait(eng, u - 2, f"S{HG - 1}")
                poolC.done(eng.tensor_copy(qg[:, par, :], qT[:, g, bass.ts(b, S)]), "q")
                poolC.done(eng.tensor_copy(kg[:, par, :], kT[:, g, bass.ts(b, S)]), "k")
                peT.wait(eng, u - 2, "O")
                poolC.done(eng.tensor_copy(vg[:, par, :, :], V[:, bass.ts(b, TPB), bass.ts(g, P)]), "v")

            copies(0, 0)
            copies(0, 1)

            def one(b, g, later):
                u, par = b * DC + g, g % 2
                for j in GH:
                    dveR.wait(eng, u, f"R{j}")
                    w = prob[:, par, j, :, :]
                    poolN.done(eng.tensor_tensor(w, w, inv[:, par, j, :].unsqueeze(2).to_broadcast([P, TPB, S]), ALU.mult), f"N{j}")
                if later(2):
                    copies(b + (g + 2) // DC, (g + 2) % DC)

            units(eng, one)


def by_unit(eng, one, n, unroll, peel):
    assert (n - peel) % unroll == 0 and peel % unroll == 0
    with eng.Fori(0, (n - peel) // unroll) as i:
        for u in range(unroll):
            one(i * unroll + u, u, lambda k: True)
    for t in range(n - peel, n):
        one(t, t % unroll, lambda k, t=t: t + k < n)


def route(nc, a, h_dram, X, qT, L, mask, m8, ident):
    with ExitStack() as ctx:
        sb = lambda name, shape, dt=F32: ctx.enter_context(nc.sbuf_tensor(name, shape, dt))
        ps = lambda name, shape, dt=F32: ctx.enter_context(nc.psum_tensor(name, shape, dt))
        sem = lambda name: ctx.enter_context(nc.semaphore(name))
        Wo, ob, Wr = sb("wo", [P, DC, D]), sb("ob", [P, D]), sb("router_w", [P, DC, E])
        oT, add, h, hT = sb("oT", [P, 2, DC, P]), sb("add", [P, 2, D]), sb("h", [P, 2, D]), sb("hT", [P, 2, DC, P])
        stats, mv, ln = sb("ln2_stats", [P, 6]), sb("ln2_mv", [P, 2]), sb("ln2", [P, 2, 3])
        eps, logit, rest, top = sb("ln2_eps", [P, 1]), sb("logit", [P, E]), sb("rest", [P, E]), sb("top", [P, K])
        po, ph, pl = [ps(f"po{i}", [P, D]) for i in range(2)], ps("ph", [P, D]), ps("pl", [P, E])
        s_apart = sem("r_apart")
        s_w, s_ob, s_r, s_eps, s_h = sem("r_w"), sem("r_ob"), sem("r_r"), sem("r_eps"), [sem(f"r_h{i}") for i in range(2)]
        poolC, poolX = Steps(nc, ctx, "r_poolC", ["oT"]), Steps(nc, ctx, "r_poolX", ["x"])
        peO, peH = Steps(nc, ctx, "r_peO", ["o"]), Steps(nc, ctx, "r_peH", ["hT", "l"])
        dveA = Steps(nc, ctx, "r_dveA", ["add", "stats", "mv", "rstd", "shift"])
        dveB = Steps(nc, ctx, "r_dveB", ["hT", "l", "top", "rest", "mask", "L", "m8"])
        actA = Steps(nc, ctx, "r_actA", ["sd", "h"])
        block = ctx.enter_context(nc.Block())

        @block.sync
        def _(eng):
            eng.dma_start(Wo[:, :, :], a["attn_wT"][3]).then_inc(s_w, 16)
            eng.dma_start(ob[:, :], a["rows"][5:6, :].to_broadcast([P, D])).then_inc(s_ob, 16)
            eng.dma_start(Wr[:, :, :], a["router_wT"]).then_inc(s_r, 16)

            def one(t, u, later):
                actA.wait(eng, t, "h")
                eng.dma_start(h_dram[bass.ts(t, P), :], h[:, u, :]).then_inc(s_h[u], 16)

            by_unit(eng, one, NT, 2, 0)
            for s in s_h:
                eng.wait_ge(s, 16 * NT // 2)

        @block.gpsimd
        def _(eng):
            poolC.start(eng)
            poolX.start(eng)

            def copy(t, u):
                peO.wait(eng, t - 2, "o")
                poolC.done(eng.tensor_copy(oT[:, u, :, :], qT[:, :, bass.ts(t, P)]), "oT")

            copy(0, 0)
            copy(1, 1)

            def one(t, u, later):
                dveA.wait(eng, t, "add")
                poolX.done(eng.tensor_tensor(X[:, t, :], X[:, t, :], add[:, u, :], ALU.add), "x")
                if later(2):
                    copy(t + 2, u)

            by_unit(eng, one, NT, 2, 2)

        @block.tensor
        def _(eng):
            peO.start(eng)
            peH.start(eng)
            eng.wait_ge(s_w, 16)

            def project_out(t, u):
                poolC.wait(eng, t, "oT")
                dveA.wait(eng, t - 2, "add")
                for c in range(DC):
                    m = eng.matmul(po[u][:, :], oT[:, u, c, :], Wo[:, c, :], start=c == 0, stop=c == DC - 1)
                peO.done(m, "o")

            project_out(0, 0)
            eng.wait_ge(s_r, 16)

            def one(t, u, later):
                if later(1):
                    project_out(t + 1, 1 - u)
                actA.wait(eng, t, "h")
                dveB.wait(eng, t - 1, "hT")
                for c in range(DC):
                    m = eng.transpose(ph[:, bass.ts(c, P)], h[:, u, bass.ts(c, P)], ident[:, :])
                peH.done(m, "hT")
                dveB.wait(eng, t, "hT")
                dveB.wait(eng, t - 1, "l")
                for c in range(DC):
                    m = eng.matmul(pl[:, :], hT[:, u, c, :], Wr[:, c, :], start=c == 0, stop=c == DC - 1)
                peH.done(m, "l")

            by_unit(eng, one, NT, 2, 2)

        @block.scalar
        def _(eng):
            actA.start(eng)
            eng.wait_ge(s_eps, 1)

            def norm(t, u):
                dveA.wait(eng, t, "mv")
                actA.done(eng.activation(ln[:, u, 2:3], mv[:, 1:2], ACT.Sqrt, bias=eps[:, 0:1]), "sd")
                dveA.wait(eng, t, "shift")
                peH.wait(eng, t - 2, "hT")
                return eng.activation(h[:, u, :], X[:, t, :], ACT.Identity, bias=ln[:, u, 1:2], scale=ln[:, u, 0:1])

            for u in range(2):
                actA.done(norm(u, u), "h")
            with eng.Fori(1, NT // 2) as i:
                for u in range(2):
                    eng.wait_ge(s_h[u], i * 16)
                    actA.done(norm(i * 2 + u, u), "h")

        @block.vector
        def _(eng):
            dveA.start(eng)
            dveB.start(eng)
            eng.memset(eps[:, :], LN_EPS).then_inc(s_eps, 1)
            eng.wait_ge(s_ob, 16)

            def residual(t, u):
                peO.wait(eng, t, "o")
                poolX.wait(eng, t - 2, "x")
                dveA.done(eng.tensor_tensor(add[:, u, :], po[u][:, :], ob[:, :], ALU.add), "add")
                poolX.wait(eng, t, "x")
                apart(eng, s_apart)
                dveA.done(eng.bn_stats(stats[:, :], X[:, t, :]), "stats")
                dveA.wait(eng, t, "stats")
                actA.wait(eng, t - 1, "sd")
                apart(eng, s_apart)
                dveA.done(eng.bn_aggr(mv[:, :], stats[:, :]), "mv")
                actA.wait(eng, t, "sd")
                actA.wait(eng, t - 2, "h")
                dveA.done(eng.reciprocal(ln[:, u, 0:1], ln[:, u, 2:3]), "rstd")
                dveA.wait(eng, t, "rstd")
                dveA.done(eng.scalar_tensor_tensor(ln[:, u, 1:2], mv[:, 0:1], -1.0, ln[:, u, 0:1], ALU.mult, ALU.mult), "shift")

            residual(0, 0)

            def one(t, u, later):
                if later(1):
                    residual(t + 1, 1 - u)
                peH.wait(eng, t, "hT")
                peH.wait(eng, t - 2, "l")
                dveB.done(eng.tensor_copy(hT[:, u, :, :], ph[:, :].rearrange("p (c n) -> p c n", c=DC)), "hT")
                peH.wait(eng, t, "l")
                dveB.done(eng.tensor_copy(logit[:, :], pl[:, :]), "l")
                dveB.wait(eng, t, "l")
                apart(eng, s_apart)
                dveB.done(eng.max(top[:, :], logit[:, :]), "top")
                dveB.wait(eng, t, "top")
                apart(eng, s_apart)
                dveB.done(eng.match_replace(rest[:, :], top[:, :], logit[:, :], -3e38), "rest")
                dveB.wait(eng, t, "rest")
                dveB.done(eng.tensor_tensor(mask[:, t, :], logit[:, :], rest[:, :], ALU.not_equal), "mask")
                dveB.done(eng.tensor_copy(L[:, t, :], logit[:, :]), "L")
                dveB.done(eng.tensor_copy(m8[:, t, :], top[:, :]), "m8")

            by_unit(eng, one, NT, 2, 2)


def place(nc, a, L, mask, m8, slot8, w8, blk_tok, endb, blk_tab, tab_dram):
    with ExitStack() as ctx:
        sb = lambda name, shape, dt=F32: ctx.enter_context(nc.sbuf_tensor(name, shape, dt))
        ps = lambda name, shape, dt=F32: ctx.enter_context(nc.psum_tensor(name, shape, dt))
        sem = lambda name: ctx.enter_context(nc.semaphore(name))
        mask16, before, ones16 = sb("mask16", [P, NT * E], F16), sb("before", [P, P], F16), sb("ones16", [P, P], F16)
        total, inv = sb("total", [P, NT]), sb("winv", [P, NT])
        pre = sb("pre", [P, NT + 1, E])
        cnt_i, nblk, one_e, first, end = sb("cnt_i", [P, E], I32), sb("nblk", [P, E]), sb("one_e", [P, E]), sb("first", [P, E]), sb("end", [P, E])
        key, key8, hit = sb("key", [P, NT, E]), sb("key8", [P, NT, K]), sb("hit", [P, NT, E])
        slot_f, slot_i = sb("slot_f", [P, NT, K]), sb("slot_i", [P, NT, K], I32)
        row_i, blk_i, row_f, blk_f = sb("row_i", [P, NT, K], I32), sb("blk_i", [P, NT, K], I32), sb("row_f", [P, NT, K]), sb("blk_f", [P, NT, K])
        it_i, it_row, it_blk = sb("it_i", [P, NBLK], I32), sb("it_row", [P, P], F16), sb("it_blk", [P, NBLK], F16)
        tok_i, tok = sb("tok_i", [P, NT], I32), sb("tok", [P, NT])
        hotr, hotb = sb("hotr", [P, K, P], F16), sb("hotb", [P, K, NBLK], F16)
        b_i, b_f, be, tab = sb("b_i", [P, 2], I32), sb("b_f", [P, 2]), sb("be", [P, 2]), sb("tab", [P, 2, 2], I32)
        le = sb("le", [P, E])
        prank, pcnt = [ps(f"prank{i}", [P, 512]) for i in range(2)], [ps(f"pcnt{i}", [P, 512]) for i in range(2)]
        plist = ps("plist", [P, NBLK])
        s_exp, s_iota, s_rank, s_m16, s_tab, s_tab2, s_ls = sem("l_exp"), sem("l_iota"), sem("l_rank"), sem("l_m16"), sem("l_tab"), sem("l_tab2"), sem("l_ls")
        s_lsub, s_list, s_pre = sem("l_lsub"), sem("l_list"), sem("l_pre")
        dveP = Steps(nc, ctx, "l_dveP", ["pre"])
        dveH = Steps(nc, ctx, "l_dveH", [f"h{k}" for k in range(K)])
        peL = Steps(nc, ctx, "l_peL", [f"l{k}" for k in range(K)])
        dual = lambda t, banks: banks[t // 8][:, bass.ts(t % 8, E)]
        block = ctx.enter_context(nc.Block())

        @block.gpsimd
        def _(eng):
            link = Chain(nc, ctx, "l_poolc", eng)
            link(eng.iota(it_i[:, :], pattern=[[1, NBLK]], base=0, channel_multiplier=0))
            link(eng.tensor_copy(it_row[:, :], it_i[:, 0:P]))
            link(eng.tensor_copy(it_blk[:, :], it_i[:, :]))
            link(eng.iota(tok_i[:, :], pattern=[[P, NT]], base=0, channel_multiplier=1))
            link(eng.tensor_copy(tok[:, :], tok_i[:, :]))
            link(eng.iota(b_i[:, :], pattern=[[P, 2]], base=0, channel_multiplier=1))
            link(eng.tensor_copy(b_f[:, :], b_i[:, :]))
            link(eng.memset(ones16[:, :], 1.0))
            link(eng.affine_select(out=before[:, :], in_=ones16[:, :], compare_op=ALU.is_gt, fill=0.0, base=0,
                                   pattern=[[1, P]], channel_multiplier=-1))
            eng.sem_inc(s_iota, 1)

        @block.tensor
        def _(eng):
            peL.start(eng)
            eng.wait_ge(s_iota, 1)
            eng.wait_ge(s_m16, 1)
            for i in range(2):
                eng.matmul(prank[i][:, :], before[:, :], mask16[:, bass.ts(i, 512)], start=True, stop=True)
                m = eng.matmul(pcnt[i][:, :], ones16[:, :], mask16[:, bass.ts(i, 512)], start=True, stop=True)
            m.then_inc(s_rank, 1)

            def one(t, start, stop):
                for k in range(K):
                    dveH.wait(eng, t, f"h{k}")
                    peL.done(eng.matmul(plist[:, :], hotr[:, k, :], hotb[:, k, :], start=start and k == 0,
                                        stop=stop and k == K - 1), f"l{k}")

            one(0, True, False)
            with eng.Fori(1, NT - 1) as t:
                one(t, False, False)
            one(NT - 1, False, True)

        @block.scalar
        def _(eng):
            eng.wait_ge(s_lsub, 1)
            eng.activation(L[:, :, :], L[:, :, :], ACT.Exp).then_inc(s_exp, 1)

        @block.sync
        def _(eng):
            eng.wait_ge(s_tab, 1)
            eng.dma_start(tab_dram[0:P, :], tab[:, 0, :]).then_inc(s_tab2, 16)
            eng.dma_start(tab_dram[P:NBLK, :], tab[0:NBLK - P, 1, :]).then_inc(s_tab2, 16)
            eng.wait_ge(s_tab2, 32)
            eng.dma_start(blk_tab[0:1, :], tab_dram.rearrange("(o b) v -> o (b v)", o=1)).then_inc(s_tab2, 16)
            eng.wait_ge(s_tab2, 48)

        @block.vector
        def _(eng):
            dveP.start(eng)
            dveH.start(eng)
            link = Chain(nc, ctx, "l_dvec", eng)
            link(eng.tensor_copy(mask16[:, :], mask[:, :, :].rearrange("p t e -> p (t e)")))
            eng.sem_inc(s_m16, 1)
            link(eng.tensor_tensor(L[:, :, :], L[:, :, :], m8[:, :, 0:1].to_broadcast([P, NT, E]), ALU.subtract))
            eng.sem_inc(s_lsub, 1)
            link(eng.memset(pre[:, 0, :], 0.0))
            link(eng.memset(one_e[:, :], 1.0))
            eng.wait_ge(s_rank, 1)
            dveP.wait(eng, -1, "pre")
            for t in range(NT):
                link(eng.tensor_tensor(pre[:, t + 1, :], pre[:, t, :], dual(t, pcnt), ALU.add))
            link(eng.tensor_scalar_add(cnt_i[:, :], pre[:, NT, :], float(P - 1)))
            link(eng.tensor_scalar(cnt_i[:, :], cnt_i[:, :], P.bit_length() - 1, None, ALU.arith_shift_right))
            link(eng.tensor_copy(nblk[:, :], cnt_i[:, :]))
            link(eng.tensor_scalar_max(nblk[:, :], nblk[:, :], 1.0))
            link(eng.tensor_tensor_scan(end[:, :], one_e[:, :], nblk[:, :], 0.0, ALU.mult, ALU.add))
            link(eng.tensor_copy(endb[:, :], end[:, :]))
            link(eng.tensor_tensor(first[:, :], end[:, :], nblk[:, :], ALU.subtract))
            link(eng.tensor_scalar_mul(first[:, :], first[:, :], float(P)))
            eng.wait_ge(s_iota, 1)
            for i in range(2):
                link(eng.tensor_scalar(le[:, :], end[:, :], b_f[:, i:i + 1], None, ALU.is_le))
                link(eng.reduce_sum(be[:, i:i + 1], le[:, :], axis=AX.X))
            link(eng.tensor_scalar_min(be[:, :], be[:, :], float(E - 1)))
            link(eng.tensor_copy(tab[:, :, 1], be[:, :]))
            link(eng.tensor_scalar(tab[:, :, 1], tab[:, :, 1], NWB - 1, None, ALU.bitwise_and))
            link(eng.tensor_scalar_add(tab[:, :, 0], be[:, :], 1.0))
            eng.sem_inc(s_tab, 1)
            for i in range(2):
                half = slice(i * 8, i * 8 + 8)
                link(eng.tensor_tensor(key[:, half, :], prank[i][:, :].rearrange("p (t e) -> p t e", e=E), pre[:, half, :], ALU.add))
            link(eng.tensor_tensor(key[:, :, :], key[:, :, :], first[:, :].unsqueeze(1).to_broadcast([P, NT, E]), ALU.add))
            link(eng.tensor_scalar(key[:, :, :], key[:, :, :], -1.0, SLOT_TOP, ALU.mult, ALU.add))
            link(eng.tensor_tensor(key[:, :, :], key[:, :, :], mask[:, :, :], ALU.mult))
            for t in range(NT):
                last = eng.max(key8[:, t, :], key[:, t, :])
            link(last)
            link(eng.tensor_scalar(slot_f[:, :, :], key8[:, :, :], -1.0, SLOT_TOP, ALU.mult, ALU.add))
            link(eng.tensor_copy(slot8[:, :, :], slot_f[:, :, :]))
            link(eng.tensor_copy(slot_i[:, :, :], slot_f[:, :, :]))
            link(eng.tensor_scalar(row_i[:, :, :], slot_i[:, :, :], P - 1, None, ALU.bitwise_and))
            link(eng.tensor_scalar(blk_i[:, :, :], slot_i[:, :, :], P.bit_length() - 1, None, ALU.arith_shift_right))
            link(eng.tensor_copy(row_f[:, :, :], row_i[:, :, :]))
            link(eng.tensor_copy(blk_f[:, :, :], blk_i[:, :, :]))
            with eng.Fori(0, NT) as t:
                for k in range(K):
                    peL.wait(eng, t - 1, f"l{k}")
                    eng.tensor_scalar(hotr[:, k, :], it_row[:, :], row_f[:, t, k:k + 1], None, ALU.is_equal)
                    dveH.done(eng.tensor_scalar(hotb[:, k, :], it_blk[:, :], blk_f[:, t, k:k + 1], tok[:, bass.ds(t, 1)],
                                                ALU.is_equal, ALU.mult), f"h{k}")
            peL.wait(eng, NT - 1, f"l{K - 1}")
            link(eng.tensor_copy(blk_tok[:, :], plist[:, :]))
            eng.wait_ge(s_exp, 1)
            link(eng.tensor_tensor(L[:, :, :], L[:, :, :], mask[:, :, :], ALU.mult))
            link(eng.reduce_sum(total[:, :], L[:, :, :], axis=AX.X))
            link(eng.reciprocal(inv[:, :], total[:, :]))
            link(eng.tensor_tensor(L[:, :, :], L[:, :, :], inv[:, :].unsqueeze(2).to_broadcast([P, NT, E]), ALU.mult))
            for k in range(K):
                link(eng.tensor_tensor(hit[:, :, :], key[:, :, :], key8[:, :, k:k + 1].to_broadcast([P, NT, E]), ALU.is_equal))
                link(eng.tensor_tensor(hit[:, :, :], hit[:, :, :], L[:, :, :], ALU.mult))
                link(eng.reduce_sum(w8[:, :, k], hit[:, :, :], axis=AX.X))


def experts(nc, a, h_dram, y_dram, blk_tok, endb, blk_tab, ident, ffn_w, ffn_src, s_ffn):
    with ExitStack() as ctx:
        sb = lambda name, shape, dt=F32: ctx.enter_context(nc.sbuf_tensor(name, shape, dt))
        ps = lambda name, shape, dt=F32: ctx.enter_context(nc.psum_tensor(name, shape, dt))
        sem = lambda name: ctx.enter_context(nc.semaphore(name))
        Wgu, Wd = sb("wgu", [P, NWB * DC, 2 * I]), sb("wd", [IH, NWB * 2, D])
        idx = [sb(f"idx{u}", [P, 1], U32) for u in range(4)]
        xg, xT = sb("xg", [P, 4, D]), sb("bxT", [P, 2, DC, P])
        act_g, hid, hidT, y = sb("act_g", [P, 2, I]), sb("hid", [P, 2, I]), sb("hidT", [IH, 2, 2, P]), sb("y", [P, 2, D])
        px, pg, ph, py = [[ps(f"m_{n}{i}", [P, D]) for i in range(2)] for n in ("x", "g", "h", "y")]
        s_ix, s_g = [sem(f"m_ix{u}") for u in range(4)], [sem(f"m_g{u}") for u in range(4)]
        s_apart = sem("m_apart")
        s_w, s_ready, s_y = [sem(f"m_w{u}") for u in range(NWB)], sem("m_ready"), [sem(f"m_y{u}") for u in range(2)]
        peX, pe = Steps(nc, ctx, "m_peX", ["xT"]), Steps(nc, ctx, "m_pe", ["hT", "y"])
        peG = Steps(nc, ctx, "m_peG", ["g"])
        dveX, dveH, dveT = Steps(nc, ctx, "m_dveX", ["xT"]), Steps(nc, ctx, "m_dveH", ["h"]), Steps(nc, ctx, "m_dveT", ["hT"])
        actS, actY = Steps(nc, ctx, "m_actS", ["silu"]), Steps(nc, ctx, "m_actY", ["y"])
        poolI = Steps(nc, ctx, "m_poolI", ["idx"])
        block = ctx.enter_context(nc.Block())

        @block.sync
        def _(eng):
            def load(e, u):
                eng.dma_start(Wgu[:, bass.ts(u, DC), :], a["exp_gu"][e]).then_inc(s_w[u], 16)
                eng.dma_start(Wd[:, bass.ts(u, 2), :], a["exp_d"][e]).then_inc(s_w[u], 16)

            for u in range(NWB):
                load(u, u)
            eng.wait_ge(s_w[0], 32)
            eng.sem_inc(s_ready, 1)
            with eng.Fori(1, E // NWB) as i:
                for u in range(NWB):
                    eng.wait_ge(s_w[(u + 1) % NWB], (i + (u + 1) // NWB) * 32)
                    eng.sem_inc(s_ready, 1)
                    e = i * NWB + u
                    end = eng.value_load(endb[0:1, bass.ds(e - NWB, 1)], min_val=0, max_val=NBLK)
                    pe.wait(eng, end - 1, "y")
                    load(e, u)
            for u in range(1, NWB):
                eng.wait_ge(s_w[u], 32 * (E // NWB))
                eng.sem_inc(s_ready, 1)

        @block.gpsimd
        def _(eng):
            poolI.start(eng)

            def one(b, u, later):
                poolI.done(eng.tensor_copy(idx[u][:, :], blk_tok[:, bass.ds(b, 1)]), "idx")
                poolI.wait(eng, b, "idx")
                peX.wait(eng, b - 4, "xT")
                apart(eng, s_apart)
                eng.indirect_dma_start(xg[:, u, :], None, h_dram, bass.IndirectOffsetOnAxis(ap=idx[u][:, 0:1], axis=0)).then_inc(s_g[u], 16)

            for u in range(4):
                one(u, u, None)
            with eng.Fori(1, NBLK // 4) as i:
                for u in range(4):
                    eng.wait_ge(s_g[u], i * 16)
                    one(i * 4 + u, u, None)

        @block.tensor
        def _(eng):
            peX.start(eng)
            peG.start(eng)
            pe.start(eng)

            def turn(b, u, n):
                eng.wait_ge(s_g[u], n * 16)
                dveX.wait(eng, b - 2, "xT")
                for c in range(DC):
                    m = eng.transpose(px[u % 2][:, bass.ts(c, P)], xg[:, u, bass.ts(c, P)], ident[:, :])
                peX.done(m, "xT")

            def gate_up(b, u):
                ready = eng.value_load(blk_tab[0:1, bass.ds(b * 2, 1)], min_val=1, max_val=E)
                buf = eng.value_load(blk_tab[0:1, bass.ds(b * 2 + 1, 1)], min_val=0, max_val=NWB - 1)
                eng.wait_ge(s_ready, ready)
                dveX.wait(eng, b, "xT")
                dveH.wait(eng, b - 2, "h")
                for c in range(DC):
                    m = eng.matmul(pg[u % 2][:, 0:2 * I], xT[:, u % 2, c, :], Wgu[:, buf * DC + c, :], start=c == 0, stop=c == DC - 1)
                peG.done(m, "g")
                return buf

            turn(0, 0, 1)
            turn(1, 1, 1)
            gate_up(0, 0)

            def one(i, u, later, n):
                b, par = i * 4 + u, u % 2
                dveH.wait(eng, b, "h")
                dveT.wait(eng, b - 2, "hT")
                for c in range(2):
                    m = eng.transpose(ph[par][0:IH, bass.ts(c, P)], hid[:, par, bass.ts(c, IH)], ident[:, :])
                pe.done(m, "hT")
                if later(1):
                    gate_up(b + 1, (u + 1) % 4)
                if later(2):
                    turn(b + 2, (u + 2) % 4, n + 1 + (u + 2) // 4)
                buf = eng.value_load(blk_tab[0:1, bass.ds(b * 2 + 1, 1)], min_val=0, max_val=NWB - 1)
                dveT.wait(eng, b, "hT")
                actY.wait(eng, b - 2, "y")
                for c in range(2):
                    m = eng.matmul(py[par][:, :], hidT[:, par, c, :], Wd[:, buf * 2 + c, :], start=c == 0, stop=c == 1)
                pe.done(m, "y")

            with eng.Fori(0, NBLK // 4 - 1) as i:
                for u in range(4):
                    one(i, u, lambda k: True, i)
            for u in range(4):
                one(NBLK // 4 - 1, u, lambda k, u=u: u + k < 4, NBLK // 4 - 1)

        @block.vector
        def _(eng):
            dveX.start(eng)
            dveH.start(eng)
            dveT.start(eng)

            def turned(b, u):
                peX.wait(eng, b, "xT")
                peG.wait(eng, b - 2, "g")
                dveX.done(eng.tensor_copy(xT[:, u % 2, :, :], px[u % 2][:, :].rearrange("p (c n) -> p c n", c=DC)), "xT")

            def hidden(b, u):
                actS.wait(eng, b, "silu")
                pe.wait(eng, b - 2, "hT")
                dveH.done(eng.tensor_tensor(hid[:, u % 2, :], pg[u % 2][:, I:2 * I], act_g[:, u % 2, :], ALU.mult), "h")

            turned(0, 0)
            turned(1, 1)
            hidden(0, 0)

            def one(b, u, later):
                pe.wait(eng, b, "hT")
                pe.wait(eng, b - 2, "y")
                dveT.done(eng.tensor_copy(hidT[:, u % 2, :, :], ph[u % 2][0:IH, 0:2 * P].rearrange("p (c n) -> p c n", c=2)), "hT")
                if later(1):
                    hidden(b + 1, u + 1)
                if later(2):
                    turned(b + 2, u + 2)

            by_unit(eng, one, NBLK, 4, 4)

        @block.scalar
        def _(eng):
            actS.start(eng)
            actY.start(eng)
            for dst, src in zip(ffn_w, ffn_src):
                eng.dma_start(dst, src).then_inc(s_ffn, 16)

            def silu(b, u):
                peG.wait(eng, b, "g")
                dveH.wait(eng, b - 2, "h")
                actS.done(eng.activation(act_g[:, u % 2, :], pg[u % 2][:, 0:I], ACT.Silu), "silu")

            def one(b, u, later, stored):
                if later(1):
                    silu(b + 1, u + 1)
                pe.wait(eng, b, "y")
                if stored is not None:
                    eng.wait_ge(s_y[u % 2], stored)
                actY.done(eng.activation(y[:, u % 2, :], py[u % 2][:, :], ACT.Copy), "y")
                actY.wait(eng, b, "y")
                eng.dma_start(y_dram[bass.ts(b, P), :], y[:, u % 2, :]).then_inc(s_y[u % 2], 16)

            silu(0, 0)
            for u in range(2):
                one(u, u, lambda k: True, None)
            with eng.Fori(1, NBLK // 2 - 1) as i:
                for u in range(2):
                    one(i * 2 + u, u, lambda k: True, i * 16)
            for u in range(2):
                one(NBLK - 2 + u, u, lambda k, u=u: u + k < 2, 16 * (NBLK // 2 - 1))
            for u in range(2):
                eng.wait_ge(s_y[u], 16 * NBLK // 2)


def norm_scales(nc, ctx, name, eng, link, mv, lnp, s_var, s_root):
    link(eng.tensor_scalar_add(mv[:, :, 1], mv[:, :, 1], LN_EPS))
    eng.sem_inc(s_var, 1)
    eng.wait_ge(s_root, 1)
    link(eng.reciprocal(lnp[:, :, 0], lnp[:, :, 0]))
    link(eng.scalar_tensor_tensor(lnp[:, :, 1], mv[:, :, 0], -1.0, lnp[:, :, 0], ALU.mult, ALU.mult))


def combine(nc, a, y_dram, X, slot8, w8, mv, lnp, ctx_sb, s_ctx):
    with ExitStack() as ctx:
        sb = lambda name, shape, dt=F32: ctx.enter_context(nc.sbuf_tensor(name, shape, dt))
        sem = lambda name: ctx.enter_context(nc.semaphore(name))
        idx = [[sb(f"cidx{u}_{k}", [P, 1], U32) for k in range(K)] for u in range(2)]
        G, stats = sb("G", [P, 2, K, D]), sb("c_stats", [P, 6])
        mv1 = sb("c_mv1", [P, 2])
        s_apart = sem("c_apart")
        s_g, s_var, s_root = [sem(f"c_g{u}") for u in range(2)], sem("c_var"), sem("c_root")
        pool = Steps(nc, ctx, "c_pool", ["idx"])
        dve = Steps(nc, ctx, "c_dve", [f"k{k}" for k in range(K)] + ["stats", "mv1", "mv"])
        block = ctx.enter_context(nc.Block())

        @block.sync
        def _(eng):
            for dst, src in ctx_sb:
                eng.dma_start(dst, src).then_inc(s_ctx, 16)

        @block.gpsimd
        def _(eng):
            pool.start(eng)

            def one(t, u):
                dve.wait(eng, t - 2, f"k{K - 1}")
                for k in range(K):
                    c = eng.tensor_copy(idx[u][k][:, :], slot8[:, t, k:k + 1])
                pool.done(c, "idx")
                pool.wait(eng, t, "idx")
                apart(eng, s_apart)
                for k in range(K):
                    eng.indirect_dma_start(G[:, u, k, :], None, y_dram, bass.IndirectOffsetOnAxis(ap=idx[u][k][:, 0:1], axis=0)).then_inc(s_g[u], 16)

            with eng.Fori(0, NT // 2) as i:
                for u in range(2):
                    one(i * 2 + u, u)

        @block.vector
        def _(eng):
            dve.start(eng)
            link = Chain(nc, ctx, "c_link", eng)
            with eng.Fori(0, NT // 2) as i:
                for u in range(2):
                    t = i * 2 + u
                    eng.wait_ge(s_g[u], 16 * K * (i + 1))
                    for k in range(K):
                        dve.done(eng.scalar_tensor_tensor(X[:, t, :], G[:, u, k, :], w8[:, t, k:k + 1], X[:, t, :], ALU.mult, ALU.add), f"k{k}")
                        dve.wait(eng, t, f"k{k}")
                    apart(eng, s_apart)
                    dve.done(eng.bn_stats(stats[:, :], X[:, t, :]), "stats")
                    dve.wait(eng, t, "stats")
                    apart(eng, s_apart)
                    dve.done(eng.bn_aggr(mv1[:, :], stats[:, :]), "mv1")
                    dve.wait(eng, t, "mv1")
                    dve.done(eng.tensor_copy(mv[:, t, :], mv1[:, :]), "mv")
            dve.wait(eng, NT - 1, "mv")
            norm_scales(nc, ctx, "c", eng, link, mv, lnp, s_var, s_root)

        @block.scalar
        def _(eng):
            eng.wait_ge(s_var, 1)
            eng.activation(lnp[:, :, 0], mv[:, :, 1], ACT.Sqrt).then_inc(s_root, 1)


def read_memory(nc, a, X, mv, lnp, ctxT, ctxR, s_ctx, ident):
    with ExitStack() as ctx:
        sb = lambda name, shape, dt=F32: ctx.enter_context(nc.sbuf_tensor(name, shape, dt))
        ps = lambda name, shape, dt=F32: ctx.enter_context(nc.psum_tensor(name, shape, dt))
        sem = lambda name: ctx.enter_context(nc.semaphore(name))
        m8b, neg, valid = sb("mask_b", [P, B, S], U8), sb("neg", [P, B, S]), sb("valid", [P, B])
        xn, xT = sb("x3n", [P, 2, D]), sb("x3T", [P, 2, DC, P])
        sc, nmax, tot, inv = sb("sc", [P, 2, S]), sb("nmax", [P, 2, 2]), sb("mtot", [P, 2]), sb("minv", [P, 2])
        pr, prT, stats = sb("mp", [P, 2, S]), sb("mpT", [P, 2, TPB, P]), sb("m_stats", [P, 6])
        mv1 = sb("d_mv1", [P, 2])
        px, psc, ppT, pr_o = [[ps(f"r_{n}{i}", [P, D]) for i in range(2)] for n in ("x", "s", "p", "o")]
        s_apart = sem("d_apart")
        s_m, s_var, s_root = sem("d_m"), sem("d_var"), sem("d_root")
        act = Steps(nc, ctx, "d_act", ["xn", "e"])
        pe = Steps(nc, ctx, "d_pe", ["xT", "s", "pT", "o"])
        dve = Steps(nc, ctx, "d_dve", ["xT", "sc", "max", "nmax", "pT", "inv", "invv", "x", "stats", "mv1", "mv"])
        block = ctx.enter_context(nc.Block())

        @block.sync
        def _(eng):
            eng.dma_start(m8b[:, :, :], a["mask"].unsqueeze(0).to_broadcast([P, B, S])).then_inc(s_m, 16)

        @block.scalar
        def _(eng):
            act.start(eng)

            def one(t, u, later):
                pe.wait(eng, t - 2, "xT")
                act.done(eng.activation(xn[:, u, :], X[:, t, :], ACT.Identity, bias=lnp[:, t, 1:2], scale=lnp[:, t, 0:1]), "xn")
                dve.wait(eng, t, "nmax")
                pe.wait(eng, t - 2, "pT")
                dve.wait(eng, t - 2, "inv")
                act.done(eng.activation(pr[:, u, :], sc[:, u, :], ACT.Exp, bias=nmax[:, u, 1:2], accum_out=tot[:, u:u + 1]), "e")

            by_unit(eng, one, NT, 2, 0)
            eng.wait_ge(s_var, 1)
            eng.activation(lnp[:, :, 0], mv[:, :, 1], ACT.Sqrt).then_inc(s_root, 1)

        @block.tensor
        def _(eng):
            pe.start(eng)
            eng.wait_ge(s_ctx, 32)
            with eng.Fori(0, B) as b:
                for u in range(2):
                    t = b * 2 + u
                    act.wait(eng, t, "xn")
                    dve.wait(eng, t - 2, "xT")
                    for c in range(DC):
                        m = eng.transpose(px[u][:, bass.ts(c, P)], xn[:, u, bass.ts(c, P)], ident[:, :])
                    pe.done(m, "xT")
                    dve.wait(eng, t, "xT")
                    for c in range(DC):
                        m = eng.matmul(psc[u][:, 0:S], xT[:, u, c, :], ctxT[:, b, c, :], start=c == 0, stop=c == DC - 1)
                    pe.done(m, "s")
                    act.wait(eng, t, "e")
                    dve.wait(eng, t - 2, "pT")
                    for kt in range(TPB):
                        m = eng.transpose(ppT[u][:, bass.ts(kt, P)], pr[:, u, bass.ts(kt, P)], ident[:, :])
                    pe.done(m, "pT")
                    dve.wait(eng, t, "pT")
                    dve.wait(eng, t - 2, "x")
                    for kt in range(TPB):
                        m = eng.matmul(pr_o[u][:, :], prT[:, u, kt, :], ctxR[:, b * TPB + kt, :], start=kt == 0, stop=kt == TPB - 1)
                    pe.done(m, "o")

        @block.vector
        def _(eng):
            dve.start(eng)
            link = Chain(nc, ctx, "d_link", eng)
            eng.wait_ge(s_m, 16)
            link(eng.tensor_scalar(neg[:, :, :], m8b[:, :, :], 1.0, 1e30, ALU.subtract, ALU.mult))
            link(eng.tensor_reduce(valid[:, :], m8b[:, :, :], axis=AX.X, op=ALU.max))
            with eng.Fori(0, B) as b:
                for u in range(2):
                    t = b * 2 + u
                    pe.wait(eng, t, "xT")
                    dve.done(eng.tensor_copy(xT[:, u, :, :], px[u][:, :].rearrange("p (c n) -> p c n", c=DC)), "xT")
                    pe.wait(eng, t, "s")
                    act.wait(eng, t - 2, "e")
                    dve.done(eng.scalar_tensor_tensor(sc[:, u, :], psc[u][:, 0:S], D ** -0.5, neg[:, b, :], ALU.mult, ALU.add), "sc")
                    dve.wait(eng, t, "sc")
                    dve.done(eng.tensor_reduce(nmax[:, u, 0:1], sc[:, u, :], axis=AX.X, op=ALU.max), "max")
                    dve.wait(eng, t, "max")
                    dve.done(eng.tensor_scalar_mul(nmax[:, u, 1:2], nmax[:, u, 0:1], -1.0), "nmax")
                    pe.wait(eng, t, "pT")
                    dve.done(eng.tensor_copy(prT[:, u, :, :], ppT[u][:, 0:S].rearrange("p (c n) -> p c n", c=TPB)), "pT")
                    dve.done(eng.reciprocal(inv[:, u:u + 1], tot[:, u:u + 1]), "inv")
                    dve.wait(eng, t, "inv")
                    dve.done(eng.tensor_tensor(inv[:, u:u + 1], inv[:, u:u + 1], valid[:, bass.ds(b, 1)], ALU.mult), "invv")
                    dve.wait(eng, t, "invv")
                    pe.wait(eng, t, "o")
                    dve.done(eng.scalar_tensor_tensor(X[:, t, :], pr_o[u][:, :], inv[:, u:u + 1], X[:, t, :], ALU.mult, ALU.add), "x")
                    dve.wait(eng, t, "x")
                    apart(eng, s_apart)
                    dve.done(eng.bn_stats(stats[:, :], X[:, t, :]), "stats")
                    dve.wait(eng, t, "stats")
                    apart(eng, s_apart)
                    dve.done(eng.bn_aggr(mv1[:, :], stats[:, :]), "mv1")
                    dve.wait(eng, t, "mv1")
                    dve.done(eng.tensor_copy(mv[:, t, :], mv1[:, :]), "mv")
            dve.wait(eng, NT - 1, "mv")
            act.wait(eng, NT - 1, "xn")
            norm_scales(nc, ctx, "d", eng, link, mv, lnp, s_var, s_root)


def feed_forward(nc, a, out, X, lnp, Wg, Wu, Wdn, s_ffn, ident):
    with ExitStack() as ctx:
        sb = lambda name, shape, dt=F32: ctx.enter_context(nc.sbuf_tensor(name, shape, dt))
        ps = lambda name, shape, dt=F32: ctx.enter_context(nc.psum_tensor(name, shape, dt))
        sem = lambda name: ctx.enter_context(nc.semaphore(name))
        gs, us, ds_ = sb("gate_s", [P, FC]), sb("up_s", [P, FC]), sb("down_s", [P, D])
        xn, xT = sb("x4n", [P, TPB, D]), sb("x4T", [P, 2, DC, S])
        gl, hT = sb("gl", [P, 2, S]), sb("fhT", [P, 2, FC, S])
        sc, o = sb("f_sc", [P, TPB, D]), sb("f_o", [P, TPB, D])
        px, pgu, py = [ps(f"f_x{i}", [P, D]) for i in range(2)], [ps(f"f_gu{i}", [P, 2, S]) for i in range(2)], [ps(f"f_y{i}", [P, D]) for i in range(2)]
        s_s, s_o = sem("f_s"), [sem(f"f_o{i}") for i in range(TPB)]
        fs = range(FC)
        actN = Steps(nc, ctx, "f_actN", [f"x{i}" for i in range(TPB)])
        actG = Steps(nc, ctx, "f_actG", [f"g{f}" for f in fs])
        peX, peY = Steps(nc, ctx, "f_peX", [f"x{i}" for i in range(TPB)]), Steps(nc, ctx, "f_peY", [f"y{i}" for i in range(TPB)])
        peG = Steps(nc, ctx, "f_peG", [f"g{f}" for f in fs])
        dveX = Steps(nc, ctx, "f_dveX", [f"x{i}" for i in range(TPB)])
        dveH = Steps(nc, ctx, "f_dveH", [f"h{f}" for f in fs])
        dveY = Steps(nc, ctx, "f_dveY", ["s0", "o0", "s1", "o1"])
        block = ctx.enter_context(nc.Block())

        @block.sync
        def _(eng):
            eng.dma_start(gs[:, :], a["gate_s"]).then_inc(s_s, 16)
            eng.dma_start(us[:, :], a["up_s"]).then_inc(s_s, 16)
            eng.dma_start(ds_[:, :], a["down_s"].unsqueeze(0).to_broadcast([P, D])).then_inc(s_s, 16)
            with eng.Fori(0, B) as b:
                for i in range(TPB):
                    dveY.wait(eng, b, f"o{i}")
                    eng.dma_start(out[bass.ts(b * TPB + i, P), :], o[:, i, :]).then_inc(s_o[i], 16)
            for s in s_o:
                eng.wait_ge(s, 16 * B)

        @block.scalar
        def _(eng):
            actN.start(eng)
            actG.start(eng)
            eng.wait_ge(s_s, 48)

            def norm(b):
                for i in range(TPB):
                    t = b * TPB + i
                    peX.wait(eng, b - 1, f"x{i}")
                    actN.done(eng.activation(xn[:, i, :], X[:, t, :], ACT.Identity, bias=lnp[:, t, 1:2], scale=lnp[:, t, 0:1]), f"x{i}")

            norm(0)

            def one(b, u, later):
                for f in fs:
                    peG.wait(eng, b, f"g{f}")
                    if f < 2:
                        dveH.wait(eng, b - 1, f"h{FC - 2 + f}")
                    else:
                        dveH.wait(eng, b, f"h{f - 2}")
                    actG.done(eng.activation(gl[:, f % 2, :], pgu[f % 2][:, 0, :], ACT.Silu, scale=gs[:, f:f + 1]), f"g{f}")
                    if f == 2 and later(1):
                        norm(b + 1)

            by_unit(eng, one, B, 2, 2)

        @block.tensor
        def _(eng):
            peX.start(eng)
            peG.start(eng)
            peY.start(eng)

            def turn(b):
                for i in range(TPB):
                    actN.wait(eng, b, f"x{i}")
                    dveX.wait(eng, b - 1, f"x{i}")
                    for c in range(DC):
                        m = eng.transpose(px[i][:, bass.ts(c, P)], xn[:, i, bass.ts(c, P)], ident[:, :])
                    peX.done(m, f"x{i}")

            turn(0)
            eng.wait_ge(s_ffn, 48)

            def one(b, u, later):
                dveX.wait(eng, b, f"x{TPB - 1}")
                for f in fs:
                    if f < 2:
                        dveH.wait(eng, b - 1, f"h{FC - 2 + (f + 1) % 2}")
                    else:
                        dveH.wait(eng, b, f"h{f - 2}")
                    for n, w in enumerate((Wg, Wu)):
                        for c in range(DC):
                            m = eng.matmul(pgu[f % 2][:, n, :], w[:, c, bass.ts(f, P)], xT[:, u, c, :], start=c == 0, stop=c == DC - 1)
                    peG.done(m, f"g{f}")
                if later(1):
                    turn(b + 1)
                dveH.wait(eng, b, f"h{FC - 1}")
                for i in range(TPB):
                    dveY.wait(eng, b - 1, f"s{i}")
                    for f in fs:
                        m = eng.matmul(py[i][:, :], hT[:, u, f, bass.ts(i, P)], Wdn[:, f, :], start=f == 0, stop=f == FC - 1)
                    peY.done(m, f"y{i}")

            by_unit(eng, one, B, 2, 2)

        @block.vector
        def _(eng):
            dveX.start(eng)
            dveH.start(eng)
            dveY.start(eng)
            eng.wait_ge(s_s, 48)

            def turned(b, u):
                for i in range(TPB):
                    peX.wait(eng, b, f"x{i}")
                    dveX.done(eng.tensor_copy(xT[:, u, :, bass.ts(i, P)], px[i][:, :].rearrange("p (c n) -> p c n", c=DC)), f"x{i}")

            turned(0, 0)

            def one(b, u, later, stored):
                for f in fs:
                    actG.wait(eng, b, f"g{f}")
                    dveH.done(eng.scalar_tensor_tensor(hT[:, u, f, :], pgu[f % 2][:, 1, :], us[:, f:f + 1], gl[:, f % 2, :],
                                                       ALU.mult, ALU.mult), f"h{f}")
                if later(1):
                    turned(b + 1, 1 - u)
                for i in range(TPB):
                    peY.wait(eng, b, f"y{i}")
                    dveY.done(eng.tensor_tensor(sc[:, i, :], py[i][:, :], ds_[:, :], ALU.mult), f"s{i}")
                    dveY.wait(eng, b, f"s{i}")
                    if stored is not None:
                        eng.wait_ge(s_o[i], stored)
                    dveY.done(eng.tensor_tensor(o[:, i, :], sc[:, i, :], X[:, b * TPB + i, :], ALU.add), f"o{i}")

            one(0, 0, lambda k: True, None)
            one(1, 1, lambda k: True, 16)
            with eng.Fori(1, B // 2 - 1) as i:
                for u in range(2):
                    one(i * 2 + u, u, lambda k: True, (i * 2 + u) * 16)
            for u in range(2):
                one(B - 2 + u, u, lambda k, u=u: u + k < 2, (B - 2 + u) * 16)


def build(nc, a, out, stop=99, dbg=None):
    h_dram = nc.dram_tensor("h_rows", (T, D), F32).ap()
    y_dram = nc.dram_tensor("y_rows", (NBLK * P, D), F32).ap()
    tab_dram = nc.dram_tensor("block_table", (NBLK, 2), I32).ap()
    with ExitStack() as ctx:
        sb = lambda name, shape, dt=F32, ctx=ctx: ctx.enter_context(nc.sbuf_tensor(name, shape, dt))
        X, ident = sb("X", [P, NT, D]), sb("ident", [P, P])
        slot8, w8 = sb("slot8", [P, NT, K], U32), sb("w8", [P, NT, K])
        blk_tok, endb, blk_tab = sb("blk_tok", [P, NBLK], U32), sb("endb", [P, E], I32), sb("blk_tab", [1, 2 * NBLK], I32)
        with ExitStack() as early:
            L, mask, m8 = sb("L", [P, NT, E], ctx=early), sb("mask", [P, NT, E], ctx=early), sb("m8", [P, NT, K], ctx=early)
            with ExitStack() as first:
                qT, kT, V = sb("qT", [P, DC, T], ctx=first), sb("kT", [P, DC, T], ctx=first), sb("V", [P, NT, D], ctx=first)
                project(nc, a["x"], a["ctxT"], a["attn_wT"], a["rows"], X, qT, kT, V, ident)
                if stop == 1:
                    return dump(nc, dbg, [qT[:, :, :], kT[:, :, :], V[:, :, :]])
                attend(nc, qT, kT, V, ident)
                if stop == 2:
                    return dump(nc, dbg, [qT[:, :, :]])
                route(nc, a, h_dram, X, qT, L, mask, m8, ident)
                if stop == 3:
                    return dump(nc, dbg, [X[:, :, :], L[:, :, :], mask[:, :, :]])
            place(nc, a, L, mask, m8, slot8, w8, blk_tok, endb, blk_tab, tab_dram)
            if stop == 4:
                return dump4(nc, dbg, [(slot8, [P, NT, K]), (w8, None), (blk_tok, [P, NBLK]), (blk_tab, [1, NBLK])])
        Wg, Wu, Wdn = sb("ffn_g", [P, DC, F]), sb("ffn_u", [P, DC, F]), sb("ffn_d", [P, FC, D])
        s_ffn, s_ctx = ctx.enter_context(nc.semaphore("s_ffn")), ctx.enter_context(nc.semaphore("s_ctx"))
        experts(nc, a, h_dram, y_dram, blk_tok, endb, blk_tab, ident,
                [Wg[:, :, :], Wu[:, :, :], Wdn[:, :, :]], [a["ffn_gT"], a["ffn_uT"], a["ffn_dT"]], s_ffn)
        mv, lnp = sb("mv", [P, NT, 2]), sb("lnp", [P, NT, 2])
        with ExitStack() as late:
            ctxT, ctxR = sb("memT_sb", [P, B, DC, S], ctx=late), sb("mem_sb", [P, NT, D], ctx=late)
            combine(nc, a, y_dram, X, slot8, w8, mv, lnp,
                    [(ctxT[:, :, :, :], a["memT"]), (ctxR[:, :, :], a["mem"])], s_ctx)
            if stop == 5:
                return dump(nc, dbg, [X[:, :, :]])
            read_memory(nc, a, X, mv, lnp, ctxT, ctxR, s_ctx, ident)
            if stop == 6:
                return dump(nc, dbg, [X[:, :, :]])
        feed_forward(nc, a, out, X, lnp, Wg, Wu, Wdn, s_ffn, ident)


def dump4(nc, dbg, srcs):
    with nc.sbuf_tensor("d0", [P, NT, K], F32) as d0, nc.sbuf_tensor("d2", [P, NBLK], F32) as d2, nc.sbuf_tensor("d3", [1, NBLK], F32) as d3, \
            nc.semaphore("dmp") as s, nc.semaphore("dmp2") as s2, nc.Block() as block:
        @block.vector
        def _(eng):
            eng.tensor_copy(d0[:, :, :], srcs[0][0][:, :, :])
            eng.tensor_copy(d2[:, :], srcs[2][0][:, :])
            eng.tensor_copy(d3[:, :], srcs[3][0][:, :].rearrange("o (b v) -> o b v", v=2)[:, :, 0]).then_inc(s, 1)
        @block.sync
        def _(eng):
            eng.wait_ge(s, 1)
            for n, ap in enumerate([d0[:, :, :], srcs[1][0][:, :, :], d2[:, :], d3[:, :]]):
                eng.dma_start(dbg[n], ap).then_inc(s2, 16)
            eng.wait_ge(s2, 64)


def dump(nc, dbg, aps):
    with nc.semaphore("dump") as s, nc.Block() as block:
        @block.sync
        def _(eng):
            for n, ap in enumerate(aps):
                eng.dma_start(dbg[n], ap).then_inc(s, 16)
            eng.wait_ge(s, 16 * len(aps))


def lay_out(i):
    f = {k: np.ascontiguousarray(v) for k, v in i.items()}
    chunks = lambda wT: np.ascontiguousarray(wT.reshape(-1, P, wT.shape[-1]).transpose(1, 0, 2))
    tok = f["ctx_2048"].reshape(NT, P, DC, P)
    mem = f["ctx_2048"].reshape(B, S, DC, P)
    gu = np.concatenate([f["L0_ffn_w_gate"], f["L0_ffn_w_up"]], axis=2)
    return {
        "x": f["x"].reshape(T, D),
        "ctxT": np.ascontiguousarray(tok.transpose(0, 3, 2, 1)),
        "attn_wT": np.stack([chunks(f["L0_xattn_" + n + "_w"].T) for n in ("q", "k_img", "v_img", "o")]),
        "rows": np.stack([f["L0_xattn_" + n] for n in ("q_b", "norm_q_w", "k_img_b", "norm_k_img_w", "v_img_b", "o_b")]),
        "router_wT": chunks(f["L0_ffn_gate_weight"].T),
        "exp_gu": np.ascontiguousarray(gu.reshape(E, DC, P, 2 * I).transpose(0, 2, 1, 3)),
        "exp_d": np.ascontiguousarray(f["L0_ffn_w_down"].reshape(E, 2, IH, D).transpose(0, 2, 1, 3)),
        "memT": np.ascontiguousarray(mem.transpose(3, 0, 2, 1)),
        "mem": chunks(f["ctx_2048"].reshape(T, D)),
        "mask": f["mask_BxS2_bk0"],
        "ffn_gT": chunks(f["L1_ffn_gate_w"].T),
        "ffn_uT": chunks(f["L1_ffn_up_w"].T),
        "ffn_dT": chunks(f["L1_ffn_down_w"].T),
        "gate_s": np.ascontiguousarray(f["L1_ffn_gate_s"].reshape(FC, P).T),
        "up_s": np.ascontiguousarray(f["L1_ffn_up_s"].reshape(FC, P).T),
        "down_s": f["L1_ffn_down_s"],
    }


def kernel(_stop=99, _dbg=(), **inputs):
    import concourse.bacc as bacc
    from concourse.bass_utils import run_bass_kernel_spmd

    arrays = lay_out(inputs)
    nc = bacc.Bacc("TRN2", target_bir_lowering=False, num_devices=1)
    a = {n: nc.dram_tensor("in_" + n, v.shape, mybir.dt.from_np(v.dtype), kind="ExternalInput").ap() for n, v in arrays.items()}
    out = nc.dram_tensor("out", (T, D), F32, kind="ExternalOutput").ap()
    dbg = [nc.dram_tensor(f"dbg{n}", s, F32, kind="ExternalOutput").ap() for n, s in enumerate(_dbg)]
    build(nc, a, out, _stop, dbg)
    got = run_bass_kernel_spmd(nc, [{"in_" + n: v for n, v in arrays.items()}], core_ids=[0])
    return got.results[0]["out"].reshape(B, S, D)
```

```python
from contextlib import ExitStack

import numpy as np
import concourse.bass as bass
from concourse import mybir

F32 = mybir.dt.float32
F16 = mybir.dt.float16
I32 = mybir.dt.int32
U32 = mybir.dt.uint32
U8 = mybir.dt.uint8
ALU = mybir.AluOpType
ACT = mybir.ActivationFunctionType
AX = mybir.AxisListType

P = 128
B, S, D = 8, 256, 512
T = B * S
NT = T // P
TPB = S // P
DC = D // P
NH, HD = 16, 32
HG = P // HD
E, K, I = 64, 8, 192
NBLK = T * K // P + E
GB = 4
NTAB = NBLK + GB
IH = I // 2
NWB = 4
F, FC = 1408, 1408 // P
LN_EPS, RMS_EPS = 1e-5, 1e-6
SLOT_TOP = 65536.0


class Steps:

    def __init__(self, nc, ctx, name, names, lag=4):
        self.sem, self.names, self.lag, self.at = ctx.enter_context(nc.semaphore(name)), names, lag, 0

    def start(self, eng):
        eng.sem_inc(self.sem, self.lag * len(self.names))

    def done(self, ins, name):
        assert self.names[self.at] == name, (self.names[self.at], name)
        self.at = (self.at + 1) % len(self.names)
        ins.then_inc(self.sem, 1)

    def value(self, unit, name):
        return (unit + self.lag) * len(self.names) + self.names.index(name) + 1

    def wait(self, eng, unit, name):
        eng.wait_ge(self.sem, self.value(unit, name))


def apart(eng, sem):
    eng.sem_inc(sem, 1)


class Chain:

    def __init__(self, nc, ctx, name, eng=None):
        self.sem, self.n, self.eng = ctx.enter_context(nc.semaphore(name)), 0, eng

    def __call__(self, ins):
        self.n += 1
        ins.then_inc(self.sem, 1)
        self.eng.wait_ge(self.sem, self.n)


def project(nc, x_in, ctxT_in, wT_in, rows_in, X, qT, kT, V, ident):
    with ExitStack() as ctx:
        sb = lambda name, shape, dt=F32: ctx.enter_context(nc.sbuf_tensor(name, shape, dt))
        ps = lambda name, shape, dt=F32: ctx.enter_context(nc.psum_tensor(name, shape, dt))
        sem = lambda name: ctx.enter_context(nc.semaphore(name))
        W = sb("proj_w", [P, 3, DC, D])
        rows = sb("proj_rows", [P, 5, D])
        ctxT = sb("ctxT", [P, 2, DC, P])
        stats, mv = sb("ln1_stats", [P, NT, 6]), sb("ln1_mv", [P, NT, 2])
        lnp = sb("ln1_scale_shift", [P, NT, 2])
        rstd, shift = lnp[:, :, 0], lnp[:, :, 1]
        xn, xnT = sb("xn", [P, 2, D]), sb("xnT", [P, 2, DC, P])
        xc, lnc = sb("xc", [P, D]), sb("ln1_col", [P, 2])
        kb, qb, kn, qn, sq = sb("kb", [P, D]), sb("qb", [P, D]), sb("kn", [P, D]), sb("qn", [P, D]), sb("sq", [P, D])
        kms, qms, krs, qrs = sb("kms", [P, 2]), sb("qms", [P, 2]), sb("krs", [P, 1]), sb("qrs", [P, 1])
        pxT, pk, pq, pv, pkT, pqT = [ps(n, [P, D]) for n in ("pxT", "pk", "pq", "pv", "pkT", "pqT")]
        s_x, s_w, s_rows, s_id = sem("p_x"), [sem(f"p_w{i}") for i in range(3)], sem("p_rows"), sem("p_id")
        s_c = [sem(f"p_c{i}") for i in range(2)]
        s_apart = sem("p_apart")
        eps, s_eps = sb("rms_eps", [P, 1]), sem("p_eps")
        s_mv, s_sd, s_ln = sem("p_mv"), sem("p_sd"), sem("p_ln")
        pe = Steps(nc, ctx, "p_pe", ["xT", "k", "q", "v", "kT", "qT"])
        dve = Steps(nc, ctx, "p_dve", ["xT", "kb", "qb", "kr", "kn", "qr", "qn", "vb"])
        act = Steps(nc, ctx, "p_act", ["ksq", "ksd", "qsq", "qsd", "kT", "qT"])
        pool = Steps(nc, ctx, "p_pool", ["xc", "lnc", "xn"])
        block = ctx.enter_context(nc.Block())

        @block.sync
        def _(eng):
            for n in range(4):
                eng.dma_start(X[:, 4 * n:4 * n + 4, :],
                              x_in.rearrange("(n t p) d -> n p t d", p=P, t=4)[n]).then_inc(s_x, 16)
            eng.dma_start(W[:, 1, :, :], wT_in[1]).then_inc(s_w[1], 16)
            with eng.Fori(0, NT // 2) as i:
                for par in range(2):
                    t = i * 2 + par
                    pe.wait(eng, t - 2, "v")
                    eng.dma_start(ctxT[:, par, :, :], ctxT_in[t, :, :, :]).then_inc(s_c[par], 16)

        @block.scalar
        def _(eng):
            act.start(eng)
            eng.dma_start(W[:, 0, :, :], wT_in[0]).then_inc(s_w[0], 16)
            eng.dma_start(rows[:, :, :], rows_in[0:5, :].unsqueeze(0).to_broadcast([P, 5, D])).then_inc(s_rows, 16)
            eng.dma_start(W[:, 2, :, :], wT_in[2]).then_inc(s_w[2], 16)
            eng.wait_ge(s_mv, 1)
            eng.activation(rstd, mv[:, :, 1], ACT.Sqrt).then_inc(s_sd, 1)
            eng.wait_ge(s_eps, 1)
            with eng.Fori(0, NT) as t:
                for x, psum, sbuf in (("k", kb, kms), ("q", qb, qms)):
                    dve.wait(eng, t, x + "b")
                    if x == "k":
                        dve.wait(eng, t - 1, "kr")
                        dve.wait(eng, t - 1, "qr")
                    act.done(eng.activation(sq[:, :], psum[:, :], ACT.Square, accum_out=sbuf[:, 0:1]), x + "sq")
                    act.wait(eng, t, x + "sq")
                    act.done(eng.activation(sbuf[:, 1:2], sbuf[:, 0:1], ACT.Sqrt, bias=eps[:, 0:1], scale=1.0 / D), x + "sd")
                for x, psum, dst in (("k", pkT, kT), ("q", pqT, qT)):
                    pe.wait(eng, t, x + "T")
                    act.done(eng.activation(dst[:, :, bass.ts(t, P)], psum[:, :].rearrange("p (c n) -> p c n", c=DC),
                                            ACT.Copy), x + "T")

        @block.gpsimd
        def _(eng):
            pool.start(eng)
            eng.memset(ident[:, :], 0.0).then_inc(s_id, 1)
            eng.wait_ge(s_id, 1)
            eng.affine_select(out=ident[:, :], in_=ident[:, :], compare_op=ALU.not_equal, fill=1.0, base=0,
                              pattern=[[-1, P]], channel_multiplier=1).then_inc(s_id, 1)
            eng.wait_ge(s_ln, 1)
            with eng.Fori(0, NT // 2) as i:
                for par in range(2):
                    t = i * 2 + par
                    pool.wait(eng, t - 1, "xn")
                    pool.done(eng.tensor_copy(xc[:, :], X[:, t, :]), "xc")
                    pool.done(eng.tensor_copy(lnc[:, :], lnp[:, t, :]), "lnc")
                    pool.wait(eng, t, "lnc")
                    pe.wait(eng, t - 2, "xT")
                    apart(eng, s_apart)
                    pool.done(eng.tensor_scalar(xn[:, par, :], xc[:, :], lnc[:, 0:1], lnc[:, 1:2], ALU.mult, ALU.add), "xn")

        @block.tensor
        def _(eng):
            pe.start(eng)
            eng.wait_ge(s_id, 2)
            for s in s_w:
                eng.wait_ge(s, 16)
            with eng.Fori(0, NT // 2) as i:
                for par in range(2):
                    t = i * 2 + par
                    pool.wait(eng, t, "xn")
                    dve.wait(eng, t - 1, "xT")
                    for c in range(DC):
                        m = eng.transpose(pxT[:, bass.ts(c, P)], xn[:, par, bass.ts(c, P)], ident[:, :])
                    pe.done(m, "xT")
                    eng.wait_ge(s_c[par], 16 * (i + 1))
                    for x, psum, lhs, w, free in (("k", pk, ctxT, 1, "kb"), ("q", pq, xnT, 0, "qb"), ("v", pv, ctxT, 2, "vb")):
                        if x == "q":
                            dve.wait(eng, t, "xT")
                        dve.wait(eng, t - 1, free)
                        for c in range(DC):
                            m = eng.matmul(psum[:, :], lhs[:, par, c, :], W[:, w, c, :], start=c == 0, stop=c == DC - 1)
                        pe.done(m, x)
                    for x, psum, src in (("k", pkT, kn), ("q", pqT, qn)):
                        dve.wait(eng, t, x + "n")
                        act.wait(eng, t - 1, x + "T")
                        for c in range(DC):
                            m = eng.transpose(psum[:, bass.ts(c, P)], src[:, bass.ts(c, P)], ident[:, :])
                        pe.done(m, x + "T")

        @block.vector
        def _(eng):
            dve.start(eng)
            link = Chain(nc, ctx, "p_link", eng)
            eng.wait_ge(s_x, 64)
            for t in range(NT):
                last = eng.bn_stats(stats[:, t, :], X[:, t, :])
            link(last)
            for t in range(NT):
                last = eng.bn_aggr(mv[:, t, :], stats[:, t, :])
            link(last)
            link(eng.tensor_scalar_add(mv[:, :, 1], mv[:, :, 1], LN_EPS))
            eng.sem_inc(s_mv, 1)
            eng.wait_ge(s_sd, 1)
            link(eng.reciprocal(rstd, rstd))
            eng.scalar_tensor_tensor(shift, mv[:, :, 0], -1.0, rstd, ALU.mult, ALU.mult).then_inc(s_ln, 1)
            eng.wait_ge(s_rows, 16)
            link(eng.tensor_scalar_mul(rows[:, 3, :], rows[:, 3, :], -HD ** -0.5))
            link(eng.memset(eps[:, :], RMS_EPS))
            eng.sem_inc(s_eps, 1)
            with eng.Fori(0, NT // 2) as i:
                for par in range(2):
                    t = i * 2 + par
                    pe.wait(eng, t, "xT")
                    pe.wait(eng, t - 2, "q")
                    dve.done(eng.tensor_copy(xnT[:, par, :, :], pxT[:, :].rearrange("p (c n) -> p c n", c=DC)), "xT")
                    for x, psum, dst, bias in (("k", pk, kb, 2), ("q", pq, qb, 0)):
                        pe.wait(eng, t, x)
                        act.wait(eng, t - 1, x + "sq")
                        dve.done(eng.tensor_tensor(dst[:, :], psum[:, :], rows[:, bias, :], ALU.add), x + "b")
                    for x, src, root, inv, dst, w in (("k", kb, kms, krs, kn, 3), ("q", qb, qms, qrs, qn, 1)):
                        act.wait(eng, t, x + "sd")
                        dve.done(eng.reciprocal(inv[:, :], root[:, 1:2]), x + "r")
                        dve.wait(eng, t, x + "r")
                        pe.wait(eng, t - 1, x + "T")
                        dve.done(eng.scalar_tensor_tensor(dst[:, :], src[:, :], inv[:, 0:1], rows[:, w, :],
                                                          ALU.mult, ALU.mult), x + "n")
                    pe.wait(eng, t, "v")
                    dve.done(eng.tensor_tensor(V[:, t, :], pv[:, :], rows[:, 4, :], ALU.add), "vb")


def attend(nc, qT, kT, V, ident, y_dram):
    GH = range(HG)
    with ExitStack() as ctx:
        sb = lambda name, shape, dt=F32: ctx.enter_context(nc.sbuf_tensor(name, shape, dt))
        ps = lambda name, shape, dt=F32: ctx.enter_context(nc.psum_tensor(name, shape, dt))
        qg, kg, vg = sb("qg", [P, 2, S]), sb("kg", [P, 2, S]), sb("vg", [P, 2, TPB, P])
        low, tot, inv = sb("low", [P, 2, HG, TPB]), sb("tot", [P, 2, HG, TPB]), sb("inv", [P, 2, HG, TPB])
        prob = sb("prob", [P, 2, HG, TPB, S])
        probT = sb("probT", [P, 2, HG, TPB, S])
        pS = [ps(f"pS{j}", [P, TPB, S]) for j in GH]
        pT = [ps(f"pT{j}", [P, TPB, S]) for j in range(2)]
        pO = [ps(f"pO{j}", [P, S]) for j in range(2)]
        peS = Steps(nc, ctx, "a_peS", [f"S{j}" for j in GH])
        peT = Steps(nc, ctx, "a_peT", [f"T{j}" for j in GH] + ["O"])
        dveM = Steps(nc, ctx, "a_dveM", [f"M{j}" for j in GH])
        dveR = Steps(nc, ctx, "a_dveR", [f"R{j}" for j in GH])
        dveT = Steps(nc, ctx, "a_dveT", [f"T{j}" for j in GH])
        actE = Steps(nc, ctx, "a_actE", [f"E{j}" for j in GH])
        actO = Steps(nc, ctx, "a_actO", ["O"])
        poolC = Steps(nc, ctx, "a_poolC", ["q", "k", "v"])
        poolN = Steps(nc, ctx, "a_poolN", [f"N{j}" for j in GH])
        zero, s_zero, s_rest = sb("zero", [P, D]), ctx.enter_context(nc.semaphore("a_zero")), ctx.enter_context(nc.semaphore("a_rest"))
        block = ctx.enter_context(nc.Block())

        @block.sync
        def _(eng):
            rest = y_dram.rearrange("(n p) d -> n p d", p=P)[T * K // P:NBLK]
            eng.wait_ge(s_zero, 1)
            for n in range(NBLK - T * K // P):
                eng.dma_start(rest[n], zero[:, :]).then_inc(s_rest, 16)
            eng.wait_ge(s_rest, 16 * (NBLK - T * K // P))

        def units(eng, one):
            with eng.Fori(0, B - 1) as b:
                for g in range(DC):
                    one(b, g, lambda n: True)
            for g in range(DC):
                one(B - 1, g, lambda n, g=g: g + n < DC)

        def scores(eng, u, par):
            poolC.wait(eng, u, "k")
            for j in GH:
                actE.wait(eng, u - 1, f"E{j}")
                for h in range(TPB):
                    m = eng.matmul(pS[j][:, h, :], qg[bass.ts(j, HD), par, bass.ts(h, P)],
                                   kg[bass.ts(j, HD), par, :], start=True, stop=True)
                peS.done(m, f"S{j}")

        @block.tensor
        def _(eng):
            peS.start(eng)
            peT.start(eng)
            scores(eng, 0, 0)

            def one(b, g, later):
                u, par = b * DC + g, g % 2
                if later(1):
                    scores(eng, u + 1, 1 - par)
                for j in GH:
                    poolN.wait(eng, u, f"N{j}")
                    if j < 2:
                        dveT.wait(eng, u - 1, f"T{j + 2}")
                    else:
                        dveT.wait(eng, u, f"T{j - 2}")
                    for kt in range(TPB):
                        for h in range(TPB):
                            m = eng.transpose(pT[j % 2][:, kt, bass.ts(h, P)], prob[:, par, j, h, bass.ts(kt, P)], ident[:, :])
                    peT.done(m, f"T{j}")
                poolC.wait(eng, u, "v")
                actO.wait(eng, u - 2, "O")
                for j in GH:
                    dveT.wait(eng, u, f"T{j}")
                    for kt in range(TPB):
                        m = eng.matmul(pO[par][bass.ts(j, HD), :], vg[:, par, kt, bass.ts(j, HD)],
                                       probT[:, par, j, kt, :], start=kt == 0, stop=kt == TPB - 1)
                peT.done(m, "O")

            units(eng, one)

        @block.vector
        def _(eng):
            dveM.start(eng)
            dveR.start(eng)
            dveT.start(eng)

            def lows(u, par, j):
                peS.wait(eng, u, f"S{j}")
                actE.wait(eng, u - 2, f"E{j}")
                dveM.done(eng.tensor_reduce(low[:, par, j, :], pS[j][:, :, :], axis=AX.X, op=ALU.min), f"M{j}")

            for j in GH:
                lows(0, 0, j)

            def one(b, g, later):
                u, par = b * DC + g, g % 2
                for j in GH:
                    actE.wait(eng, u, f"E{j}")
                    poolN.wait(eng, u - 2, f"N{j}")
                    dveR.done(eng.reciprocal(inv[:, par, j, :], tot[:, par, j, :]), f"R{j}")
                    if later(1):
                        lows(u + 1, 1 - par, j)
                for j in GH:
                    peT.wait(eng, u, f"T{j}")
                    peT.wait(eng, u - 2, "O")
                    dveT.done(eng.tensor_copy(probT[:, par, j, :, :], pT[j % 2][:, :, :]), f"T{j}")

            units(eng, one)

        @block.scalar
        def _(eng):
            actE.start(eng)
            actO.start(eng)

            def exps(u, par):
                for j in GH:
                    dveM.wait(eng, u, f"M{j}")
                    peT.wait(eng, u - 2, f"T{j}")
                    dveR.wait(eng, u - 2, f"R{j}")
                    for h in range(TPB):
                        a = eng.activation(prob[:, par, j, h, :], pS[j][:, h, :], ACT.Exp, bias=low[:, par, j, h:h + 1],
                                           scale=-1.0, accum_out=tot[:, par, j, h:h + 1])
                    actE.done(a, f"E{j}")

            exps(0, 0)

            def one(b, g, later):
                u, par = b * DC + g, g % 2
                if later(1):
                    exps(u + 1, 1 - par)
                peT.wait(eng, u, "O")
                actO.done(eng.activation(qT[:, g, bass.ts(b, S)], pO[par][:, :], ACT.Copy), "O")

            units(eng, one)

        @block.gpsimd
        def _(eng):
            poolC.start(eng)
            poolN.start(eng)
            eng.memset(zero[:, :], 0.0).then_inc(s_zero, 1)

            def copies(b, g):
                u, par = b * DC + g, g % 2
                peS.wait(eng, u - 2, f"S{HG - 1}")
                poolC.done(eng.tensor_copy(qg[:, par, :], qT[:, g, bass.ts(b, S)]), "q")
                poolC.done(eng.tensor_copy(kg[:, par, :], kT[:, g, bass.ts(b, S)]), "k")
                peT.wait(eng, u - 2, "O")
                poolC.done(eng.tensor_copy(vg[:, par, :, :], V[:, bass.ts(b, TPB), bass.ts(g, P)]), "v")

            copies(0, 0)
            copies(0, 1)

            def one(b, g, later):
                u, par = b * DC + g, g % 2
                for j in GH:
                    dveR.wait(eng, u, f"R{j}")
                    w = prob[:, par, j, :, :]
                    poolN.done(eng.tensor_tensor(w, w, inv[:, par, j, :].unsqueeze(2).to_broadcast([P, TPB, S]), ALU.mult), f"N{j}")
                if later(2):
                    copies(b + (g + 2) // DC, (g + 2) % DC)

            units(eng, one)


def by_unit(eng, one, n, unroll, peel):
    assert (n - peel) % unroll == 0 and peel % unroll == 0
    with eng.Fori(0, (n - peel) // unroll) as i:
        for u in range(unroll):
            one(i * unroll + u, u, lambda k: True)
    for t in range(n - peel, n):
        one(t, t % unroll, lambda k, t=t: t + k < n)


def route(nc, a, h_dram, X, qT, L, mask, m8, ident):
    with ExitStack() as ctx:
        sb = lambda name, shape, dt=F32: ctx.enter_context(nc.sbuf_tensor(name, shape, dt))
        ps = lambda name, shape, dt=F32: ctx.enter_context(nc.psum_tensor(name, shape, dt))
        sem = lambda name: ctx.enter_context(nc.semaphore(name))
        Wo, ob, Wr = sb("wo", [P, DC, D]), sb("ob", [P, D]), sb("router_w", [P, DC, E])
        oT, add, h, hT = sb("oT", [P, 2, DC, P]), sb("add", [P, D]), sb("h", [P, 2, D]), sb("hT", [P, 2, DC, P])
        stats, mv, lnp = sb("ln2_stats", [P, NT, 6]), sb("ln2_mv", [P, NT, 2]), sb("ln2_scale_shift", [P, NT, 2])
        logit, rest, top = sb("logit", [P, E]), sb("rest", [P, E]), sb("top", [P, K])
        po, ph, pl = [ps(f"po{i}", [P, D]) for i in range(2)], [ps(f"ph{i}", [P, D]) for i in range(2)], [ps(f"pl{i}", [P, E]) for i in range(2)]
        s_w, s_ob, s_r, s_h = sem("r_w"), sem("r_ob"), sem("r_r"), [sem(f"r_h{i}") for i in range(2)]
        s_apart, s_var, s_root, s_ln = sem("r_apart"), sem("r_var"), sem("r_root"), sem("r_ln")
        pool = Steps(nc, ctx, "r_pool", ["oT"])
        peO, peH, peL = Steps(nc, ctx, "r_peO", ["o"]), Steps(nc, ctx, "r_peH", ["hT"]), Steps(nc, ctx, "r_peL", ["l"])
        dveA = Steps(nc, ctx, "r_dveA", ["add", "x", "stats"])
        dveH = Steps(nc, ctx, "r_dveH", ["hT"])
        dveB = Steps(nc, ctx, "r_dveB", ["l", "top", "rest", "mask", "L", "m8"])
        act = Steps(nc, ctx, "r_act", ["h"])
        block = ctx.enter_context(nc.Block())

        @block.sync
        def _(eng):
            eng.dma_start(Wo[:, :, :], a["attn_wT"][3]).then_inc(s_w, 16)
            eng.dma_start(ob[:, :], a["rows"][5:6, :].to_broadcast([P, D])).then_inc(s_ob, 16)
            eng.dma_start(Wr[:, :, :], a["router_wT"]).then_inc(s_r, 16)

            def one(t, u, later):
                act.wait(eng, t, "h")
                eng.dma_start(h_dram[bass.ts(t, P), :], h[:, u, :]).then_inc(s_h[u], 16)

            by_unit(eng, one, NT, 2, 0)
            for s in s_h:
                eng.wait_ge(s, 16 * NT // 2)

        @block.gpsimd
        def _(eng):
            pool.start(eng)

            def one(t, u, later):
                peO.wait(eng, t - 2, "o")
                pool.done(eng.tensor_copy(oT[:, u, :, :], qT[:, :, bass.ts(t, P)]), "oT")

            by_unit(eng, one, NT, 2, 0)

        @block.tensor
        def _(eng):
            for x in (peO, peH, peL):
                x.start(eng)
            eng.wait_ge(s_w, 16)

            def project_out(t, u, later):
                pool.wait(eng, t, "oT")
                dveA.wait(eng, t - 2, "add")
                for c in range(DC):
                    m = eng.matmul(po[u][:, :], oT[:, u, c, :], Wo[:, c, :], start=c == 0, stop=c == DC - 1)
                peO.done(m, "o")

            by_unit(eng, project_out, NT, 2, 0)

            def turn(t, u):
                act.wait(eng, t, "h")
                dveH.wait(eng, t - 2, "hT")
                for c in range(DC):
                    m = eng.transpose(ph[u][:, bass.ts(c, P)], h[:, u, bass.ts(c, P)], ident[:, :])
                peH.done(m, "hT")

            turn(0, 0)
            eng.wait_ge(s_r, 16)

            def one(t, u, later):
                if later(1):
                    turn(t + 1, 1 - u)
                dveH.wait(eng, t, "hT")
                dveB.wait(eng, t - 2, "l")
                for c in range(DC):
                    m = eng.matmul(pl[u][:, :], hT[:, u, c, :], Wr[:, c, :], start=c == 0, stop=c == DC - 1)
                peL.done(m, "l")

            by_unit(eng, one, NT, 2, 2)

        @block.scalar
        def _(eng):
            act.start(eng)
            eng.wait_ge(s_var, 1)
            eng.activation(lnp[:, :, 0], mv[:, :, 1], ACT.Sqrt).then_inc(s_root, 1)
            eng.wait_ge(s_ln, 1)

            def norm(t, u):
                peH.wait(eng, t - 2, "hT")
                act.done(eng.activation(h[:, u, :], X[:, t, :], ACT.Identity, bias=lnp[:, t, 1:2], scale=lnp[:, t, 0:1]), "h")

            for u in range(2):
                norm(u, u)
            with eng.Fori(1, NT // 2) as i:
                for u in range(2):
                    eng.wait_ge(s_h[u], i * 16)
                    norm(i * 2 + u, u)

        @block.vector
        def _(eng):
            for x in (dveA, dveH, dveB):
                x.start(eng)
            link = Chain(nc, ctx, "r_link", eng)
            eng.wait_ge(s_ob, 16)

            def residual(t, u, later):
                peO.wait(eng, t, "o")
                dveA.done(eng.tensor_tensor(add[:, :], po[u][:, :], ob[:, :], ALU.add), "add")
                dveA.wait(eng, t, "add")
                dveA.done(eng.tensor_tensor(X[:, t, :], X[:, t, :], add[:, :], ALU.add), "x")
                dveA.wait(eng, t, "x")
                apart(eng, s_apart)
                dveA.done(eng.bn_stats(stats[:, t, :], X[:, t, :]), "stats")

            by_unit(eng, residual, NT, 2, 0)
            dveA.wait(eng, NT - 1, "stats")
            for t in range(NT):
                last = eng.bn_aggr(mv[:, t, :], stats[:, t, :])
            link(last)
            norm_scales(nc, ctx, "r", eng, link, mv, lnp, s_var, s_root)
            eng.sem_inc(s_ln, 1)

            def turned(t, u):
                peH.wait(eng, t, "hT")
                peL.wait(eng, t - 2, "l")
                dveH.done(eng.tensor_copy(hT[:, u, :, :], ph[u][:, :].rearrange("p (c n) -> p c n", c=DC)), "hT")

            turned(0, 0)

            def one(t, u, later):
                if later(1):
                    turned(t + 1, 1 - u)
                peL.wait(eng, t, "l")
                dveB.wait(eng, t - 1, "m8")
                dveB.done(eng.tensor_copy(logit[:, :], pl[u][:, :]), "l")
                dveB.wait(eng, t, "l")
                apart(eng, s_apart)
                dveB.done(eng.max(top[:, :], logit[:, :]), "top")
                dveB.wait(eng, t, "top")
                apart(eng, s_apart)
                dveB.done(eng.match_replace(rest[:, :], top[:, :], logit[:, :], -3e38), "rest")
                dveB.wait(eng, t, "rest")
                dveB.done(eng.tensor_tensor(mask[:, t, :], logit[:, :], rest[:, :], ALU.not_equal), "mask")
                dveB.done(eng.tensor_copy(L[:, t, :], logit[:, :]), "L")
                dveB.done(eng.tensor_copy(m8[:, t, :], top[:, :]), "m8")

            by_unit(eng, one, NT, 2, 2)


def place(nc, a, L, mask, m8, slot8, w8, blk_tok, endb, blk_tab, tab_dram):
    with ExitStack() as ctx:
        sb = lambda name, shape, dt=F32: ctx.enter_context(nc.sbuf_tensor(name, shape, dt))
        ps = lambda name, shape, dt=F32: ctx.enter_context(nc.psum_tensor(name, shape, dt))
        sem = lambda name: ctx.enter_context(nc.semaphore(name))
        mask16, before, ones16 = sb("mask16", [P, NT * E], F16), sb("before", [P, P], F16), sb("ones16", [P, P], F16)
        total, inv = sb("total", [P, NT]), sb("winv", [P, NT])
        pre = sb("pre", [P, NT + 1, E])
        cnt_i, nblk, one_e, first, end = sb("cnt_i", [P, E], I32), sb("nblk", [P, E]), sb("one_e", [P, E]), sb("first", [P, E]), sb("end", [P, E])
        key, key8, hit = sb("key", [P, NT, E]), sb("key8", [P, NT, K]), sb("hit", [P, NT, E])
        slot_f, slot_i = sb("slot_f", [P, NT, K]), sb("slot_i", [P, NT, K], I32)
        row_i, blk_i, row_f, blk_f = sb("row_i", [P, NT, K], I32), sb("blk_i", [P, NT, K], I32), sb("row_f", [P, NT, K]), sb("blk_f", [P, NT, K])
        it_i, it_row, it_blk = sb("it_i", [P, NTAB], I32), sb("it_row", [P, P], F16), sb("it_blk", [P, NTAB], F16)
        tok_i, tok = sb("tok_i", [P, NT], I32), sb("tok", [P, NT])
        hotr, hotb = sb("hotr", [P, K, P], F16), sb("hotb", [P, K, NTAB], F16)
        b_i, b_f, be, tab = sb("b_i", [P, 2], I32), sb("b_f", [P, 2]), sb("be", [P, 2]), sb("tab", [P, 2, 2], I32)
        le = sb("le", [P, E])
        prank, pcnt = [ps(f"prank{i}", [P, 512]) for i in range(2)], [ps(f"pcnt{i}", [P, 512]) for i in range(2)]
        plist = ps("plist", [P, NTAB])
        s_exp, s_iota, s_rank, s_m16, s_tab, s_tab2, s_ls = sem("l_exp"), sem("l_iota"), sem("l_rank"), sem("l_m16"), sem("l_tab"), sem("l_tab2"), sem("l_ls")
        s_lsub, s_list, s_pre = sem("l_lsub"), sem("l_list"), sem("l_pre")
        dveP = Steps(nc, ctx, "l_dveP", ["pre"])
        dveH = Steps(nc, ctx, "l_dveH", [f"h{k}" for k in range(K)])
        peL = Steps(nc, ctx, "l_peL", [f"l{k}" for k in range(K)])
        dual = lambda t, banks: banks[t // 8][:, bass.ts(t % 8, E)]
        block = ctx.enter_context(nc.Block())

        @block.gpsimd
        def _(eng):
            link = Chain(nc, ctx, "l_poolc", eng)
            link(eng.iota(it_i[:, :], pattern=[[1, NTAB]], base=0, channel_multiplier=0))
            link(eng.tensor_copy(it_row[:, :], it_i[:, 0:P]))
            link(eng.tensor_copy(it_blk[:, :], it_i[:, :]))
            link(eng.iota(tok_i[:, :], pattern=[[P, NT]], base=0, channel_multiplier=1))
            link(eng.tensor_copy(tok[:, :], tok_i[:, :]))
            link(eng.iota(b_i[:, :], pattern=[[P, 2]], base=0, channel_multiplier=1))
            link(eng.tensor_copy(b_f[:, :], b_i[:, :]))
            link(eng.memset(ones16[:, :], 1.0))
            link(eng.affine_select(out=before[:, :], in_=ones16[:, :], compare_op=ALU.is_gt, fill=0.0, base=0,
                                   pattern=[[1, P]], channel_multiplier=-1))
            eng.sem_inc(s_iota, 1)

        @block.tensor
        def _(eng):
            peL.start(eng)
            eng.wait_ge(s_iota, 1)
            eng.wait_ge(s_m16, 1)
            for i in range(2):
                eng.matmul(prank[i][:, :], before[:, :], mask16[:, bass.ts(i, 512)], start=True, stop=True)
                m = eng.matmul(pcnt[i][:, :], ones16[:, :], mask16[:, bass.ts(i, 512)], start=True, stop=True)
            m.then_inc(s_rank, 1)

            def one(t, start, stop):
                for k in range(K):
                    dveH.wait(eng, t, f"h{k}")
                    peL.done(eng.matmul(plist[:, :], hotr[:, k, :], hotb[:, k, :], start=start and k == 0,
                                        stop=stop and k == K - 1), f"l{k}")

            one(0, True, False)
            with eng.Fori(1, NT - 1) as t:
                one(t, False, False)
            one(NT - 1, False, True)

        @block.scalar
        def _(eng):
            eng.wait_ge(s_lsub, 1)
            eng.activation(L[:, :, :], L[:, :, :], ACT.Exp).then_inc(s_exp, 1)

        @block.sync
        def _(eng):
            eng.wait_ge(s_tab, 1)
            eng.dma_start(tab_dram[0:P, :], tab[:, 0, :]).then_inc(s_tab2, 16)
            eng.dma_start(tab_dram[P:NTAB, :], tab[0:NTAB - P, 1, :]).then_inc(s_tab2, 16)
            eng.wait_ge(s_tab2, 32)
            eng.dma_start(blk_tab[0:1, :], tab_dram.rearrange("(o b) v -> o (b v)", o=1)).then_inc(s_tab2, 16)
            eng.wait_ge(s_tab2, 48)

        @block.vector
        def _(eng):
            dveP.start(eng)
            dveH.start(eng)
            link = Chain(nc, ctx, "l_dvec", eng)
            link(eng.tensor_copy(mask16[:, :], mask[:, :, :].rearrange("p t e -> p (t e)")))
            eng.sem_inc(s_m16, 1)
            link(eng.tensor_tensor(L[:, :, :], L[:, :, :], m8[:, :, 0:1].to_broadcast([P, NT, E]), ALU.subtract))
            eng.sem_inc(s_lsub, 1)
            link(eng.memset(pre[:, 0, :], 0.0))
            link(eng.memset(one_e[:, :], 1.0))
            eng.wait_ge(s_rank, 1)
            dveP.wait(eng, -1, "pre")
            for t in range(NT):
                link(eng.tensor_tensor(pre[:, t + 1, :], pre[:, t, :], dual(t, pcnt), ALU.add))
            link(eng.tensor_scalar_add(cnt_i[:, :], pre[:, NT, :], float(P - 1)))
            link(eng.tensor_scalar(cnt_i[:, :], cnt_i[:, :], P.bit_length() - 1, None, ALU.arith_shift_right))
            link(eng.tensor_copy(nblk[:, :], cnt_i[:, :]))
            link(eng.tensor_scalar_max(nblk[:, :], nblk[:, :], 1.0))
            link(eng.tensor_tensor_scan(end[:, :], one_e[:, :], nblk[:, :], 0.0, ALU.mult, ALU.add))
            link(eng.tensor_copy(endb[:, :], end[:, :]))
            link(eng.tensor_tensor(first[:, :], end[:, :], nblk[:, :], ALU.subtract))
            link(eng.tensor_scalar_mul(first[:, :], first[:, :], float(P)))
            eng.wait_ge(s_iota, 1)
            for i in range(2):
                link(eng.tensor_scalar(le[:, :], end[:, :], b_f[:, i:i + 1], None, ALU.is_le))
                link(eng.reduce_sum(be[:, i:i + 1], le[:, :], axis=AX.X))
            link(eng.tensor_scalar_min(be[:, :], be[:, :], float(E - 1)))
            link(eng.tensor_copy(tab[:, :, 1], be[:, :]))
            link(eng.tensor_scalar(tab[:, :, 1], tab[:, :, 1], NWB - 1, None, ALU.bitwise_and))
            link(eng.tensor_scalar_add(tab[:, :, 0], be[:, :], 1.0))
            eng.sem_inc(s_tab, 1)
            for i in range(2):
                half = slice(i * 8, i * 8 + 8)
                link(eng.tensor_tensor(key[:, half, :], prank[i][:, :].rearrange("p (t e) -> p t e", e=E), pre[:, half, :], ALU.add))
            link(eng.tensor_tensor(key[:, :, :], key[:, :, :], first[:, :].unsqueeze(1).to_broadcast([P, NT, E]), ALU.add))
            link(eng.tensor_scalar(key[:, :, :], key[:, :, :], -1.0, SLOT_TOP, ALU.mult, ALU.add))
            link(eng.tensor_tensor(key[:, :, :], key[:, :, :], mask[:, :, :], ALU.mult))
            for t in range(NT):
                last = eng.max(key8[:, t, :], key[:, t, :])
            link(last)
            link(eng.tensor_scalar(slot_f[:, :, :], key8[:, :, :], -1.0, SLOT_TOP, ALU.mult, ALU.add))
            link(eng.tensor_copy(slot8[:, :, :], slot_f[:, :, :]))
            link(eng.tensor_copy(slot_i[:, :, :], slot_f[:, :, :]))
            link(eng.tensor_scalar(row_i[:, :, :], slot_i[:, :, :], P - 1, None, ALU.bitwise_and))
            link(eng.tensor_scalar(blk_i[:, :, :], slot_i[:, :, :], P.bit_length() - 1, None, ALU.arith_shift_right))
            link(eng.tensor_copy(row_f[:, :, :], row_i[:, :, :]))
            link(eng.tensor_copy(blk_f[:, :, :], blk_i[:, :, :]))
            with eng.Fori(0, NT) as t:
                for k in range(K):
                    peL.wait(eng, t - 1, f"l{k}")
                    eng.tensor_scalar(hotr[:, k, :], it_row[:, :], row_f[:, t, k:k + 1], None, ALU.is_equal)
                    dveH.done(eng.tensor_scalar(hotb[:, k, :], it_blk[:, :], blk_f[:, t, k:k + 1], tok[:, bass.ds(t, 1)],
                                                ALU.is_equal, ALU.mult), f"h{k}")
            peL.wait(eng, NT - 1, f"l{K - 1}")
            link(eng.tensor_copy(blk_tok[:, :], plist[:, :]))
            eng.wait_ge(s_exp, 1)
            link(eng.tensor_tensor(L[:, :, :], L[:, :, :], mask[:, :, :], ALU.mult))
            link(eng.reduce_sum(total[:, :], L[:, :, :], axis=AX.X))
            link(eng.reciprocal(inv[:, :], total[:, :]))
            link(eng.tensor_tensor(L[:, :, :], L[:, :, :], inv[:, :].unsqueeze(2).to_broadcast([P, NT, E]), ALU.mult))
            for k in range(K):
                link(eng.tensor_tensor(hit[:, :, :], key[:, :, :], key8[:, :, k:k + 1].to_broadcast([P, NT, E]), ALU.is_equal))
                link(eng.tensor_tensor(hit[:, :, :], hit[:, :, :], L[:, :, :], ALU.mult))
                link(eng.reduce_sum(w8[:, :, k], hit[:, :, :], axis=AX.X))


def used_groups(eng, endb):
    end = eng.value_load(endb[0:1, E - 1:E], min_val=T * K // P, max_val=NBLK)
    return eng.snap((end + GB - 1) // GB, min_val=T * K // P // GB, max_val=NBLK // GB)


def norm_scales(nc, ctx, name, eng, link, mv, lnp, s_var, s_root):
    link(eng.tensor_scalar_add(mv[:, :, 1], mv[:, :, 1], LN_EPS))
    eng.sem_inc(s_var, 1)
    eng.wait_ge(s_root, 1)
    link(eng.reciprocal(lnp[:, :, 0], lnp[:, :, 0]))
    link(eng.scalar_tensor_tensor(lnp[:, :, 1], mv[:, :, 0], -1.0, lnp[:, :, 0], ALU.mult, ALU.mult))


def experts(nc, a, h_dram, y_dram, blk_tok, endb, blk_tab, ident, ffn_w, ffn_src, s_ffn):
    with ExitStack() as ctx:
        sb = lambda name, shape, dt=F32: ctx.enter_context(nc.sbuf_tensor(name, shape, dt))
        ps = lambda name, shape, dt=F32: ctx.enter_context(nc.psum_tensor(name, shape, dt))
        sem = lambda name: ctx.enter_context(nc.semaphore(name))
        Wgu, Wd = sb("wgu", [P, NWB * DC, 2 * I]), sb("wd", [IH, NWB * 2, D])
        idx = [sb(f"idx{u}", [P, 1], U32) for u in range(4)]
        xg, xT = sb("xg", [P, 4, D]), sb("bxT", [P, 2, DC, P])
        act_g, hid, hidT, y = sb("act_g", [P, 2, I]), sb("hid", [P, 2, I]), sb("hidT", [IH, 2, 2, P]), sb("y", [P, 2, D])
        px, pg, ph, py = [[ps(f"m_{n}{i}", [P, D]) for i in range(2)] for n in ("x", "g", "h", "y")]
        s_ix, s_g = [sem(f"m_ix{u}") for u in range(4)], [sem(f"m_g{u}") for u in range(4)]
        s_apart = sem("m_apart")
        s_w, s_ready, s_y = [sem(f"m_w{u}") for u in range(NWB)], sem("m_ready"), [sem(f"m_y{u}") for u in range(2)]
        peX, pe = Steps(nc, ctx, "m_peX", ["xT"]), Steps(nc, ctx, "m_pe", ["hT", "y"])
        peG = Steps(nc, ctx, "m_peG", ["g"])
        dveX, dveH, dveT = Steps(nc, ctx, "m_dveX", ["xT"]), Steps(nc, ctx, "m_dveH", ["h"]), Steps(nc, ctx, "m_dveT", ["hT"])
        actS, actY = Steps(nc, ctx, "m_actS", ["silu"]), Steps(nc, ctx, "m_actY", ["y"])
        poolI = Steps(nc, ctx, "m_poolI", ["idx"])
        block = ctx.enter_context(nc.Block())

        @block.sync
        def _(eng):
            def load(e, u):
                eng.dma_start(Wgu[:, bass.ts(u, DC), :], a["exp_gu"][e]).then_inc(s_w[u], 16)
                eng.dma_start(Wd[:, bass.ts(u, 2), :], a["exp_d"][e]).then_inc(s_w[u], 16)

            for u in range(NWB):
                load(u, u)
            eng.wait_ge(s_w[0], 32)
            eng.sem_inc(s_ready, 1)
            with eng.Fori(1, E // NWB) as i:
                for u in range(NWB):
                    eng.wait_ge(s_w[(u + 1) % NWB], (i + (u + 1) // NWB) * 32)
                    eng.sem_inc(s_ready, 1)
                    e = i * NWB + u
                    end = eng.value_load(endb[0:1, bass.ds(e - NWB, 1)], min_val=0, max_val=NBLK)
                    pe.wait(eng, end - 1, "y")
                    load(e, u)
            for u in range(1, NWB):
                eng.wait_ge(s_w[u], 32 * (E // NWB))
                eng.sem_inc(s_ready, 1)

        @block.gpsimd
        def _(eng):
            poolI.start(eng)

            def one(b, u, later):
                poolI.done(eng.tensor_copy(idx[u][:, :], blk_tok[:, bass.ds(b, 1)]), "idx")
                poolI.wait(eng, b, "idx")
                peX.wait(eng, b - 4, "xT")
                apart(eng, s_apart)
                eng.indirect_dma_start(xg[:, u, :], None, h_dram, bass.IndirectOffsetOnAxis(ap=idx[u][:, 0:1], axis=0)).then_inc(s_g[u], 16)

            last = used_groups(eng, endb)
            for u in range(GB):
                one(u, u, None)
            with eng.Fori(1, NTAB // GB) as i:
                with eng.If(i <= last):
                    for u in range(GB):
                        eng.wait_ge(s_g[u], i * 16)
                        one(i * GB + u, u, None)
            for u in range(GB):
                eng.wait_ge(s_g[u], (last + 1) * 16)
            apart(eng, s_apart)

        @block.tensor
        def _(eng):
            peX.start(eng)
            peG.start(eng)
            pe.start(eng)

            def turn(b, u, n):
                eng.wait_ge(s_g[u], n * 16)
                dveX.wait(eng, b - 2, "xT")
                for c in range(DC):
                    m = eng.transpose(px[u % 2][:, bass.ts(c, P)], xg[:, u, bass.ts(c, P)], ident[:, :])
                peX.done(m, "xT")

            def gate_up(b, u):
                ready = eng.value_load(blk_tab[0:1, bass.ds(b * 2, 1)], min_val=1, max_val=E)
                buf = eng.value_load(blk_tab[0:1, bass.ds(b * 2 + 1, 1)], min_val=0, max_val=NWB - 1)
                eng.wait_ge(s_ready, ready)
                dveX.wait(eng, b, "xT")
                dveH.wait(eng, b - 2, "h")
                for c in range(DC):
                    m = eng.matmul(pg[u % 2][:, 0:2 * I], xT[:, u % 2, c, :], Wgu[:, buf * DC + c, :], start=c == 0, stop=c == DC - 1)
                peG.done(m, "g")
                return buf

            turn(0, 0, 1)
            turn(1, 1, 1)
            gate_up(0, 0)

            def one(i, u, later, n):
                b, par = i * 4 + u, u % 2
                dveH.wait(eng, b, "h")
                dveT.wait(eng, b - 2, "hT")
                for c in range(2):
                    m = eng.transpose(ph[par][0:IH, bass.ts(c, P)], hid[:, par, bass.ts(c, IH)], ident[:, :])
                pe.done(m, "hT")
                if later(1):
                    gate_up(b + 1, (u + 1) % 4)
                if later(2):
                    turn(b + 2, (u + 2) % 4, n + 1 + (u + 2) // 4)
                buf = eng.value_load(blk_tab[0:1, bass.ds(b * 2 + 1, 1)], min_val=0, max_val=NWB - 1)
                dveT.wait(eng, b, "hT")
                actY.wait(eng, b - 2, "y")
                for c in range(2):
                    m = eng.matmul(py[par][:, :], hidT[:, par, c, :], Wd[:, buf * 2 + c, :], start=c == 0, stop=c == 1)
                pe.done(m, "y")

            groups = used_groups(eng, endb)
            with eng.Fori(0, NBLK // GB) as i:
                with eng.If(i < groups):
                    for u in range(GB):
                        one(i, u, lambda k: True, i)

        @block.vector
        def _(eng):
            dveX.start(eng)
            dveH.start(eng)
            dveT.start(eng)

            def turned(b, u):
                peX.wait(eng, b, "xT")
                peG.wait(eng, b - 2, "g")
                dveX.done(eng.tensor_copy(xT[:, u % 2, :, :], px[u % 2][:, :].rearrange("p (c n) -> p c n", c=DC)), "xT")

            def hidden(b, u):
                actS.wait(eng, b, "silu")
                pe.wait(eng, b - 2, "hT")
                dveH.done(eng.tensor_tensor(hid[:, u % 2, :], pg[u % 2][:, I:2 * I], act_g[:, u % 2, :], ALU.mult), "h")

            turned(0, 0)
            turned(1, 1)
            hidden(0, 0)

            def one(b, u, later):
                pe.wait(eng, b, "hT")
                pe.wait(eng, b - 2, "y")
                dveT.done(eng.tensor_copy(hidT[:, u % 2, :, :], ph[u % 2][0:IH, 0:2 * P].rearrange("p (c n) -> p c n", c=2)), "hT")
                if later(1):
                    hidden(b + 1, u + 1)
                if later(2):
                    turned(b + 2, u + 2)

            groups = used_groups(eng, endb)
            with eng.Fori(0, NBLK // GB) as i:
                with eng.If(i < groups):
                    for u in range(GB):
                        one(i * GB + u, u, lambda k: True)

        @block.scalar
        def _(eng):
            actS.start(eng)
            actY.start(eng)
            for dst, src in zip(ffn_w, ffn_src):
                eng.dma_start(dst, src).then_inc(s_ffn, 16)

            def silu(b, u):
                peG.wait(eng, b, "g")
                dveH.wait(eng, b - 2, "h")
                actS.done(eng.activation(act_g[:, u % 2, :], pg[u % 2][:, 0:I], ACT.Silu), "silu")

            def one(b, u, later, stored):
                if later(1):
                    silu(b + 1, u + 1)
                pe.wait(eng, b, "y")
                if stored is not None:
                    eng.wait_ge(s_y[u % 2], stored)
                actY.done(eng.activation(y[:, u % 2, :], py[u % 2][:, :], ACT.Copy), "y")
                actY.wait(eng, b, "y")
                eng.dma_start(y_dram[bass.ts(b, P), :], y[:, u % 2, :]).then_inc(s_y[u % 2], 16)

            silu(0, 0)
            groups = used_groups(eng, endb)
            for u in range(GB):
                one(u, u, lambda k: True, None if u < 2 else 16)
            with eng.Fori(1, NBLK // GB) as i:
                with eng.If(i < groups):
                    for u in range(GB):
                        one(i * GB + u, u, lambda k: True, i * 32 + u // 2 * 16)
            for u in range(2):
                eng.wait_ge(s_y[u], groups * 32)
            apart(eng, s_apart)


def norm_scales(nc, ctx, name, eng, link, mv, lnp, s_var, s_root):
    link(eng.tensor_scalar_add(mv[:, :, 1], mv[:, :, 1], LN_EPS))
    eng.sem_inc(s_var, 1)
    eng.wait_ge(s_root, 1)
    link(eng.reciprocal(lnp[:, :, 0], lnp[:, :, 0]))
    link(eng.scalar_tensor_tensor(lnp[:, :, 1], mv[:, :, 0], -1.0, lnp[:, :, 0], ALU.mult, ALU.mult))


def finish(nc, a, out, y_dram, X, slot8, w8, Wg, Wu, Wdn, s_ffn, ident):
    TI = range(TPB)
    fs = range(FC)
    downs = [(i, f) for i in TI for f in fs]
    cuts = [0, 4, 8, 11, 15, 19, 22]
    with ExitStack() as ctx:
        sb = lambda name, shape, dt=F32: ctx.enter_context(nc.sbuf_tensor(name, shape, dt))
        ps = lambda name, shape, dt=F32: ctx.enter_context(nc.psum_tensor(name, shape, dt))
        sem = lambda name: ctx.enter_context(nc.semaphore(name))
        idx = [[sb(f"cidx{i}_{k}", [P, 1], U32) for k in range(K)] for i in TI]
        G = sb("G", [P, TPB, K, D])
        memT, mem = sb("memT_sb", [P, 2, DC, S]), sb("mem_sb", [P, 2, TPB, D])
        open8, neg, valid = sb("mask_b", [P, B, S], U8), sb("neg", [P, S]), sb("valid", [P, B])
        stats, mv, lnp = sb("n_stats", [P, TPB, 6]), sb("n_mv", [P, TPB, 2]), sb("n_lnp", [P, TPB, 2])
        stats4, mv4, lnp4 = sb("n_stats4", [P, TPB, 6]), sb("n_mv4", [P, TPB, 2]), sb("n_lnp4", [P, TPB, 2])
        xn, x3T, x4T = sb("xn_f", [P, TPB, D]), sb("x3T", [P, TPB, DC, P]), sb("x4T", [P, 2, DC, S])
        score, nmax, tot, inv = sb("score", [P, TPB, S]), sb("nmax", [P, TPB, 2]), sb("mtot", [P, TPB]), sb("minv", [P, TPB])
        pr, prT = sb("mp", [P, TPB, S]), sb("mpT", [P, TPB, TPB, P])
        gs, us, ds_ = sb("gate_s", [P, FC]), sb("up_s", [P, FC]), sb("down_s", [P, D])
        gl, hT, o = sb("gl", [P, 2, S]), sb("fhT", [P, FC, S]), sb("f_o", [P, TPB, D])
        eps = sb("f_eps", [P, 1])
        px, pgu, py = [[ps(f"f_{n}{i}", [P, D]) for i in range(2)] for n in ("x", "g", "y")]
        psc, ppT = ps("f_sc", [P, TPB, S]), ps("f_pT", [P, TPB, S])
        s_g, s_m, s_s, s_eps, s_apart = [sem(f"f_g{i}") for i in TI], sem("f_m"), sem("f_s"), sem("f_eps"), sem("f_apart")
        s_mem, s_o = [sem(f"f_mem{u}") for u in range(2)], [sem(f"f_o{i}") for i in TI]
        each = lambda *names: [f"{n}{i}" for n in names for i in TI]
        poolC = Steps(nc, ctx, "f_pool", each("idx"))
        peC = Steps(nc, ctx, "f_peC", each("x3T", "s", "pT", "r", "x4T"))
        peG, peY = Steps(nc, ctx, "f_peG", [f"g{f}" for f in fs]), Steps(nc, ctx, "f_peY", each("y"))
        dveC = Steps(nc, ctx, "f_dveC", [f"k{k}_{i}" for i in TI for k in range(K)] + each("st", "mv") + ["rstd", "shift", "neg"]
                     + each("x3T", "sc", "max", "nmax", "pT", "inv", "invv", "x", "st4", "mv4") + ["rstd4", "shift4"] + each("x4T"))
        dveH = Steps(nc, ctx, "f_dveH", [f"h{f}" for f in fs])
        dveY = Steps(nc, ctx, "f_dveY", [n for i in TI for n in (f"s{i}", f"o{i}")])
        actC = Steps(nc, ctx, "f_actC", ["root"] + each("n", "e") + ["root4"] + each("n4_"))
        actG = Steps(nc, ctx, "f_actG", [f"g{f}" for f in fs])
        block = ctx.enter_context(nc.Block())

        def by_batch(eng, one):
            with eng.Fori(0, B // 2 - 1) as i:
                for u in range(2):
                    one(i * 2 + u, u, True)
            one(B - 2, 0, True)
            one(B - 1, 1, False)

        @block.sync
        def _(eng):
            eng.dma_start(open8[:, :, :], a["mask"].unsqueeze(0).to_broadcast([P, B, S])).then_inc(s_m, 16)

            def load(b, u):
                eng.dma_start(memT[:, u, :, :], a["memT"][:, b, :, :]).then_inc(s_mem[u], 16)
                eng.dma_start(mem[:, u, :, :], a["mem"][:, bass.ts(b, TPB), :]).then_inc(s_mem[u], 16)

            for u in range(2):
                load(u, u)
            eng.dma_start(gs[:, :], a["gate_s"]).then_inc(s_s, 16)
            eng.dma_start(us[:, :], a["up_s"]).then_inc(s_s, 16)
            eng.dma_start(ds_[:, :], a["down_s"].unsqueeze(0).to_broadcast([P, D])).then_inc(s_s, 16)

            def one(b, u, more):
                for i in TI:
                    dveY.wait(eng, b, f"o{i}")
                    eng.dma_start(out[bass.ts(b * TPB + i, P), :], o[:, i, :]).then_inc(s_o[i], 16)

            with eng.Fori(0, B // 2 - 1) as i2:
                for u in range(2):
                    one(i2 * 2 + u, u, True)
                    peC.wait(eng, i2 * 2 + u, f"r{TPB - 1}")
                    load(i2 * 2 + u + 2, u)
            one(B - 2, 0, True)
            one(B - 1, 1, False)
            for s in s_o:
                eng.wait_ge(s, 16 * B)

        @block.gpsimd
        def _(eng):
            poolC.start(eng)

            def gather(b, first):
                for i in TI:
                    if not first:
                        dveC.wait(eng, b - 1, f"k{K - 1}_{i}")
                    for k in range(K):
                        c = eng.tensor_copy(idx[i][k][:, :], slot8[:, b * TPB + i, k:k + 1])
                    poolC.done(c, f"idx{i}")
                    poolC.wait(eng, b, f"idx{i}")
                    apart(eng, s_apart)
                    for k in range(K):
                        eng.indirect_dma_start(G[:, i, k, :], None, y_dram,
                                               bass.IndirectOffsetOnAxis(ap=idx[i][k][:, 0:1], axis=0)).then_inc(s_g[i], 16)

            gather(0, True)
            with eng.Fori(1, B) as b:
                gather(b, False)

        @block.tensor
        def _(eng):
            for x in (peC, peG, peY):
                x.start(eng)

            def turn(b, step, ready, i):
                actC.wait(eng, b, f"{ready}{i}")
                if step == "x3T":
                    dveC.wait(eng, b - 1, f"x4T{i}")
                else:
                    dveC.wait(eng, b, f"x{i}")
                for c in range(DC):
                    m = eng.transpose(px[i][:, bass.ts(c, P)], xn[:, i, bass.ts(c, P)], ident[:, :])
                peC.done(m, f"{step}{i}")

            def scores(b, u):
                for i in TI:
                    dveC.wait(eng, b, f"x3T{i}")
                    dveC.wait(eng, b - 1, f"sc{TPB - 1}")
                    for c in range(DC):
                        m = eng.matmul(psc[:, i, :], x3T[:, i, c, :], memT[:, u, c, :], start=c == 0, stop=c == DC - 1)
                    peC.done(m, f"s{i}")

            def turn_probs(b):
                for i in TI:
                    actC.wait(eng, b, f"e{i}")
                    dveC.wait(eng, b - 1, f"pT{TPB - 1}")
                    for kt in range(TPB):
                        m = eng.transpose(ppT[:, i, bass.ts(kt, P)], pr[:, i, bass.ts(kt, P)], ident[:, :])
                    peC.done(m, f"pT{i}")

            def read(b, u):
                for i in TI:
                    dveC.wait(eng, b, f"pT{i}")
                    for kt in range(TPB):
                        m = eng.matmul(px[i][:, :], prT[:, i, kt, :], mem[:, u, kt, :], start=kt == 0, stop=kt == TPB - 1)
                    peC.done(m, f"r{i}")

            def before(b, u, piece):
                if piece == 0:
                    for i in TI:
                        turn(b, "x3T", "n", i)
                elif piece == 1:
                    scores(b, u)
                elif piece == 3:
                    turn_probs(b)
                elif piece == 4:
                    read(b, u)
                elif piece == 5:
                    for i in TI:
                        turn(b, "x4T", "n4_", i)

            def arrived(u, n):
                eng.wait_ge(s_mem[u], n)

            arrived(0, 32)
            for piece in range(6):
                before(0, 0, piece)
            eng.wait_ge(s_ffn, 48)

            def one(b, u, more, mem_count):
                dveC.wait(eng, b, f"x4T{TPB - 1}")
                for f in fs:
                    if f < 2:
                        dveH.wait(eng, b - 1, f"h{FC - 2 + (f + 1) % 2}")
                    else:
                        dveH.wait(eng, b, f"h{f - 2}")
                    for n, w in enumerate((Wg, Wu)):
                        for c in range(DC):
                            m = eng.matmul(pgu[f % 2][:, bass.ts(n, S)], w[:, c, bass.ts(f, P)], x4T[:, u, c, :], start=c == 0, stop=c == DC - 1)
                    peG.done(m, f"g{f}")
                if more:
                    arrived(1 - u, mem_count)
                for piece in range(6):
                    for i, f in downs[cuts[piece]:cuts[piece + 1]]:
                        if f == 0:
                            dveY.wait(eng, b - 1, f"s{i}")
                        if i == 0:
                            dveH.wait(eng, b, f"h{f}")
                        m = eng.matmul(py[i][:, :], hT[:, f, bass.ts(i, P)], Wdn[:, f, :], start=f == 0, stop=f == FC - 1)
                        if f == FC - 1:
                            peY.done(m, f"y{i}")
                    if more:
                        before(b + 1, 1 - u, piece)

            with eng.Fori(0, B // 2 - 1) as i:
                one(i * 2, 0, True, (i + 1) * 32)
                one(i * 2 + 1, 1, True, (i + 2) * 32)
            one(B - 2, 0, True, B // 2 * 32)
            one(B - 1, 1, False, None)

        @block.vector
        def _(eng):
            for x in (dveC, dveH, dveY):
                x.start(eng)
            link = Chain(nc, ctx, "f_link", eng)
            eng.memset(eps[:, :], LN_EPS).then_inc(s_eps, 1)
            eng.wait_ge(s_m, 16)
            link(eng.tensor_reduce(valid[:, :], open8[:, :, :], axis=AX.X, op=ALU.max))

            def add_expert(b, i, k, landed):
                t = b * TPB + i
                if k == 0:
                    eng.wait_ge(s_g[i], landed)
                else:
                    dveC.wait(eng, b, f"k{k - 1}_{i}")
                dveC.done(eng.scalar_tensor_tensor(X[:, t, :], G[:, i, k, :], w8[:, t, k:k + 1], X[:, t, :], ALU.mult, ALU.add), f"k{k}_{i}")

            def moments(b, tag, last, st, m):
                for i in TI:
                    dveC.wait(eng, b, last.format(i))
                    apart(eng, s_apart)
                    dveC.done(eng.bn_stats(st[:, i, :], X[:, b * TPB + i, :]), f"st{tag}{i}")
                for i in TI:
                    dveC.wait(eng, b, f"st{tag}{i}")
                    apart(eng, s_apart)
                    dveC.done(eng.bn_aggr(m[:, i, :], st[:, i, :]), f"mv{tag}{i}")

            def scales(b, tag, m, ln):
                actC.wait(eng, b, "root" + tag)
                dveC.done(eng.reciprocal(ln[:, :, 0], ln[:, :, 0]), "rstd" + tag)
                dveC.wait(eng, b, "rstd" + tag)
                dveC.done(eng.scalar_tensor_tensor(ln[:, :, 1], m[:, :, 0], -1.0, ln[:, :, 0], ALU.mult, ALU.mult), "shift" + tag)

            def attend_open(b):
                dveC.done(eng.tensor_scalar(neg[:, :], open8[:, b, :], 1.0, 1e30, ALU.subtract, ALU.mult), "neg")
                for i in TI:
                    peC.wait(eng, b, f"x3T{i}")
                    dveC.done(eng.tensor_copy(x3T[:, i, :, :], px[i][:, :].rearrange("p (c n) -> p c n", c=DC)), f"x3T{i}")
                dveC.wait(eng, b, "neg")
                peC.wait(eng, b, f"s{TPB - 1}")
                for i in TI:
                    dveC.done(eng.scalar_tensor_tensor(score[:, i, :], psc[:, i, :], D ** -0.5, neg[:, :], ALU.mult, ALU.add), f"sc{i}")
                for i in TI:
                    dveC.wait(eng, b, f"sc{i}")
                    dveC.done(eng.tensor_reduce(nmax[:, i, 0:1], score[:, i, :], axis=AX.X, op=ALU.max), f"max{i}")
                for i in TI:
                    dveC.wait(eng, b, f"max{i}")
                    dveC.done(eng.tensor_scalar_mul(nmax[:, i, 1:2], nmax[:, i, 0:1], -1.0), f"nmax{i}")

            def attend_close(b):
                peC.wait(eng, b, f"pT{TPB - 1}")
                for i in TI:
                    dveC.done(eng.tensor_copy(prT[:, i, :, :], ppT[:, i, :].rearrange("p (c n) -> p c n", c=TPB)), f"pT{i}")
                for i in TI:
                    dveC.done(eng.reciprocal(inv[:, i:i + 1], tot[:, i:i + 1]), f"inv{i}")
                for i in TI:
                    dveC.wait(eng, b, f"inv{i}")
                    dveC.done(eng.tensor_tensor(inv[:, i:i + 1], inv[:, i:i + 1], valid[:, bass.ds(b, 1)], ALU.mult), f"invv{i}")
                for i in TI:
                    dveC.wait(eng, b, f"invv{i}")
                    peC.wait(eng, b, f"r{i}")
                    t = b * TPB + i
                    dveC.done(eng.scalar_tensor_tensor(X[:, t, :], px[i][:, :], inv[:, i:i + 1], X[:, t, :], ALU.mult, ALU.add), f"x{i}")
                moments(b, "4", "x{}", stats4, mv4)
                scales(b, "4", mv4, lnp4)

            def turned(b, u):
                for i in TI:
                    peC.wait(eng, b, f"x4T{i}")
                    dveC.done(eng.tensor_copy(x4T[:, u, :, bass.ts(i, P)], px[i][:, :].rearrange("p (c n) -> p c n", c=DC)), f"x4T{i}")

            def store(b, i, stored):
                peY.wait(eng, b, f"y{i}")
                if stored is not None:
                    eng.wait_ge(s_o[i], stored)
                dveY.done(eng.tensor_tensor(o[:, i, :], py[i][:, :], ds_[:, :], ALU.mult), f"s{i}")
                dveY.wait(eng, b, f"s{i}")
                dveY.done(eng.tensor_tensor(o[:, i, :], o[:, i, :], X[:, b * TPB + i, :], ALU.add), f"o{i}")

            for i in TI:
                for k in range(K):
                    add_expert(0, i, k, 16 * K)
            moments(0, "", "k7_{}", stats, mv)
            scales(0, "", mv, lnp)
            attend_open(0)
            attend_close(0)
            turned(0, 0)
            eng.wait_ge(s_s, 48)

            def one(b, u, more, stored, landed):
                adds = [(i, k) for i in TI for k in range(K)]
                for f in fs:
                    actG.wait(eng, b, f"g{f}")
                    dveH.done(eng.scalar_tensor_tensor(hT[:, f, :], pgu[f % 2][:, S:2 * S], us[:, f:f + 1], gl[:, f % 2, :],
                                                       ALU.mult, ALU.mult), f"h{f}")
                    if more:
                        for i, k in adds[2 * f:2 * f + 2]:
                            add_expert(b + 1, i, k, landed)
                        if f == 8:
                            moments(b + 1, "", "k7_{}", stats, mv)
                if more:
                    scales(b + 1, "", mv, lnp)
                    attend_open(b + 1)
                store(b, 0, stored)
                if more:
                    attend_close(b + 1)
                    turned(b + 1, 1 - u)
                store(b, 1, stored)

            one(0, 0, True, None, 2 * 16 * K)
            with eng.Fori(0, B // 2 - 1) as i:
                one(i * 2 + 1, 1, True, (i * 2 + 1) * 16, (i * 2 + 3) * 16 * K)
                one(i * 2 + 2, 0, True, (i * 2 + 2) * 16, (i * 2 + 4) * 16 * K)
            one(B - 1, 1, False, (B - 1) * 16, None)

        @block.scalar
        def _(eng):
            actC.start(eng)
            actG.start(eng)
            eng.wait_ge(s_eps, 1)

            def root(b, tag, m, ln):
                dveC.wait(eng, b, f"mv{tag}{TPB - 1}")
                actC.done(eng.activation(ln[:, :, 0], m[:, :, 1], ACT.Sqrt, bias=eps[:, 0:1]), "root" + tag)

            def norm(b, tag, ln, step):
                dveC.wait(eng, b, "shift" + tag)
                for i in TI:
                    if tag:
                        peC.wait(eng, b, f"x3T{i}")
                    else:
                        peC.wait(eng, b - 1, f"x4T{i}")
                    apart(eng, s_apart)
                    actC.done(eng.activation(xn[:, i, :], X[:, b * TPB + i, :], ACT.Identity, bias=ln[:, i, 1:2], scale=ln[:, i, 0:1]), f"{step}{i}")

            def exps(b):
                for i in TI:
                    dveC.wait(eng, b, f"nmax{i}")
                    peC.wait(eng, b - 1, f"pT{i}")
                    dveC.wait(eng, b - 1, f"inv{i}")
                    actC.done(eng.activation(pr[:, i, :], score[:, i, :], ACT.Exp, bias=nmax[:, i, 1:2], accum_out=tot[:, i:i + 1]), f"e{i}")

            def whole(b):
                norm(b, "", lnp, "n")
                exps(b)
                root(b, "4", mv4, lnp4)
                norm(b, "4", lnp4, "n4_")

            root(0, "", mv, lnp)
            whole(0)
            eng.wait_ge(s_s, 48)

            def one(b, u, more):
                for f in fs:
                    peG.wait(eng, b, f"g{f}")
                    if f < 2:
                        dveH.wait(eng, b - 1, f"h{FC - 2 + f}")
                    else:
                        dveH.wait(eng, b, f"h{f - 2}")
                    actG.done(eng.activation(gl[:, f % 2, :], pgu[f % 2][:, 0:S], ACT.Silu, scale=gs[:, f:f + 1]), f"g{f}")
                    if f == 9 and more:
                        root(b + 1, "", mv, lnp)
                if more:
                    whole(b + 1)

            by_batch(eng, one)


def build(nc, a, out, stop=99, dbg=None):
    h_dram = nc.dram_tensor("h_rows", (T, D), F32).ap()
    y_dram = nc.dram_tensor("y_rows", (NBLK * P, D), F32).ap()
    tab_dram = nc.dram_tensor("block_table", (NTAB, 2), I32).ap()
    with ExitStack() as ctx:
        sb = lambda name, shape, dt=F32, ctx=ctx: ctx.enter_context(nc.sbuf_tensor(name, shape, dt))
        X, ident = sb("X", [P, NT, D]), sb("ident", [P, P])
        slot8, w8 = sb("slot8", [P, NT, K], U32), sb("w8", [P, NT, K])
        blk_tok, endb, blk_tab = sb("blk_tok", [P, NTAB], U32), sb("endb", [P, E], I32), sb("blk_tab", [1, 2 * NTAB], I32)
        with ExitStack() as early:
            L, mask, m8 = sb("L", [P, NT, E], ctx=early), sb("mask", [P, NT, E], ctx=early), sb("m8", [P, NT, K], ctx=early)
            with ExitStack() as first:
                qT, kT, V = sb("qT", [P, DC, T], ctx=first), sb("kT", [P, DC, T], ctx=first), sb("V", [P, NT, D], ctx=first)
                project(nc, a["x"], a["ctxT"], a["attn_wT"], a["rows"], X, qT, kT, V, ident)
                if stop == 1:
                    return dump(nc, dbg, [qT[:, :, :], kT[:, :, :], V[:, :, :]])
                attend(nc, qT, kT, V, ident, y_dram)
                if stop == 2:
                    return dump(nc, dbg, [qT[:, :, :]])
                route(nc, a, h_dram, X, qT, L, mask, m8, ident)
                if stop == 3:
                    return dump(nc, dbg, [X[:, :, :], L[:, :, :], mask[:, :, :]])
            place(nc, a, L, mask, m8, slot8, w8, blk_tok, endb, blk_tab, tab_dram)
            if stop == 4:
                return dump4(nc, dbg, [(slot8, [P, NT, K]), (w8, None), (blk_tok, None), (blk_tab, None)])
        Wg, Wu, Wdn = sb("ffn_g", [P, DC, F]), sb("ffn_u", [P, DC, F]), sb("ffn_d", [P, FC, D])
        s_ffn = ctx.enter_context(nc.semaphore("s_ffn"))
        experts(nc, a, h_dram, y_dram, blk_tok, endb, blk_tab, ident,
                [Wg[:, :, :], Wu[:, :, :], Wdn[:, :, :]], [a["ffn_gT"], a["ffn_uT"], a["ffn_dT"]], s_ffn)
        finish(nc, a, out, y_dram, X, slot8, w8, Wg, Wu, Wdn, s_ffn, ident)


def dump4(nc, dbg, srcs):
    with nc.sbuf_tensor("d0", [P, NT, K], F32) as d0, nc.sbuf_tensor("d2", [P, NBLK], F32) as d2, nc.sbuf_tensor("d3", [1, NBLK], F32) as d3, \
            nc.semaphore("dmp") as s, nc.semaphore("dmp2") as s2, nc.Block() as block:
        @block.vector
        def _(eng):
            eng.tensor_copy(d0[:, :, :], srcs[0][0][:, :, :])
            eng.tensor_copy(d2[:, :], srcs[2][0][:, :])
            eng.tensor_copy(d3[:, :], srcs[3][0][:, :].rearrange("o (b v) -> o b v", v=2)[:, :, 0]).then_inc(s, 1)
        @block.sync
        def _(eng):
            eng.wait_ge(s, 1)
            for n, ap in enumerate([d0[:, :, :], srcs[1][0][:, :, :], d2[:, :], d3[:, :]]):
                eng.dma_start(dbg[n], ap).then_inc(s2, 16)
            eng.wait_ge(s2, 64)


def dump(nc, dbg, aps):
    with nc.semaphore("dump") as s, nc.Block() as block:
        @block.sync
        def _(eng):
            for n, ap in enumerate(aps):
                eng.dma_start(dbg[n], ap).then_inc(s, 16)
            eng.wait_ge(s, 16 * len(aps))


def lay_out(i):
    f = {k: np.ascontiguousarray(v) for k, v in i.items()}
    chunks = lambda wT: np.ascontiguousarray(wT.reshape(-1, P, wT.shape[-1]).transpose(1, 0, 2))
    tok = f["ctx_2048"].reshape(NT, P, DC, P)
    mem = f["ctx_2048"].reshape(B, S, DC, P)
    gu = np.concatenate([f["L0_ffn_w_gate"], f["L0_ffn_w_up"]], axis=2)
    return {
        "x": f["x"].reshape(T, D),
        "ctxT": np.ascontiguousarray(tok.transpose(0, 3, 2, 1)),
        "attn_wT": np.stack([chunks(f["L0_xattn_" + n + "_w"].T) for n in ("q", "k_img", "v_img", "o")]),
        "rows": np.stack([f["L0_xattn_" + n] for n in ("q_b", "norm_q_w", "k_img_b", "norm_k_img_w", "v_img_b", "o_b")]),
        "router_wT": chunks(f["L0_ffn_gate_weight"].T),
        "exp_gu": np.ascontiguousarray(gu.reshape(E, DC, P, 2 * I).transpose(0, 2, 1, 3)),
        "exp_d": np.ascontiguousarray(f["L0_ffn_w_down"].reshape(E, 2, IH, D).transpose(0, 2, 1, 3)),
        "memT": np.ascontiguousarray(mem.transpose(3, 0, 2, 1)),
        "mem": chunks(f["ctx_2048"].reshape(T, D)),
        "mask": f["mask_BxS2_bk0"],
        "ffn_gT": chunks(f["L1_ffn_gate_w"].T),
        "ffn_uT": chunks(f["L1_ffn_up_w"].T),
        "ffn_dT": chunks(f["L1_ffn_down_w"].T),
        "gate_s": np.ascontiguousarray(f["L1_ffn_gate_s"].reshape(FC, P).T),
        "up_s": np.ascontiguousarray(f["L1_ffn_up_s"].reshape(FC, P).T),
        "down_s": f["L1_ffn_down_s"],
    }


def kernel(_stop=99, _dbg=(), **inputs):
    import concourse.bacc as bacc
    from concourse.bass_utils import run_bass_kernel_spmd

    arrays = lay_out(inputs)
    nc = bacc.Bacc("TRN2", target_bir_lowering=False, num_devices=1)
    a = {n: nc.dram_tensor("in_" + n, v.shape, mybir.dt.from_np(v.dtype), kind="ExternalInput").ap() for n, v in arrays.items()}
    out = nc.dram_tensor("out", (T, D), F32, kind="ExternalOutput").ap()
    dbg = [nc.dram_tensor(f"dbg{n}", s, F32, kind="ExternalOutput").ap() for n, s in enumerate(_dbg)]
    build(nc, a, out, _stop, dbg)
    got = run_bass_kernel_spmd(nc, [{"in_" + n: v for n, v in arrays.items()}], core_ids=[0])
    return got.results[0]["out"].reshape(B, S, D)
```

```python
from contextlib import ExitStack

import numpy as np
import concourse.bass as bass
from concourse import mybir

F32 = mybir.dt.float32
F32R = mybir.dt.float32r
F16 = mybir.dt.float16
I32 = mybir.dt.int32
U32 = mybir.dt.uint32
U8 = mybir.dt.uint8
ALU = mybir.AluOpType
ACT = mybir.ActivationFunctionType
AX = mybir.AxisListType

P = 128
B, S, D = 8, 256, 512
T = B * S
NT = T // P
TPB = S // P
DC = D // P
NH, HD = 16, 32
HG = P // HD
E, K, I = 64, 8, 192
NBLK = T * K // P + E
GB = 4
NTAB = NBLK + GB
IH = I // 2
NWB = 3
F, FC = 1408, 1408 // P
LN_EPS, RMS_EPS = 1e-5, 1e-6
LOW_BITS = 0xFFF
SLOT_TOP = 65536.0


class Steps:

    def __init__(self, nc, ctx, name, names, lag=4):
        self.sem, self.names, self.lag, self.at = ctx.enter_context(nc.semaphore(name)), names, lag, 0

    def start(self, eng):
        eng.sem_inc(self.sem, self.lag * len(self.names))

    def done(self, ins, name):
        assert self.names[self.at] == name, (self.names[self.at], name)
        self.at = (self.at + 1) % len(self.names)
        ins.then_inc(self.sem, 1)

    def value(self, unit, name):
        return (unit + self.lag) * len(self.names) + self.names.index(name) + 1

    def wait(self, eng, unit, name):
        eng.wait_ge(self.sem, self.value(unit, name))


def apart(eng, sem):
    eng.sem_inc(sem, 1)


class Chain:

    def __init__(self, nc, ctx, name, eng=None):
        self.sem, self.n, self.eng = ctx.enter_context(nc.semaphore(name)), 0, eng

    def __call__(self, ins):
        self.n += 1
        ins.then_inc(self.sem, 1)
        self.eng.wait_ge(self.sem, self.n)


def project(nc, x_in, ctxT_in, wT_in, rows_in, X, qT, kT, V, ident):
    with ExitStack() as ctx:
        sb = lambda name, shape, dt=F32: ctx.enter_context(nc.sbuf_tensor(name, shape, dt))
        ps = lambda name, shape, dt=F32: ctx.enter_context(nc.psum_tensor(name, shape, dt))
        sem = lambda name: ctx.enter_context(nc.semaphore(name))
        W = sb("proj_w", [P, 3, DC, D])
        rows = sb("proj_rows", [P, 5, D])
        ctxT = sb("ctxT", [P, 2, DC, P])
        stats, mv = sb("ln1_stats", [P, NT, 6]), sb("ln1_mv", [P, NT, 2])
        lnp = sb("ln1_scale_shift", [P, NT, 2])
        rstd, shift = lnp[:, :, 0], lnp[:, :, 1]
        xn, xnT = sb("xn", [P, 2, D]), sb("xnT", [P, 2, DC, P])
        xc, lnc = sb("xc", [P, D]), sb("ln1_col", [P, 2])
        kb, qb, kn, qn, sq = sb("kb", [P, D]), sb("qb", [P, D]), sb("kn", [P, D]), sb("qn", [P, D]), sb("sq", [P, D])
        kms, qms, krs, qrs = sb("kms", [P, 2]), sb("qms", [P, 2]), sb("krs", [P, 1]), sb("qrs", [P, 1])
        pxT, pk, pq, pv, pkT, pqT = [ps(n, [P, D]) for n in ("pxT", "pk", "pq", "pv", "pkT", "pqT")]
        s_x, s_w, s_rows, s_id = [sem(f"p_x{n}") for n in range(4)], [sem(f"p_w{i}") for i in range(3)], sem("p_rows"), sem("p_id")
        s_c = [sem(f"p_c{i}") for i in range(2)]
        s_apart = sem("p_apart")
        eps, s_eps = sb("rms_eps", [P, 1]), sem("p_eps")
        s_mv, s_sd, s_ln = sem("p_mv"), sem("p_sd"), sem("p_ln")
        pe = Steps(nc, ctx, "p_pe", ["xT", "k", "q", "v", "kT", "qT"])
        dve = Steps(nc, ctx, "p_dve", ["xT", "kb", "qb", "kr", "kn", "qr", "qn", "vb"])
        act = Steps(nc, ctx, "p_act", ["ksq", "ksd", "qsq", "qsd", "kT", "qT"])
        pool = Steps(nc, ctx, "p_pool", ["xc", "lnc", "xn"])
        block = ctx.enter_context(nc.Block())

        @block.sync
        def _(eng):
            for n in range(4):
                eng.dma_start(X[:, 4 * n:4 * n + 4, :],
                              x_in.rearrange("(n t p) d -> n p t d", p=P, t=4)[n]).then_inc(s_x[n], 16)
            eng.dma_start(W[:, 1, :, :], wT_in[1]).then_inc(s_w[1], 16)
            with eng.Fori(0, NT // 2) as i:
                for par in range(2):
                    t = i * 2 + par
                    pe.wait(eng, t - 2, "v")
                    eng.dma_start(ctxT[:, par, :, :], ctxT_in[t, :, :, :]).then_inc(s_c[par], 16)

        @block.scalar
        def _(eng):
            act.start(eng)
            eng.dma_start(W[:, 0, :, :], wT_in[0]).then_inc(s_w[0], 16)
            eng.dma_start(rows[:, :, :], rows_in[0:5, :].unsqueeze(0).to_broadcast([P, 5, D])).then_inc(s_rows, 16)
            eng.dma_start(W[:, 2, :, :], wT_in[2]).then_inc(s_w[2], 16)
            eng.wait_ge(s_mv, 1)
            eng.activation(rstd, mv[:, :, 1], ACT.Sqrt).then_inc(s_sd, 1)
            eng.wait_ge(s_eps, 1)
            with eng.Fori(0, NT) as t:
                for x, psum, sbuf in (("k", kb, kms), ("q", qb, qms)):
                    dve.wait(eng, t, x + "b")
                    if x == "k":
                        dve.wait(eng, t - 1, "kr")
                        dve.wait(eng, t - 1, "qr")
                    act.done(eng.activation(sq[:, :], psum[:, :], ACT.Square, accum_out=sbuf[:, 0:1]), x + "sq")
                    act.wait(eng, t, x + "sq")
                    act.done(eng.activation(sbuf[:, 1:2], sbuf[:, 0:1], ACT.Sqrt, bias=eps[:, 0:1], scale=1.0 / D), x + "sd")
                for x, psum, dst in (("k", pkT, kT), ("q", pqT, qT)):
                    pe.wait(eng, t, x + "T")
                    act.done(eng.activation(dst[:, :, bass.ts(t, P)], psum[:, :].rearrange("p (c n) -> p c n", c=DC),
                                            ACT.Copy), x + "T")

        @block.gpsimd
        def _(eng):
            pool.start(eng)
            eng.memset(ident[:, :], 0.0).then_inc(s_id, 1)
            eng.wait_ge(s_id, 1)
            eng.affine_select(out=ident[:, :], in_=ident[:, :], compare_op=ALU.not_equal, fill=1.0, base=0,
                              pattern=[[-1, P]], channel_multiplier=1).then_inc(s_id, 1)
            eng.wait_ge(s_ln, 1)
            with eng.Fori(0, NT // 2) as i:
                for par in range(2):
                    t = i * 2 + par
                    pool.wait(eng, t - 1, "xn")
                    pool.done(eng.tensor_copy(xc[:, :], X[:, t, :]), "xc")
                    pool.done(eng.tensor_copy(lnc[:, :], lnp[:, t, :]), "lnc")
                    pool.wait(eng, t, "lnc")
                    pe.wait(eng, t - 2, "xT")
                    apart(eng, s_apart)
                    pool.done(eng.tensor_scalar(xn[:, par, :], xc[:, :], lnc[:, 0:1], lnc[:, 1:2], ALU.mult, ALU.add), "xn")

        @block.tensor
        def _(eng):
            pe.start(eng)
            eng.wait_ge(s_id, 2)
            for s in s_w:
                eng.wait_ge(s, 16)
            with eng.Fori(0, NT // 2) as i:
                for par in range(2):
                    t = i * 2 + par
                    pool.wait(eng, t, "xn")
                    dve.wait(eng, t - 1, "xT")
                    for c in range(DC):
                        m = eng.transpose(pxT[:, bass.ts(c, P)], xn[:, par, bass.ts(c, P)], ident[:, :])
                    pe.done(m, "xT")
                    eng.wait_ge(s_c[par], 16 * (i + 1))
                    for x, psum, lhs, w, free in (("k", pk, ctxT, 1, "kb"), ("q", pq, xnT, 0, "qb"), ("v", pv, ctxT, 2, "vb")):
                        if x == "q":
                            dve.wait(eng, t, "xT")
                        dve.wait(eng, t - 1, free)
                        for c in range(DC):
                            m = eng.matmul(psum[:, :], lhs[:, par, c, :], W[:, w, c, :], start=c == 0, stop=c == DC - 1)
                        pe.done(m, x)
                    for x, psum, src in (("k", pkT, kn), ("q", pqT, qn)):
                        dve.wait(eng, t, x + "n")
                        act.wait(eng, t - 1, x + "T")
                        for c in range(DC):
                            m = eng.transpose(psum[:, bass.ts(c, P)], src[:, bass.ts(c, P)], ident[:, :])
                        pe.done(m, x + "T")

        @block.vector
        def _(eng):
            dve.start(eng)
            link = Chain(nc, ctx, "p_link", eng)
            for t in range(NT):
                if t % 4 == 0:
                    eng.wait_ge(s_x[t // 4], 16)
                    apart(eng, s_apart)
                last = eng.bn_stats(stats[:, t, :], X[:, t, :])
            link(last)
            for t in range(NT):
                last = eng.bn_aggr(mv[:, t, :], stats[:, t, :])
            link(last)
            link(eng.tensor_scalar_add(mv[:, :, 1], mv[:, :, 1], LN_EPS))
            eng.sem_inc(s_mv, 1)
            eng.wait_ge(s_sd, 1)
            link(eng.reciprocal(rstd, rstd))
            eng.scalar_tensor_tensor(shift, mv[:, :, 0], -1.0, rstd, ALU.mult, ALU.mult).then_inc(s_ln, 1)
            eng.wait_ge(s_rows, 16)
            link(eng.tensor_scalar_mul(rows[:, 3, :], rows[:, 3, :], -HD ** -0.5))
            link(eng.memset(eps[:, :], RMS_EPS))
            eng.sem_inc(s_eps, 1)
            with eng.Fori(0, NT // 2) as i:
                for par in range(2):
                    t = i * 2 + par
                    pe.wait(eng, t, "xT")
                    pe.wait(eng, t - 2, "q")
                    dve.done(eng.tensor_copy(xnT[:, par, :, :], pxT[:, :].rearrange("p (c n) -> p c n", c=DC)), "xT")
                    for x, psum, dst, bias in (("k", pk, kb, 2), ("q", pq, qb, 0)):
                        pe.wait(eng, t, x)
                        act.wait(eng, t - 1, x + "sq")
                        dve.done(eng.tensor_tensor(dst[:, :], psum[:, :], rows[:, bias, :], ALU.add), x + "b")
                    for x, src, root, inv, dst, w in (("k", kb, kms, krs, kn, 3), ("q", qb, qms, qrs, qn, 1)):
                        act.wait(eng, t, x + "sd")
                        dve.done(eng.reciprocal(inv[:, :], root[:, 1:2]), x + "r")
                        dve.wait(eng, t, x + "r")
                        pe.wait(eng, t - 1, x + "T")
                        dve.done(eng.scalar_tensor_tensor(dst[:, :], src[:, :], inv[:, 0:1], rows[:, w, :],
                                                          ALU.mult, ALU.mult), x + "n")
                    pe.wait(eng, t, "v")
                    dve.done(eng.tensor_tensor(V[:, t, :], pv[:, :], rows[:, 4, :], ALU.add), "vb")


def attend(nc, qT, kT, V, ident, y_dram):
    GH = range(HG)
    with ExitStack() as ctx:
        sb = lambda name, shape, dt=F32: ctx.enter_context(nc.sbuf_tensor(name, shape, dt))
        ps = lambda name, shape, dt=F32: ctx.enter_context(nc.psum_tensor(name, shape, dt))
        qg, kg, vg = sb("qg", [P, 2, S]), sb("kg", [P, 2, S]), sb("vg", [P, 2, TPB, P])
        low, tot, inv = sb("low", [P, 2, HG, TPB]), sb("tot", [P, 2, HG, TPB]), sb("inv", [P, 2, HG, TPB])
        prob = sb("prob", [P, 2, HG, TPB, S])
        probT = sb("probT", [P, 2, HG, TPB, S])
        pS = [ps(f"pS{j}", [P, TPB, S]) for j in GH]
        pT = [ps(f"pT{j}", [P, TPB, S]) for j in range(2)]
        pO = [ps(f"pO{j}", [P, S]) for j in range(2)]
        peS = Steps(nc, ctx, "a_peS", [f"S{j}" for j in GH])
        peT = Steps(nc, ctx, "a_peT", [f"T{j}" for j in GH] + ["O"])
        dveM = Steps(nc, ctx, "a_dveM", [f"M{j}" for j in GH])
        dveR = Steps(nc, ctx, "a_dveR", [f"R{j}" for j in GH])
        dveT = Steps(nc, ctx, "a_dveT", [f"T{j}" for j in GH])
        actE = Steps(nc, ctx, "a_actE", [f"E{j}" for j in GH])
        actO = Steps(nc, ctx, "a_actO", ["O"])
        poolC = Steps(nc, ctx, "a_poolC", ["q", "k", "v"])
        poolN = Steps(nc, ctx, "a_poolN", [f"N{j}" for j in GH])
        zero, s_zero, s_rest = sb("zero", [P, D]), ctx.enter_context(nc.semaphore("a_zero")), ctx.enter_context(nc.semaphore("a_rest"))
        block = ctx.enter_context(nc.Block())

        @block.sync
        def _(eng):
            rest = y_dram.rearrange("(n p) d -> n p d", p=P)[T * K // P:NBLK]
            eng.wait_ge(s_zero, 1)
            for n in range(NBLK - T * K // P):
                eng.dma_start(rest[n], zero[:, :]).then_inc(s_rest, 16)
            eng.wait_ge(s_rest, 16 * (NBLK - T * K // P))

        def units(eng, one):
            with eng.Fori(0, B - 1) as b:
                for g in range(DC):
                    one(b, g, lambda n: True)
            for g in range(DC):
                one(B - 1, g, lambda n, g=g: g + n < DC)

        def scores(eng, u, par):
            poolC.wait(eng, u, "k")
            for j in GH:
                actE.wait(eng, u - 1, f"E{j}")
                for h in range(TPB):
                    m = eng.matmul(pS[j][:, h, :], qg[bass.ts(j, HD), par, bass.ts(h, P)],
                                   kg[bass.ts(j, HD), par, :], start=True, stop=True)
                peS.done(m, f"S{j}")

        @block.tensor
        def _(eng):
            peS.start(eng)
            peT.start(eng)
            scores(eng, 0, 0)

            def one(b, g, later):
                u, par = b * DC + g, g % 2
                if later(1):
                    scores(eng, u + 1, 1 - par)
                for j in GH:
                    poolN.wait(eng, u, f"N{j}")
                    if j < 2:
                        dveT.wait(eng, u - 1, f"T{j + 2}")
                    else:
                        dveT.wait(eng, u, f"T{j - 2}")
                    for kt in range(TPB):
                        for h in range(TPB):
                            m = eng.transpose(pT[j % 2][:, kt, bass.ts(h, P)], prob[:, par, j, h, bass.ts(kt, P)], ident[:, :])
                    peT.done(m, f"T{j}")
                poolC.wait(eng, u, "v")
                actO.wait(eng, u - 2, "O")
                for j in GH:
                    dveT.wait(eng, u, f"T{j}")
                    for kt in range(TPB):
                        m = eng.matmul(pO[par][bass.ts(j, HD), :], vg[:, par, kt, bass.ts(j, HD)],
                                       probT[:, par, j, kt, :], start=kt == 0, stop=kt == TPB - 1)
                peT.done(m, "O")

            units(eng, one)

        @block.vector
        def _(eng):
            dveM.start(eng)
            dveR.start(eng)
            dveT.start(eng)

            def lows(u, par, j):
                peS.wait(eng, u, f"S{j}")
                actE.wait(eng, u - 2, f"E{j}")
                dveM.done(eng.tensor_reduce(low[:, par, j, :], pS[j][:, :, :], axis=AX.X, op=ALU.min), f"M{j}")

            for j in GH:
                lows(0, 0, j)

            def one(b, g, later):
                u, par = b * DC + g, g % 2
                for j in GH:
                    actE.wait(eng, u, f"E{j}")
                    poolN.wait(eng, u - 2, f"N{j}")
                    dveR.done(eng.reciprocal(inv[:, par, j, :], tot[:, par, j, :]), f"R{j}")
                    if later(1):
                        lows(u + 1, 1 - par, j)
                for j in GH:
                    peT.wait(eng, u, f"T{j}")
                    peT.wait(eng, u - 2, "O")
                    dveT.done(eng.tensor_copy(probT[:, par, j, :, :], pT[j % 2][:, :, :]), f"T{j}")

            units(eng, one)

        @block.scalar
        def _(eng):
            actE.start(eng)
            actO.start(eng)

            def exps(u, par):
                for j in GH:
                    dveM.wait(eng, u, f"M{j}")
                    peT.wait(eng, u - 2, f"T{j}")
                    dveR.wait(eng, u - 2, f"R{j}")
                    for h in range(TPB):
                        a = eng.activation(prob[:, par, j, h, :], pS[j][:, h, :], ACT.Exp, bias=low[:, par, j, h:h + 1],
                                           scale=-1.0, accum_out=tot[:, par, j, h:h + 1])
                    actE.done(a, f"E{j}")

            exps(0, 0)

            def one(b, g, later):
                u, par = b * DC + g, g % 2
                if later(1):
                    exps(u + 1, 1 - par)
                peT.wait(eng, u, "O")
                actO.done(eng.activation(qT[:, g, bass.ts(b, S)], pO[par][:, :], ACT.Copy), "O")

            units(eng, one)

        @block.gpsimd
        def _(eng):
            poolC.start(eng)
            poolN.start(eng)
            eng.memset(zero[:, :], 0.0).then_inc(s_zero, 1)

            def copies(b, g):
                u, par = b * DC + g, g % 2
                peS.wait(eng, u - 2, f"S{HG - 1}")
                poolC.done(eng.tensor_copy(qg[:, par, :], qT[:, g, bass.ts(b, S)]), "q")
                poolC.done(eng.tensor_copy(kg[:, par, :], kT[:, g, bass.ts(b, S)]), "k")
                peT.wait(eng, u - 2, "O")
                poolC.done(eng.tensor_copy(vg[:, par, :, :], V[:, bass.ts(b, TPB), bass.ts(g, P)]), "v")

            copies(0, 0)
            copies(0, 1)

            def one(b, g, later):
                u, par = b * DC + g, g % 2
                for j in GH:
                    dveR.wait(eng, u, f"R{j}")
                    w = prob[:, par, j, :, :]
                    poolN.done(eng.tensor_tensor(w, w, inv[:, par, j, :].unsqueeze(2).to_broadcast([P, TPB, S]), ALU.mult), f"N{j}")
                if later(2):
                    copies(b + (g + 2) // DC, (g + 2) % DC)

            units(eng, one)


def by_unit(eng, one, n, unroll, peel):
    assert (n - peel) % unroll == 0 and peel % unroll == 0
    with eng.Fori(0, (n - peel) // unroll) as i:
        for u in range(unroll):
            one(i * unroll + u, u, lambda k: True)
    for t in range(n - peel, n):
        one(t, t % unroll, lambda k, t=t: t + k < n)


def route(nc, a, h_dram, X, qT, L, mask, m8, ident):
    with ExitStack() as ctx:
        sb = lambda name, shape, dt=F32: ctx.enter_context(nc.sbuf_tensor(name, shape, dt))
        ps = lambda name, shape, dt=F32: ctx.enter_context(nc.psum_tensor(name, shape, dt))
        sem = lambda name: ctx.enter_context(nc.semaphore(name))
        Wo, ob, Wr = sb("wo", [P, DC, D]), sb("ob", [P, D]), sb("router_w", [P, DC, E])
        oT, add, h, hT = sb("oT", [P, 2, DC, P]), sb("add", [P, D]), sb("h", [P, 2, D]), sb("hT", [P, 2, DC, P])
        stats, mv, lnp = sb("ln2_stats", [P, NT, 6]), sb("ln2_mv", [P, NT, 2]), sb("ln2_scale_shift", [P, NT, 2])
        logit, rest, top = sb("logit", [P, E]), sb("rest", [P, E]), sb("top", [P, K])
        po, ph, pl = [ps(f"po{i}", [P, D]) for i in range(2)], [ps(f"ph{i}", [P, D]) for i in range(2)], [ps(f"pl{i}", [P, E]) for i in range(2)]
        s_w, s_ob, s_r, s_h = sem("r_w"), sem("r_ob"), sem("r_r"), [sem(f"r_h{i}") for i in range(2)]
        s_apart, s_var, s_root, s_ln = sem("r_apart"), sem("r_var"), sem("r_root"), sem("r_ln")
        pool = Steps(nc, ctx, "r_pool", ["oT"])
        peO, peH, peL = Steps(nc, ctx, "r_peO", ["o"]), Steps(nc, ctx, "r_peH", ["hT"]), Steps(nc, ctx, "r_peL", ["l"])
        dveA = Steps(nc, ctx, "r_dveA", ["add", "x", "stats"])
        dveH = Steps(nc, ctx, "r_dveH", ["hT"])
        dveB = Steps(nc, ctx, "r_dveB", ["l", "top", "rest", "mask", "L", "m8"])
        act = Steps(nc, ctx, "r_act", ["h"])
        block = ctx.enter_context(nc.Block())

        @block.sync
        def _(eng):
            eng.dma_start(Wo[:, :, :], a["attn_wT"][3]).then_inc(s_w, 16)
            eng.dma_start(ob[:, :], a["rows"][5:6, :].to_broadcast([P, D])).then_inc(s_ob, 16)
            eng.dma_start(Wr[:, :, :], a["router_wT"]).then_inc(s_r, 16)

            def one(t, u, later):
                act.wait(eng, t, "h")
                eng.dma_start(h_dram[bass.ts(t, P), :], h[:, u, :]).then_inc(s_h[u], 16)

            by_unit(eng, one, NT, 2, 0)
            for s in s_h:
                eng.wait_ge(s, 16 * NT // 2)

        @block.gpsimd
        def _(eng):
            pool.start(eng)

            def one(t, u, later):
                peO.wait(eng, t - 2, "o")
                pool.done(eng.tensor_copy(oT[:, u, :, :], qT[:, :, bass.ts(t, P)]), "oT")

            by_unit(eng, one, NT, 2, 0)

        @block.tensor
        def _(eng):
            for x in (peO, peH, peL):
                x.start(eng)
            eng.wait_ge(s_w, 16)

            def project_out(t, u, later):
                pool.wait(eng, t, "oT")
                dveA.wait(eng, t - 2, "add")
                for c in range(DC):
                    m = eng.matmul(po[u][:, :], oT[:, u, c, :], Wo[:, c, :], start=c == 0, stop=c == DC - 1)
                peO.done(m, "o")

            by_unit(eng, project_out, NT, 2, 0)

            def turn(t, u):
                act.wait(eng, t, "h")
                dveH.wait(eng, t - 2, "hT")
                for c in range(DC):
                    m = eng.transpose(ph[u][:, bass.ts(c, P)], h[:, u, bass.ts(c, P)], ident[:, :])
                peH.done(m, "hT")

            turn(0, 0)
            eng.wait_ge(s_r, 16)

            def one(t, u, later):
                if later(1):
                    turn(t + 1, 1 - u)
                dveH.wait(eng, t, "hT")
                dveB.wait(eng, t - 2, "l")
                for c in range(DC):
                    m = eng.matmul(pl[u][:, :], hT[:, u, c, :], Wr[:, c, :], start=c == 0, stop=c == DC - 1)
                peL.done(m, "l")

            by_unit(eng, one, NT, 2, 2)

        @block.scalar
        def _(eng):
            act.start(eng)
            eng.wait_ge(s_var, 1)
            eng.activation(lnp[:, :, 0], mv[:, :, 1], ACT.Sqrt).then_inc(s_root, 1)
            eng.wait_ge(s_ln, 1)

            def norm(t, u):
                peH.wait(eng, t - 2, "hT")
                act.done(eng.activation(h[:, u, :], X[:, t, :], ACT.Identity, bias=lnp[:, t, 1:2], scale=lnp[:, t, 0:1]), "h")

            for u in range(2):
                norm(u, u)
            with eng.Fori(1, NT // 2) as i:
                for u in range(2):
                    eng.wait_ge(s_h[u], i * 16)
                    norm(i * 2 + u, u)

        @block.vector
        def _(eng):
            for x in (dveA, dveH, dveB):
                x.start(eng)
            link = Chain(nc, ctx, "r_link", eng)
            eng.wait_ge(s_ob, 16)

            def residual(t, u, later):
                peO.wait(eng, t, "o")
                dveA.done(eng.tensor_tensor(add[:, :], po[u][:, :], ob[:, :], ALU.add), "add")
                dveA.wait(eng, t, "add")
                dveA.done(eng.tensor_tensor(X[:, t, :], X[:, t, :], add[:, :], ALU.add), "x")
                dveA.wait(eng, t, "x")
                apart(eng, s_apart)
                dveA.done(eng.bn_stats(stats[:, t, :], X[:, t, :]), "stats")

            by_unit(eng, residual, NT, 2, 0)
            dveA.wait(eng, NT - 1, "stats")
            for t in range(NT):
                last = eng.bn_aggr(mv[:, t, :], stats[:, t, :])
            link(last)
            norm_scales(nc, ctx, "r", eng, link, mv, lnp, s_var, s_root)
            eng.sem_inc(s_ln, 1)

            def turned(t, u):
                peH.wait(eng, t, "hT")
                peL.wait(eng, t - 2, "l")
                dveH.done(eng.tensor_copy(hT[:, u, :, :], ph[u][:, :].rearrange("p (c n) -> p c n", c=DC)), "hT")

            turned(0, 0)

            def one(t, u, later):
                if later(1):
                    turned(t + 1, 1 - u)
                peL.wait(eng, t, "l")
                dveB.wait(eng, t - 1, "m8")
                dveB.done(eng.tensor_copy(logit[:, :], pl[u][:, :]), "l")
                dveB.wait(eng, t, "l")
                apart(eng, s_apart)
                dveB.done(eng.max(top[:, :], logit[:, :]), "top")
                dveB.wait(eng, t, "top")
                apart(eng, s_apart)
                dveB.done(eng.match_replace(rest[:, :], top[:, :], logit[:, :], -3e38), "rest")
                dveB.wait(eng, t, "rest")
                dveB.done(eng.tensor_tensor(mask[:, t, :], logit[:, :], rest[:, :], ALU.not_equal), "mask")
                dveB.done(eng.tensor_copy(L[:, t, :], logit[:, :]), "L")
                dveB.done(eng.tensor_copy(m8[:, t, :], top[:, :]), "m8")

            by_unit(eng, one, NT, 2, 2)


def place(nc, a, W, Wgu, s_ffn, L, mask, m8, slot8, w8, blk_tok, endb, blk_tab, tab_dram):
    with ExitStack() as ctx:
        sb = lambda name, shape, dt=F32: ctx.enter_context(nc.sbuf_tensor(name, shape, dt))
        ps = lambda name, shape, dt=F32: ctx.enter_context(nc.psum_tensor(name, shape, dt))
        sem = lambda name: ctx.enter_context(nc.semaphore(name))
        mask16, before, ones16 = sb("mask16", [P, NT * E], F16), sb("before", [P, P], F16), sb("ones16", [P, P], F16)
        total, inv = sb("total", [P, NT]), sb("winv", [P, NT])
        pre = sb("pre", [P, NT + 1, E])
        cnt_i, nblk, one_e, first, end = sb("cnt_i", [P, E], I32), sb("nblk", [P, E]), sb("one_e", [P, E]), sb("first", [P, E]), sb("end", [P, E])
        key, key8, hit = sb("key", [P, NT, E]), sb("key8", [P, NT, K]), sb("hit", [P, NT, E])
        slot_f, slot_i = sb("slot_f", [P, NT, K]), sb("slot_i", [P, NT, K], I32)
        row_i, blk_i, row_f, blk_f = sb("row_i", [P, NT, K], I32), sb("blk_i", [P, NT, K], I32), sb("row_f", [P, NT, K]), sb("blk_f", [P, NT, K])
        it_i, it_row, it_blk = sb("it_i", [P, NTAB], I32), sb("it_row", [P, P], F16), sb("it_blk", [P, NTAB], F16)
        tok_i, tok = sb("tok_i", [P, NT], I32), sb("tok", [P, NT])
        hotr, hotb = sb("hotr", [P, K, P], F16), sb("hotb", [P, K, NTAB], F16)
        b_i, b_f, be, tab = sb("b_i", [P, 2], I32), sb("b_f", [P, 2, 2]), sb("be", [P, 2, 2]), sb("tab", [P, 2, 2], I32)
        new = sb("new", [P, 2])
        le = sb("le", [P, E])
        prank, pcnt = [ps(f"prank{i}", [P, 512]) for i in range(2)], [ps(f"pcnt{i}", [P, 512]) for i in range(2)]
        plist = ps("plist", [P, NTAB])
        s_exp, s_iota, s_rank, s_m16, s_tab, s_tab2, s_ls = sem("l_exp"), sem("l_iota"), sem("l_rank"), sem("l_m16"), sem("l_tab"), sem("l_tab2"), sem("l_ls")
        s_lsub, s_apart = sem("l_lsub"), sem("l_apart")
        dveP = Steps(nc, ctx, "l_dveP", ["pre"])
        dveH = Steps(nc, ctx, "l_dveH", [f"h{k}" for k in range(K)])
        peL = Steps(nc, ctx, "l_peL", [f"l{k}" for k in range(K)])
        dual = lambda t, banks: banks[t // 8][:, bass.ts(t % 8, E)]
        block = ctx.enter_context(nc.Block())

        @block.gpsimd
        def _(eng):
            link = Chain(nc, ctx, "l_poolc", eng)
            link(eng.iota(it_i[:, :], pattern=[[1, NTAB]], base=0, channel_multiplier=0))
            link(eng.tensor_copy(it_row[:, :], it_i[:, 0:P]))
            link(eng.tensor_copy(it_blk[:, :], it_i[:, :]))
            link(eng.iota(tok_i[:, :], pattern=[[P, NT]], base=0, channel_multiplier=1))
            link(eng.tensor_copy(tok[:, :], tok_i[:, :]))
            link(eng.iota(b_i[:, :], pattern=[[P, 2]], base=-1, channel_multiplier=1))
            link(eng.tensor_copy(b_f[:, :, 0], b_i[:, :]))
            link(eng.tensor_scalar_add(b_f[:, :, 1], b_f[:, :, 0], -1.0))
            link(eng.memset(ones16[:, :], 1.0))
            link(eng.affine_select(out=before[:, :], in_=ones16[:, :], compare_op=ALU.is_gt, fill=0.0, base=0,
                                   pattern=[[1, P]], channel_multiplier=-1))
            eng.sem_inc(s_iota, 1)
            for n in range(NWB):
                W.low_v(eng, n, n)
                W.low_p(eng, n, n)

        @block.tensor
        def _(eng):
            peL.start(eng)
            eng.wait_ge(s_iota, 1)
            eng.wait_ge(s_m16, 1)
            for i in range(2):
                eng.matmul(prank[i][:, :], before[:, :], mask16[:, bass.ts(i, 512)], start=True, stop=True)
                m = eng.matmul(pcnt[i][:, :], ones16[:, :], mask16[:, bass.ts(i, 512)], start=True, stop=True)
            m.then_inc(s_rank, 1)

            def one(t, start, stop):
                for k in range(K):
                    dveH.wait(eng, t, f"h{k}")
                    peL.done(eng.matmul(plist[:, :], hotr[:, k, :], hotb[:, k, :], start=start and k == 0,
                                        stop=stop and k == K - 1), f"l{k}")

            one(0, True, False)
            with eng.Fori(1, NT - 1) as t:
                one(t, False, False)
            one(NT - 1, False, True)

        @block.scalar
        def _(eng):
            eng.wait_ge(s_lsub, 1)
            eng.activation(L[:, :, :], L[:, :, :], ACT.Exp).then_inc(s_exp, 1)
            for n in range(NWB):
                W.high_gu(eng, n, n)
                W.high_d(eng, n, n)

        @block.sync
        def _(eng):
            for n in range(NWB):
                W.load(eng, n, n, W.s_landing[n])
            for n, src in enumerate(("ffn_gT", "ffn_uT")):
                eng.dma_start(Wgu[:, n, :, :], a[src]).then_inc(s_ffn, 16)
            for n in range(NWB):
                W.landed(eng, W.s_landing[n], 1)
            for n in range(NWB, NWB + 2):
                W.raw_free(eng, n - NWB, s_apart)
                W.load(eng, n, n - NWB, W.s_landing[NWB])
                if n == NWB:
                    W.landed(eng, W.s_landing[NWB], 1)
            eng.wait_ge(s_tab, 1)
            eng.dma_start(tab_dram[0:P, :], tab[:, 0, :]).then_inc(s_tab2, 16)
            eng.dma_start(tab_dram[P:NTAB, :], tab[0:NTAB - P, 1, :]).then_inc(s_tab2, 16)
            eng.wait_ge(s_tab2, 32)
            eng.dma_start(blk_tab[0:1, :], tab_dram.rearrange("(o b) v -> o (b v)", o=1)).then_inc(s_tab2, 16)
            eng.wait_ge(s_tab2, 48)

        @block.vector
        def _(eng):
            dveP.start(eng)
            dveH.start(eng)
            link = Chain(nc, ctx, "l_dvec", eng)
            link(eng.tensor_copy(mask16[:, :], mask[:, :, :].rearrange("p t e -> p (t e)")))
            eng.sem_inc(s_m16, 1)
            link(eng.tensor_tensor(L[:, :, :], L[:, :, :], m8[:, :, 0:1].to_broadcast([P, NT, E]), ALU.subtract))
            eng.sem_inc(s_lsub, 1)
            link(eng.memset(pre[:, 0, :], 0.0))
            link(eng.memset(one_e[:, :], 1.0))
            eng.wait_ge(s_rank, 1)
            dveP.wait(eng, -1, "pre")
            for t in range(NT):
                link(eng.tensor_tensor(pre[:, t + 1, :], pre[:, t, :], dual(t, pcnt), ALU.add))
            link(eng.tensor_scalar_add(cnt_i[:, :], pre[:, NT, :], float(P - 1)))
            link(eng.tensor_scalar(cnt_i[:, :], cnt_i[:, :], P.bit_length() - 1, None, ALU.arith_shift_right))
            link(eng.tensor_copy(nblk[:, :], cnt_i[:, :]))
            link(eng.tensor_scalar_max(nblk[:, :], nblk[:, :], 1.0))
            link(eng.tensor_tensor_scan(end[:, :], one_e[:, :], nblk[:, :], 0.0, ALU.mult, ALU.add))
            link(eng.tensor_copy(endb[:, :], end[:, :]))
            link(eng.tensor_tensor(first[:, :], end[:, :], nblk[:, :], ALU.subtract))
            link(eng.tensor_scalar_mul(first[:, :], first[:, :], float(P)))
            eng.wait_ge(s_iota, 1)
            for i in range(2):
                for prev in range(2):
                    link(eng.tensor_scalar(le[:, :], end[:, :], b_f[:, i, prev:prev + 1], None, ALU.is_le))
                    link(eng.reduce_sum(be[:, i, prev:prev + 1], le[:, :], axis=AX.X))
            link(eng.tensor_scalar_min(be[:, :, :], be[:, :, :], float(E - 1)))
            link(eng.tensor_copy(tab[:, :, 0], be[:, :, 0]))
            link(eng.tensor_tensor(new[:, :], be[:, :, 0], be[:, :, 1], ALU.subtract))
            link(eng.tensor_tensor(new[:, :], new[:, :], be[:, :, 0], ALU.mult))
            link(eng.tensor_scalar(be[:, :, 0], be[:, :, 0], float(E - NWB), None, ALU.is_le))
            link(eng.tensor_tensor(tab[:, :, 1], new[:, :], be[:, :, 0], ALU.mult))
            eng.sem_inc(s_tab, 1)
            for i in range(2):
                half = slice(i * 8, i * 8 + 8)
                link(eng.tensor_tensor(key[:, half, :], prank[i][:, :].rearrange("p (t e) -> p t e", e=E), pre[:, half, :], ALU.add))
            link(eng.tensor_tensor(key[:, :, :], key[:, :, :], first[:, :].unsqueeze(1).to_broadcast([P, NT, E]), ALU.add))
            link(eng.tensor_scalar(key[:, :, :], key[:, :, :], -1.0, SLOT_TOP, ALU.mult, ALU.add))
            link(eng.tensor_tensor(key[:, :, :], key[:, :, :], mask[:, :, :], ALU.mult))
            for t in range(NT):
                last = eng.max(key8[:, t, :], key[:, t, :])
            link(last)
            link(eng.tensor_scalar(slot_f[:, :, :], key8[:, :, :], -1.0, SLOT_TOP, ALU.mult, ALU.add))
            link(eng.tensor_copy(slot8[:, :, :], slot_f[:, :, :]))
            link(eng.tensor_copy(slot_i[:, :, :], slot_f[:, :, :]))
            link(eng.tensor_scalar(row_i[:, :, :], slot_i[:, :, :], P - 1, None, ALU.bitwise_and))
            link(eng.tensor_scalar(blk_i[:, :, :], slot_i[:, :, :], P.bit_length() - 1, None, ALU.arith_shift_right))
            link(eng.tensor_copy(row_f[:, :, :], row_i[:, :, :]))
            link(eng.tensor_copy(blk_f[:, :, :], blk_i[:, :, :]))
            with eng.Fori(0, NT) as t:
                for k in range(K):
                    peL.wait(eng, t - 1, f"l{k}")
                    eng.tensor_scalar(hotr[:, k, :], it_row[:, :], row_f[:, t, k:k + 1], None, ALU.is_equal)
                    dveH.done(eng.tensor_scalar(hotb[:, k, :], it_blk[:, :], blk_f[:, t, k:k + 1], tok[:, bass.ds(t, 1)],
                                                ALU.is_equal, ALU.mult), f"h{k}")
            peL.wait(eng, NT - 1, f"l{K - 1}")
            link(eng.tensor_copy(blk_tok[:, :], plist[:, :]))
            eng.wait_ge(s_exp, 1)
            link(eng.tensor_tensor(L[:, :, :], L[:, :, :], mask[:, :, :], ALU.mult))
            link(eng.reduce_sum(total[:, :], L[:, :, :], axis=AX.X))
            link(eng.reciprocal(inv[:, :], total[:, :]))
            link(eng.tensor_tensor(L[:, :, :], L[:, :, :], inv[:, :].unsqueeze(2).to_broadcast([P, NT, E]), ALU.mult))
            for k in range(K):
                link(eng.tensor_tensor(hit[:, :, :], key[:, :, :], key8[:, :, k:k + 1].to_broadcast([P, NT, E]), ALU.is_equal))
                link(eng.tensor_tensor(hit[:, :, :], hit[:, :, :], L[:, :, :], ALU.mult))
                link(eng.reduce_sum(w8[:, :, k], hit[:, :, :], axis=AX.X))


class ExpertWeights:
    VC = 1

    def __init__(self, nc, ctx, a):
        sb = lambda name, shape, dt=F32: ctx.enter_context(nc.sbuf_tensor(name, shape, dt))
        sem = lambda name: ctx.enter_context(nc.semaphore(name))
        self.a = a
        self.raw_gu, self.raw_d = sb("raw_gu", [P, NWB * DC, 2 * I]), sb("raw_d", [IH, NWB * 2, D])
        self.gu = [sb(f"wgu_{h}", [P, NWB * DC, 2 * I], F32R) for h in ("high", "low")]
        self.d = [sb(f"wd_{h}", [IH, NWB * 2, D], F32R) for h in ("high", "low")]
        self.s_landing = [sem(f"w_landing{u}") for u in range(NWB)] + [sem("w_landing")]
        self.s_raw, self.s_high_gu, self.s_high_d = sem("w_raw"), sem("w_high_gu"), sem("w_high_d")
        self.s_low_v, self.s_low_p = sem("w_low_v"), sem("w_low_p")

    def load(self, eng, n, buf, landing):
        eng.dma_start(self.raw_gu[:, bass.ds(buf * DC, DC), :], self.a["exp_gu"][n]).then_inc(landing, 16)
        eng.dma_start(self.raw_d[:, bass.ds(buf * 2, 2), :], self.a["exp_d"][n]).then_inc(landing, 16)

    def landed(self, eng, landing, loads):
        eng.wait_ge(landing, loads * 32)
        eng.sem_inc(self.s_raw, 1)

    def high_gu(self, eng, n, buf):
        eng.wait_ge(self.s_raw, n + 1)
        at = bass.ds(buf * DC, DC)
        eng.activation(self.gu[0][:, at, :], self.raw_gu[:, at, :], ACT.Copy).then_inc(self.s_high_gu, 1)

    def high_d(self, eng, n, buf):
        eng.wait_ge(self.s_raw, n + 1)
        at = bass.ds(buf * 2, 2)
        eng.activation(self.d[0][:, at, :], self.raw_d[:, at, :], ACT.Copy).then_inc(self.s_high_d, 1)

    def low_v(self, eng, n, buf):
        eng.wait_ge(self.s_high_gu, n + 1)
        at = bass.ds(buf * DC, self.VC)
        eng.tensor_tensor(self.gu[1][:, at, :], self.raw_gu[:, at, :], self.gu[0][:, at, :].bitcast(F32), ALU.subtract).then_inc(self.s_low_v, 1)

    def low_p(self, eng, n, buf):
        eng.wait_ge(self.s_high_gu, n + 1)
        at = bass.ds(buf * DC + self.VC, DC - self.VC)
        eng.tensor_tensor(self.gu[1][:, at, :], self.raw_gu[:, at, :], self.gu[0][:, at, :].bitcast(F32), ALU.subtract).then_inc(self.s_low_p, 1)
        eng.wait_ge(self.s_high_d, n + 1)
        at = bass.ds(buf * 2, 2)
        eng.tensor_tensor(self.d[1][:, at, :], self.raw_d[:, at, :], self.d[0][:, at, :].bitcast(F32), ALU.subtract).then_inc(self.s_low_p, 1)

    def raw_free(self, eng, n, s_apart):
        eng.wait_ge(self.s_low_v, n + 1)
        apart(eng, s_apart)
        eng.wait_ge(self.s_low_p, n * 2 + 2)
        apart(eng, s_apart)

    def ready_gu(self, eng, n):
        eng.wait_ge(self.s_low_v, n + 1)
        eng.wait_ge(self.s_low_p, n * 2 + 1)

    def ready_d(self, eng, n):
        eng.wait_ge(self.s_low_p, n * 2 + 2)


def used_groups(eng, endb):
    end = eng.value_load(endb[0:1, E - 1:E], min_val=T * K // P, max_val=NBLK)
    return eng.snap((end + GB - 1) // GB, min_val=T * K // P // GB, max_val=NBLK // GB)


def norm_scales(nc, ctx, name, eng, link, mv, lnp, s_var, s_root):
    link(eng.tensor_scalar_add(mv[:, :, 1], mv[:, :, 1], LN_EPS))
    eng.sem_inc(s_var, 1)
    eng.wait_ge(s_root, 1)
    link(eng.reciprocal(lnp[:, :, 0], lnp[:, :, 0]))
    link(eng.scalar_tensor_tensor(lnp[:, :, 1], mv[:, :, 0], -1.0, lnp[:, :, 0], ALU.mult, ALU.mult))


def experts(nc, h_dram, y_dram, W, Wgu, low_bits, s_ffn, blk_tok, endb, blk_tab, ident):
    with ExitStack() as ctx:
        sb = lambda name, shape, dt=F32: ctx.enter_context(nc.sbuf_tensor(name, shape, dt))
        ps = lambda name, shape, dt=F32: ctx.enter_context(nc.psum_tensor(name, shape, dt))
        sem = lambda name: ctx.enter_context(nc.semaphore(name))
        idx = [sb(f"idx{u}", [P, 1], U32) for u in range(GB)]
        xg, xT = sb("xg", [P, GB, D]), [sb(f"bxT{h}", [P, 2, DC, P], F32R) for h in "hl"]
        act_g, hid, hidT, y = sb("act_g", [P, 2, I]), sb("hid", [P, 2, I]), [sb(f"hidT{h}", [IH, 2, 2, P], F32R) for h in "hl"], sb("y", [P, 2, D])
        px, pg, ph, py = [[ps(f"m_{n}{i}", [P, D]) for i in range(2)] for n in ("x", "g", "h", "y")]
        s_g, s_apart = [sem(f"m_g{u}") for u in range(GB)], sem("m_apart")
        s_y = [sem(f"m_y{u}") for u in range(2)]
        peX, pe = Steps(nc, ctx, "m_peX", ["xT"]), Steps(nc, ctx, "m_pe", ["hT", "y"])
        peG = Steps(nc, ctx, "m_peG", ["g"])
        dveX, dveH, dveT = Steps(nc, ctx, "m_dveX", ["xTl"]), Steps(nc, ctx, "m_dveH", ["h"]), Steps(nc, ctx, "m_dveT", ["hTh", "hTl"])
        actX = Steps(nc, ctx, "m_actX", ["xTh"])
        actS, actY = Steps(nc, ctx, "m_actS", ["silu"]), Steps(nc, ctx, "m_actY", ["y"])
        poolI = Steps(nc, ctx, "m_poolI", ["idx"])
        dveB = Steps(nc, ctx, "m_dveB", ["bits"])
        block = ctx.enter_context(nc.Block())
        THREE = ((0, 0), (0, 1), (1, 0))

        def entry(eng, b):
            e = eng.value_load(blk_tab[0:1, bass.ds(b * 2 + 2, 1)], min_val=0, max_val=E - 1)
            return e, eng.snap(e % NWB, min_val=0, max_val=NWB - 1)

        def begun(eng, b, most=E - NWB):
            return eng.value_load(blk_tab[0:1, bass.ds(b * 2 + 3, 1)], min_val=0, max_val=most)

        def split_next(eng, e, first, *parts):
            with eng.If(e > 0):
                n = e + (NWB - 1)
                pe.wait(eng, first - 1, "y")
                for part in parts:
                    part(eng, n, n % NWB)

        @block.sync
        def _(eng):
            def one(b, u):
                e = begun(eng, b)
                actY.wait(eng, b, "y")
                eng.dma_start(y_dram[bass.ts(b, P), :], y[:, u % 2, :]).then_inc(s_y[u % 2], 16)
                with eng.If(e > 0):
                    with eng.If(e < E - NWB):
                        W.landed(eng, W.s_landing[NWB], e + 1)
                        with eng.If(e < E - NWB - 1):
                            W.raw_free(eng, e + 1, s_apart)
                            W.load(eng, begun(eng, b, E - NWB - 2) + (NWB + 1), (e + 1) % NWB, W.s_landing[NWB])

            groups = used_groups(eng, endb)
            with eng.Fori(0, NBLK // GB) as i:
                with eng.If(i < groups):
                    for u in range(GB):
                        one(i * GB + u, u)
            for u in range(2):
                eng.wait_ge(s_y[u], groups * 32)
            apart(eng, s_apart)

        @block.gpsimd
        def _(eng):
            poolI.start(eng)

            def gather(b, u):
                poolI.done(eng.tensor_copy(idx[u][:, :], blk_tok[:, bass.ds(b, 1)]), "idx")
                poolI.wait(eng, b, "idx")
                peX.wait(eng, b - GB, "xT")
                apart(eng, s_apart)
                eng.indirect_dma_start(xg[:, u, :], None, h_dram, bass.IndirectOffsetOnAxis(ap=idx[u][:, 0:1], axis=0)).then_inc(s_g[u], 16)

            groups = used_groups(eng, endb)
            for u in range(GB):
                gather(u, u)
            with eng.Fori(0, NBLK // GB) as i:
                with eng.If(i < groups):
                    for u in range(GB):
                        eng.wait_ge(s_g[u], (i + 1) * 16)
                        gather((i + 1) * GB + u, u)
                        first = i * GB + u - 1
                        split_next(eng, begun(eng, first), first, W.low_p)
            for u in range(GB):
                eng.wait_ge(s_g[u], (groups + 1) * 16)
            apart(eng, s_apart)

        @block.tensor
        def _(eng):
            peX.start(eng)
            peG.start(eng)
            pe.start(eng)

            def turn(b, u, n):
                eng.wait_ge(s_g[u], n * 16)
                dveX.wait(eng, b - 2, "xTl")
                for c in range(DC):
                    m = eng.transpose(px[u % 2][:, bass.ts(c, P)], xg[:, u, bass.ts(c, P)], ident[:, :])
                peX.done(m, "xT")

            def products(out, left, right, chunks):
                for c in range(chunks):
                    for n, (l, r) in enumerate(THREE):
                        m = eng.matmul(out, left[l](c), right[r](c), start=c == 0 and n == 0, stop=c == chunks - 1 and n == 2)
                return m

            def needs(b, e):
                return [(sem, eng.snap(value)) for sem, value in ((W.s_low_v, e + 1), (W.s_low_p, e * 2 + 1), (dveX.sem, dveX.value(b, "xTl")))]

            def gate_up(b, u, e, buf, needed):
                for sem, value in needed:
                    eng.wait_ge(sem, value)
                m = products(pg[u % 2][:, 0:2 * I], [lambda c, x=x: x[:, u % 2, c, :] for x in xT],
                             [lambda c, w=w: w[:, buf * DC + c, :] for w in W.gu], DC)
                peG.done(m, "g")

            turn(0, 0, 1)
            turn(1, 1, 1)
            e, buf = entry(eng, 0)
            gate_up(0, 0, e, buf, needs(0, e))

            def one(i, u, this, following):
                b, par = i * GB + u, u % 2
                needed = needs(b + 1, following[0])
                dveH.wait(eng, b, "h")
                dveT.wait(eng, b - 2, "hTl")
                for c in range(2):
                    m = eng.transpose(ph[par][0:IH, bass.ts(c, P)], hid[:, par, bass.ts(c, IH)], ident[:, :])
                pe.done(m, "hT")
                turn(b + 2, (u + 2) % GB, i + 1 + (u + 2) // GB)
                gate_up(b + 1, (u + 1) % GB, *following, needed)
                if u > 0:
                    after = entry(eng, b + 2) if u < GB - 1 else None
                e, buf = entry(eng, b) if this is None else this
                W.ready_d(eng, e)
                dveT.wait(eng, b, "hTl")
                actY.wait(eng, b - 2, "y")
                m = products(py[par][:, :], [lambda c, x=x: x[:, par, c, :] for x in hidT],
                             [lambda c, w=w: w[:, buf * 2 + c, :] for w in W.d], 2)
                pe.done(m, "y")
                if u == 0:
                    after = entry(eng, b + 2)
                return following, after

            groups = used_groups(eng, endb)
            with eng.Fori(0, NBLK // GB) as i:
                with eng.If(i < groups):
                    this, following = None, entry(eng, i * GB + 1)
                    for u in range(GB):
                        this, following = one(i, u, this, following)

        @block.vector
        def _(eng):
            dveX.start(eng)
            dveH.start(eng)
            dveT.start(eng)
            eng.sem_inc(dveB.sem, dveB.lag - 1)

            def halves(step, unit, name, high, low, value):
                step.done(eng.tensor_copy(high, value), name + "h")
                step.wait(eng, unit, name + "h")
                step.done(eng.tensor_tensor(low, value, high.bitcast(F32), ALU.subtract), name + "l")

            def turned(b, u):
                actX.wait(eng, b, "xTh")
                peG.wait(eng, b - 2, "g")
                dveX.done(eng.tensor_tensor(xT[1][:, u % 2, :, :], px[u % 2][:, :].rearrange("p (c n) -> p c n", c=DC),
                                            xT[0][:, u % 2, :, :].bitcast(F32), ALU.subtract), "xTl")

            def hidden(b, u):
                actS.wait(eng, b, "silu")
                pe.wait(eng, b - 2, "hT")
                dveH.done(eng.tensor_tensor(hid[:, u % 2, :], pg[u % 2][:, I:2 * I], act_g[:, u % 2, :], ALU.mult), "h")

            all_bits = Wgu[:, :, :, :].rearrange("p n c f -> p (n c f)").bitcast(I32)
            dveB.done(eng.memset(low_bits[:, :], 0), "bits")
            eng.wait_ge(s_ffn, 32)
            turned(0, 0)
            turned(1, 1)
            hidden(0, 0)

            def one(b, u):
                e = begun(eng, b - 1)
                pe.wait(eng, b, "hT")
                pe.wait(eng, b - 2, "y")
                halves(dveT, b, "hT", hidT[0][:, u % 2, :, :], hidT[1][:, u % 2, :, :], ph[u % 2][0:IH, 0:2 * P].rearrange("p (c n) -> p c n", c=2))
                split_next(eng, e, b - 1, W.low_v)
                turned(b + 2, u + 2)
                hidden(b + 1, u + 1)

            groups = used_groups(eng, endb)
            with eng.Fori(0, NBLK // GB) as i:
                with eng.If(i < groups):
                    for u in range(GB):
                        one(i * GB + u, u)
                    with eng.If(i < 2 * FC):
                        dveB.wait(eng, i - 1, "bits")
                        dveB.done(eng.tensor_tensor(low_bits[:, :], low_bits[:, :], all_bits[:, bass.ts(eng.snap(i % (2 * FC), min_val=0, max_val=2 * FC - 1), D)], ALU.bitwise_or), "bits")

        @block.scalar
        def _(eng):
            actS.start(eng)
            actY.start(eng)
            actX.start(eng)

            def silu(b, u):
                peG.wait(eng, b, "g")
                dveH.wait(eng, b - 2, "h")
                actS.done(eng.activation(act_g[:, u % 2, :], pg[u % 2][:, 0:I], ACT.Silu), "silu")

            def turned(b, u):
                peX.wait(eng, b, "xT")
                peG.wait(eng, b - 2, "g")
                actX.done(eng.activation(xT[0][:, u % 2, :, :], px[u % 2][:, :].rearrange("p (c n) -> p c n", c=DC), ACT.Copy), "xTh")

            def one(b, u, before, stored):
                turned(b + 2, u + 2)
                silu(b + 1, u + 1)
                e = begun(eng, b)
                split_next(eng, before, b - 1, W.high_d)
                split_next(eng, e, b, W.high_gu)
                pe.wait(eng, b, "y")
                if stored is not None:
                    eng.wait_ge(s_y[u % 2], stored)
                actY.done(eng.activation(y[:, u % 2, :], py[u % 2][:, :], ACT.Copy), "y")
                return e

            turned(0, 0)
            turned(1, 1)
            silu(0, 0)
            groups = used_groups(eng, endb)
            before = begun(eng, -1)
            for u in range(GB):
                before = one(u, u, before, None if u < 2 else 16)
            with eng.Fori(1, NBLK // GB) as i:
                with eng.If(i < groups):
                    before = begun(eng, i * GB - 1)
                    for u in range(GB):
                        before = one(i * GB + u, u, before, i * 32 + u // 2 * 16)


def finish(nc, a, out, y_dram, X, spare, slot8, w8, Wgu, Wdn, low_bits, s_ffn, ident):
    TI, fs = range(TPB), range(FC)
    downs = [(i, f) for i in TI for f in fs]
    TURN_AT = FC + 5
    ADDS = {0: 2, 1: 1, 2: 2, 3: 2, 5: 2, 6: 2, 7: 1, 8: 2, FC: 2}
    GATHERS = {1: 1, 2: 1, 4: 1, 5: 1, 6: 1, 8: 1, 9: 1, 10: 1}
    with ExitStack() as ctx:
        sb = lambda name, shape, dt=F32: ctx.enter_context(nc.sbuf_tensor(name, shape, dt))
        ps = lambda name, shape, dt=F32: ctx.enter_context(nc.psum_tensor(name, shape, dt))
        sem = lambda name: ctx.enter_context(nc.semaphore(name))
        idx = [[sb(f"cidx{i}_{k}", [P, 1], U32) for k in range(K)] for i in TI]
        G = sb("G", [P, TPB, K, D])
        memT, mem = sb("memT_sb", [P, DC, S]), sb("mem_sb", [P, TPB, D])
        open8, neg, valid = sb("mask_b", [P, B, S], U8), sb("neg", [P, S]), sb("valid", [P, B])
        stats, mv, lnp = sb("n_stats", [P, TPB, 6]), sb("n_mv", [P, TPB, 2]), sb("n_lnp", [P, TPB, 2])
        stats4, mv4, lnp4 = sb("n_stats4", [P, TPB, 6]), sb("n_mv4", [P, TPB, 2]), sb("n_lnp4", [P, TPB, 2])
        xn = spare[0].rearrange("p (i d) -> p i d", i=TPB)
        x3T = spare[1].rearrange("p (i c n) -> p i c n", i=TPB, c=DC)
        x4T = [sb(f"x4T_{h}", [P, DC, S], F32R) for h in ("high", "low")]
        score, nmax, tot, inv = sb("score", [P, TPB, S]), sb("nmax", [P, TPB, 2]), sb("mtot", [P, TPB]), sb("minv", [P, TPB])
        pr, prT = sb("mp", [P, TPB, S]), sb("mpT", [P, TPB, TPB, P])
        gs, us, ds_ = sb("gate_s", [P, FC]), sb("up_s", [P, FC]), sb("down_s", [P, D])
        gl, hid, o = sb("gl", [P, 2, S]), sb("f_hid", [P, 2, S]), sb("f_o", [P, TPB, D])
        hT = [sb(f"hT_{h}", [P, FC, S], F32R) for h in ("high", "low")]
        ones, minus_half = sb("f_ones", [P, 1]), sb("minus_half", [P, TPB])
        odd_f, odd, exact = sb("odd_f", [P, D]), sb("odd", [P, 2]), sb("exact", [1, 2], I32)
        px, pgu, py = [[ps(f"f_{n}{i}", [P, D]) for i in range(2)] for n in ("x", "g", "y")]
        psc, ppT = ps("f_sc", [P, TPB, S]), ps("f_pT", [P, TPB, S])
        s_g, s_m, s_s, s_apart = [[sem(f"f_g{i}_{k}") for k in range(K)] for i in TI], sem("f_m"), sem("f_s"), sem("f_apart")
        s_mem, s_o = sem("f_mem"), [sem(f"f_o{i}") for i in TI]
        s_rounded_gu, s_rounded_d, s_odd, s_sum, s_exact = sem("f_rounded_gu"), sem("f_rounded_d"), sem("f_odd"), sem("f_sum"), sem("f_exact")
        each = lambda *names: [f"{n}{i}" for n in names for i in TI]
        poolA, poolH = Steps(nc, ctx, "f_poolA", [f"idx{k}_{i}" for k in range(K) for i in TI]), Steps(nc, ctx, "f_poolH", [f"l{f}" for f in fs])
        poolR, poolR4 = Steps(nc, ctx, "f_poolR", ["eps", "rstd"]), Steps(nc, ctx, "f_poolR4", ["eps4", "rstd4"])
        peC = Steps(nc, ctx, "f_peC", each("x3T", "s", "pT", "r", "x4T"))
        peG, peY = Steps(nc, ctx, "f_peG", [f"g{f}" for f in fs]), Steps(nc, ctx, "f_peY", each("y"))
        dveA = Steps(nc, ctx, "f_dveA", [f"k{k}_{i}" for k in range(K) for i in TI] + each("st", "mv") + ["shift"])
        dveC = Steps(nc, ctx, "f_dveC", ["neg"] + each("sc", "max", "nmax", "inv", "invv", "x", "st4", "mv4") + ["shift4"] + each("x4Tl"))
        dveH = Steps(nc, ctx, "f_dveH", [f"h{f}" for f in fs])
        dveY = Steps(nc, ctx, "f_dveY", [n for i in TI for n in (f"s{i}", f"o{i}")])
        actC = Steps(nc, ctx, "f_actC", each("n", "x3T", "e", "pT") + each("n4_", "x4Th"))
        actG, actH = Steps(nc, ctx, "f_actG", [f"g{f}" for f in fs]), Steps(nc, ctx, "f_actH", [f"h{f}" for f in fs])
        block = ctx.enter_context(nc.Block())

        def load_exact(eng, n):
            eng.wait_ge(s_exact, n + 1)
            apart(eng, s_apart)
            return eng.value_load(exact[0:1, n:n + 1], min_val=0, max_val=1)

        def by_batch(eng, one):
            with eng.Fori(0, B - 2) as b:
                one(b, True, True)
            one(B - 2, True, False)
            one(B - 1, False, False)

        @block.sync
        def _(eng):
            eng.dma_start(open8[:, :, :], a["mask"].unsqueeze(0).to_broadcast([P, B, S])).then_inc(s_m, 16)
            for s in s_o:
                eng.sem_inc(s, 16)

            def load(b):
                eng.dma_start(memT[:, :, :], a["memT"][:, b, :, :]).then_inc(s_mem, 16)
                eng.dma_start(mem[:, :, :], a["mem"][:, bass.ts(b, TPB), :]).then_inc(s_mem, 16)

            load(0)
            eng.dma_start(Wdn[0][:, :, :], a["ffn_dT"]).then_inc(s_ffn, 16)
            eng.dma_start(gs[:, :], a["gate_s"]).then_inc(s_s, 16)
            eng.dma_start(us[:, :], a["up_s"]).then_inc(s_s, 16)
            eng.dma_start(ds_[:, :], a["down_s"].unsqueeze(0).to_broadcast([P, D])).then_inc(s_s, 16)
            peC.wait(eng, 0, f"r{TPB - 1}")
            load(1)

            def one(b, more, more2):
                if more2:
                    peC.wait(eng, b + 1, f"r{TPB - 1}")
                    load(b + 2)
                for i in TI:
                    dveY.wait(eng, b, f"o{i}")
                    eng.dma_start(out[bass.ts(b * TPB + i, P), :], o[:, i, :]).then_inc(s_o[i], 16)

            by_batch(eng, one)
            for s in s_o:
                eng.wait_ge(s, 16 * (B + 1))

        @block.gpsimd
        def _(eng):
            for x in (poolA, poolH, poolR, poolR4):
                x.start(eng)

            places = [(i, k) for k in range(K) for i in TI]

            def gather(b, which, first=False):
                for i, k in which:
                    if not first:
                        dveA.wait(eng, b - 1, f"k{k}_{i}")
                    poolA.done(eng.tensor_copy(idx[i][k][:, :], slot8[:, b * TPB + i, k:k + 1]), f"idx{k}_{i}")
                for i, k in which:
                    poolA.wait(eng, b, f"idx{k}_{i}")
                    apart(eng, s_apart)
                    eng.indirect_dma_start(G[:, i, k, :], None, y_dram,
                                           bass.IndirectOffsetOnAxis(ap=idx[i][k][:, 0:1], axis=0)).then_inc(s_g[i][k], 16)

            def low(b, f):
                actH.wait(eng, b, f"h{f}")
                poolH.done(eng.tensor_tensor(hT[1][:, f, :], hid[:, f % 2, :], hT[0][:, f, :].bitcast(F32), ALU.subtract), f"l{f}")

            Chain(nc, ctx, "f_poolc", eng)(eng.memset(minus_half[:, :], -0.5))

            def deviations(b, step, written, tag, m, ln):
                written.wait(eng, b, f"mv{tag}{TPB - 1}")
                apart(eng, s_apart)
                step.done(eng.tensor_scalar_add(ln[:, :, 0], m[:, :, 1], LN_EPS), "eps" + tag)
                step.wait(eng, b, "eps" + tag)
                step.done(eng.tensor_tensor(ln[:, :, 0], ln[:, :, 0], minus_half[:, :], ALU.pow), "rstd" + tag)

            def deviations_a(b):
                deviations(b, poolR, dveA, "", mv, lnp)

            def deviations_4(b):
                deviations(b, poolR4, dveC, "4", mv4, lnp4)

            gather(0, places, first=True)
            deviations_a(0)
            gather(1, places[:6])
            deviations_4(0)
            gather(1, places[6:])
            deviations_a(1)
            gather(2, places)

            def one(b, more, more2, more3):
                n = 0
                for f in fs:
                    low(b, f)
                    if more3:
                        gather(b + 3, places[n:n + GATHERS.get(f, 0)])
                        n += GATHERS.get(f, 0)
                if more:
                    deviations_4(b + 1)
                if more3:
                    gather(b + 3, places[n:-2])
                if more2:
                    deviations_a(b + 2)
                if more3:
                    gather(b + 3, places[-2:])

            with eng.Fori(0, B - 3) as b:
                one(b, True, True, True)
            for b in range(B - 3, B):
                one(b, b < B - 1, b < B - 2, False)

        @block.tensor
        def _(eng):
            for x in (peC, peG, peY):
                x.start(eng)

            def turn(b, step, ready):
                for i in TI:
                    actC.wait(eng, b, f"{ready}{i}")
                    if step == "x3T":
                        dveC.wait(eng, b - 1, f"x4Tl{i}")
                    else:
                        dveC.wait(eng, b, f"x{i}")
                    for c in range(DC):
                        m = eng.transpose(px[i][:, bass.ts(c, P)], xn[:, i, bass.ts(c, P)], ident[:, :])
                    peC.done(m, f"{step}{i}")

            def scores(b):
                eng.wait_ge(s_mem, (b + 1) * 32)
                for i in TI:
                    actC.wait(eng, b, f"x3T{i}")
                    dveC.wait(eng, b - 1, f"sc{TPB - 1}")
                    for c in range(DC):
                        m = eng.matmul(psc[:, i, :], x3T[:, i, c, :], memT[:, c, :], start=c == 0, stop=c == DC - 1)
                    peC.done(m, f"s{i}")

            def turn_probs(b):
                for i in TI:
                    actC.wait(eng, b, f"e{i}")
                    actC.wait(eng, b - 1, f"pT{TPB - 1}")
                    for kt in range(TPB):
                        m = eng.transpose(ppT[:, i, bass.ts(kt, P)], pr[:, i, bass.ts(kt, P)], ident[:, :])
                    peC.done(m, f"pT{i}")

            def read(b):
                for i in TI:
                    actC.wait(eng, b, f"pT{i}")
                    for kt in range(TPB):
                        m = eng.matmul(px[i][:, :], prT[:, i, kt, :], mem[:, kt, :], start=kt == 0, stop=kt == TPB - 1)
                    peC.done(m, f"r{i}")

            def sum_odd(n):
                eng.wait_ge(s_odd, n + 1)
                eng.matmul(psc[0:1, 0, 0:1], odd[:, n:n + 1], ones[:, :], start=True, stop=True).then_inc(s_sum, 1)
                return load_exact(eng, n)

            exact_gu = sum_odd(0)
            turn(0, "x3T", "n")
            scores(0)
            turn_probs(0)
            read(0)
            exact_d = sum_odd(1)
            turn(0, "x4T", "n4_")
            eng.wait_ge(s_rounded_gu, 1)

            def gate_up(b, more, way):
                beside = {2: lambda: turn(b + 1, "x3T", "n"), 4: lambda: scores(b + 1), 7: lambda: turn_probs(b + 1), 9: lambda: read(b + 1)}
                for f in fs:
                    if more and f in beside:
                        beside[f]()
                    if f < 2:
                        dveH.wait(eng, b - 1, f"h{FC - 2 + (f + 1) % 2}")
                    else:
                        dveH.wait(eng, b, f"h{f - 2}")
                    for n in range(2):
                        for c in range(DC):
                            for part, x in enumerate(x4T):
                                m = eng.matmul(pgu[f % 2][:, bass.ts(n, S)], Wgu[way][:, n, c, bass.ts(f, P)], x[:, c, :].bitcast((F32, F32R)[way]),
                                               start=c == 0 and part == 0, stop=c == DC - 1 and part == 1)
                    peG.done(m, f"g{f}")

            def down(b, more, way):
                eng.wait_ge(s_rounded_d, 1)
                for at, (i, f) in enumerate(downs):
                    if more and at == TURN_AT:
                        turn(b + 1, "x4T", "n4_")
                    if f == 0:
                        dveY.wait(eng, b - 1, f"s{i}")
                    if i == 0:
                        poolH.wait(eng, b, f"l{f}")
                    for part, h in enumerate(hT):
                        m = eng.matmul(py[i][:, :], h[:, f, bass.ts(i, P)].bitcast((F32, F32R)[way]), Wdn[way][:, f, :],
                                       start=f == 0 and part == 0, stop=f == FC - 1 and part == 1)
                    if f == FC - 1:
                        peY.done(m, f"y{i}")

            def one(b, more):
                dveC.wait(eng, b, f"x4Tl{TPB - 1}")
                apart(eng, s_apart)
                for product, exactly in ((gate_up, exact_gu), (down, exact_d)):
                    at = [x.at for x in (peC, peG, peY)]
                    with eng.If(exactly > 0):
                        product(b, more, 1)
                    for x, n in zip((peC, peG, peY), at):
                        x.at = n
                    with eng.If(exactly < 1):
                        product(b, more, 0)

            with eng.Fori(0, B - 1) as b:
                one(b, True)
            one(B - 1, False)

        @block.vector
        def _(eng):
            for x in (dveA, dveC, dveH, dveY):
                x.start(eng)
            link = Chain(nc, ctx, "f_link", eng)
            link(eng.memset(ones[:, :], 1.0))
            eng.wait_ge(s_m, 16)
            link(eng.tensor_reduce(valid[:, :], open8[:, :, :], axis=AX.X, op=ALU.max))

            def add_expert(b, i, k):
                t = b * TPB + i
                if k > 0:
                    dveA.wait(eng, b, f"k{k - 1}_{i}")
                eng.wait_ge(s_g[i][k], (b + 1) * 16)
                dveA.done(eng.scalar_tensor_tensor(X[:, t, :], G[:, i, k, :], w8[:, t, k:k + 1], X[:, t, :], ALU.mult, ALU.add), f"k{k}_{i}")

            def moments(b, step, tag, last, written, st, m):
                for i in TI:
                    written.wait(eng, b, last.format(i))
                    apart(eng, s_apart)
                    step.done(eng.bn_stats(st[:, i, :], X[:, b * TPB + i, :]), f"st{tag}{i}")
                for i in TI:
                    step.wait(eng, b, f"st{tag}{i}")
                    apart(eng, s_apart)
                    step.done(eng.bn_aggr(m[:, i, :], st[:, i, :]), f"mv{tag}{i}")

            def scales(b, step, rstd, tag, m, ln):
                rstd.wait(eng, b, "rstd" + tag)
                step.done(eng.scalar_tensor_tensor(ln[:, :, 1], m[:, :, 0], -1.0, ln[:, :, 0], ALU.mult, ALU.mult), "shift" + tag)

            def moments_a(b):
                moments(b, dveA, "", f"k{K - 1}_{{}}", dveA, stats, mv)

            def scales_a(b):
                scales(b, dveA, poolR, "", mv, lnp)

            def negatives(b):
                dveC.wait(eng, b - 1, f"sc{TPB - 1}")
                dveC.done(eng.tensor_scalar(neg[:, :], open8[:, b, :], 1.0, 1e30, ALU.subtract, ALU.mult), "neg")

            def maxima(b):
                dveC.wait(eng, b, "neg")
                peC.wait(eng, b, f"s{TPB - 1}")
                for i in TI:
                    actC.wait(eng, b - 1, f"e{i}")
                    dveC.done(eng.scalar_tensor_tensor(score[:, i, :], psc[:, i, :], D ** -0.5, neg[:, :], ALU.mult, ALU.add), f"sc{i}")
                for i in TI:
                    dveC.wait(eng, b, f"sc{i}")
                    dveC.done(eng.tensor_reduce(nmax[:, i, 0:1], score[:, i, :], axis=AX.X, op=ALU.max), f"max{i}")
                for i in TI:
                    dveC.wait(eng, b, f"max{i}")
                    dveC.done(eng.tensor_scalar_mul(nmax[:, i, 1:2], nmax[:, i, 0:1], -1.0), f"nmax{i}")

            def inverses(b):
                for i in TI:
                    actC.wait(eng, b, f"e{i}")
                    dveC.done(eng.reciprocal(inv[:, i:i + 1], tot[:, i:i + 1]), f"inv{i}")
                for i in TI:
                    dveC.wait(eng, b, f"inv{i}")
                    dveC.done(eng.tensor_tensor(inv[:, i:i + 1], inv[:, i:i + 1], valid[:, bass.ds(b, 1)], ALU.mult), f"invv{i}")

            def add_read(b):
                for i in TI:
                    dveC.wait(eng, b, f"invv{i}")
                    peC.wait(eng, b, f"r{i}")
                    t = b * TPB + i
                    dveC.done(eng.scalar_tensor_tensor(X[:, t, :], px[i][:, :], inv[:, i:i + 1], X[:, t, :], ALU.mult, ALU.add), f"x{i}")
                moments(b, dveC, "4", "x{}", dveC, stats4, mv4)

            def scales_4(b):
                scales(b, dveC, poolR4, "4", mv4, lnp4)

            def low(b):
                for i in TI:
                    actC.wait(eng, b, f"x4Th{i}")
                    at = bass.ts(i, P)
                    dveC.done(eng.tensor_tensor(x4T[1][:, :, at], px[i][:, :].rearrange("p (c n) -> p c n", c=DC),
                                                x4T[0][:, :, at].bitcast(F32), ALU.subtract), f"x4Tl{i}")

            def store(b, i):
                peY.wait(eng, b, f"y{i}")
                eng.wait_ge(s_o[i], (b + 1) * 16)
                dveY.done(eng.tensor_tensor(o[:, i, :], py[i][:, :], ds_[:, :], ALU.mult), f"s{i}")
                dveY.wait(eng, b, f"s{i}")
                dveY.done(eng.tensor_tensor(o[:, i, :], o[:, i, :], X[:, b * TPB + i, :], ALU.add), f"o{i}")

            def find_exact(n):
                link(eng.tensor_scalar(low_bits[:, :], low_bits[:, :], LOW_BITS, None, ALU.bitwise_and))
                link(eng.tensor_copy(odd_f[:, :], low_bits[:, :]))
                link(eng.tensor_reduce(odd[:, n:n + 1], odd_f[:, :], axis=AX.X, op=ALU.max))
                eng.sem_inc(s_odd, 1)
                eng.wait_ge(s_sum, n + 1)
                link(eng.tensor_scalar(exact[:, n:n + 1], psc[0:1, 0, 0:1], 0.0, None, ALU.is_equal))
                eng.sem_inc(s_exact, 1)

            find_exact(0)
            adds = [(i, k) for k in range(K) for i in TI]
            for i, k in adds:
                add_expert(0, i, k)
            moments_a(0)
            scales_a(0)
            negatives(0)
            maxima(0)
            eng.wait_ge(s_ffn, 48)
            bits = [Wdn[0][:, f, :].bitcast(I32) for f in fs]
            for f in range(1, FC):
                link(eng.tensor_tensor(low_bits[:, :], bits[0] if f == 1 else low_bits[:, :], bits[f], ALU.bitwise_or))
            find_exact(1)
            inverses(0)
            add_read(0)
            scales_4(0)
            low(0)
            for i, k in adds:
                add_expert(1, i, k)
            moments_a(1)
            scales_a(1)
            eng.wait_ge(s_s, 48)

            def one(b, more, more2):
                beside = {1: negatives, 4: maxima, 7: inverses, 9: add_read, 10: scales_4}
                n = 0
                for f in fs:
                    actG.wait(eng, b, f"g{f}")
                    if f < 2:
                        poolH.wait(eng, b - 1, f"l{FC - 2 + (f + 1) % 2}")
                    else:
                        poolH.wait(eng, b, f"l{f - 2}")
                    dveH.done(eng.scalar_tensor_tensor(hid[:, f % 2, :], pgu[f % 2][:, S:2 * S], us[:, f:f + 1], gl[:, f % 2, :],
                                                       ALU.mult, ALU.mult), f"h{f}")
                    if more and f in beside:
                        beside[f](b + 1)
                    if more2:
                        for i, k in adds[n:n + ADDS.get(f, 0)]:
                            add_expert(b + 2, i, k)
                        n += ADDS.get(f, 0)
                if more2:
                    for i, k in adds[n:]:
                        add_expert(b + 2, i, k)
                    moments_a(b + 2)
                store(b, 0)
                if more:
                    low(b + 1)
                if more2:
                    scales_a(b + 2)
                store(b, 1)

            by_batch(eng, one)

        @block.scalar
        def _(eng):
            for x in (actC, actG, actH):
                x.start(eng)

            def norm(b, written, tag, ln, step):
                written.wait(eng, b, "shift" + tag)
                for i in TI:
                    if tag:
                        peC.wait(eng, b, f"x3T{i}")
                    else:
                        peC.wait(eng, b - 1, f"x4T{i}")
                    apart(eng, s_apart)
                    actC.done(eng.activation(xn[:, i, :], X[:, b * TPB + i, :], ACT.Identity, bias=ln[:, i, 1:2], scale=ln[:, i, 0:1]), f"{step}{i}")

            def norm_3(b):
                norm(b, dveA, "", lnp, "n")

            def turned_3(b):
                for i in TI:
                    peC.wait(eng, b, f"x3T{i}")
                    peC.wait(eng, b - 1, f"s{i}")
                    actC.done(eng.activation(x3T[:, i, :, :], px[i][:, :].rearrange("p (c n) -> p c n", c=DC), ACT.Copy), f"x3T{i}")

            def exps(b):
                for i in TI:
                    dveC.wait(eng, b, f"nmax{i}")
                    peC.wait(eng, b - 1, f"pT{i}")
                    dveC.wait(eng, b - 1, f"inv{i}")
                    actC.done(eng.activation(pr[:, i, :], score[:, i, :], ACT.Exp, bias=nmax[:, i, 1:2], accum_out=tot[:, i:i + 1]), f"e{i}")

            def turned_probs(b):
                peC.wait(eng, b, f"pT{TPB - 1}")
                for i in TI:
                    peC.wait(eng, b - 1, f"r{i}")
                    actC.done(eng.activation(prT[:, i, :, :], ppT[:, i, :].rearrange("p (c n) -> p c n", c=TPB), ACT.Copy), f"pT{i}")

            def norm_4(b):
                norm(b, dveC, "4", lnp4, "n4_")

            def high_4(b):
                for i in TI:
                    peC.wait(eng, b, f"x4T{i}")
                    actC.done(eng.activation(x4T[0][:, :, bass.ts(i, P)], px[i][:, :].rearrange("p (c n) -> p c n", c=DC), ACT.Copy), f"x4Th{i}")

            def high(b, f):
                dveH.wait(eng, b, f"h{f}")
                actH.done(eng.activation(hT[0][:, f, :], hid[:, f % 2, :], ACT.Copy), f"h{f}")

            def name_float32r(n, weights, done):
                with eng.If(load_exact(eng, n) > 0):
                    eng.activation(weights[1].ap(), weights[0].ap(), ACT.Copy)
                eng.sem_inc(done, 1)

            name_float32r(0, Wgu, s_rounded_gu)
            for stage in (norm_3, turned_3, exps, turned_probs):
                stage(0)
            name_float32r(1, Wdn, s_rounded_d)
            norm_4(0)
            high_4(0)
            eng.wait_ge(s_s, 48)

            def one(b, more, more2):
                beside = {0: norm_3, 2: turned_3, 5: exps, 7: turned_probs}
                for f in fs:
                    peG.wait(eng, b, f"g{f}")
                    if f < 2:
                        dveH.wait(eng, b - 1, f"h{FC - 2 + f}")
                    else:
                        dveH.wait(eng, b, f"h{f - 2}")
                    actG.done(eng.activation(gl[:, f % 2, :], pgu[f % 2][:, 0:S], ACT.Silu, scale=gs[:, f:f + 1]), f"g{f}")
                    if f > 0:
                        high(b, f - 1)
                    if more and f in beside:
                        beside[f](b + 1)
                high(b, FC - 1)
                if more:
                    norm_4(b + 1)
                if more:
                    high_4(b + 1)

            by_batch(eng, one)


def as_float32r_too(nc, ctx, name, shape):
    base = nc.sbuf_base
    whole = ctx.enter_context(nc.sbuf_tensor(name, shape, F32))
    assert nc.sbuf_base - base == int(np.prod(shape[1:])) * 4
    return whole, nc.alloc_sbuf_tensor_at(name + "_r", shape, F32R, offset=base)


def build(nc, a, out):
    h_dram = nc.dram_tensor("h_rows", (T, D), F32).ap()
    y_dram = nc.dram_tensor("y_rows", (NBLK * P, D), F32).ap()
    tab_dram = nc.dram_tensor("block_table", (NTAB, 2), I32).ap()
    with ExitStack() as ctx:
        sb = lambda name, shape, dt=F32, ctx=ctx: ctx.enter_context(nc.sbuf_tensor(name, shape, dt))
        X, ident = sb("X", [P, NT, D]), sb("ident", [P, P])
        slot8, w8 = sb("slot8", [P, NT, K], U32), sb("w8", [P, NT, K])
        blk_tok, endb, blk_tab = sb("blk_tok", [P, NTAB], U32), sb("endb", [P, E], I32), sb("blk_tab", [1, 2 * NTAB], I32)
        spare, m8 = [sb(f"spare{i}", [P, NT * E])[:, :] for i in range(2)], sb("m8", [P, NT, K])
        L, mask = [x.rearrange("p (t e) -> p t e", t=NT) for x in spare]
        low_bits = sb("low_bits", [P, D], I32)
        with ExitStack() as first:
            qT, kT, V = sb("qT", [P, DC, T], ctx=first), sb("kT", [P, DC, T], ctx=first), sb("V", [P, NT, D], ctx=first)
            project(nc, a["x"], a["ctxT"], a["attn_wT"], a["rows"], X, qT, kT, V, ident)
            attend(nc, qT, kT, V, ident, y_dram)
            route(nc, a, h_dram, X, qT, L, mask, m8, ident)
        Wgu = as_float32r_too(nc, ctx, "ffn_gu", [P, 2, DC, F])
        s_ffn = ctx.enter_context(nc.semaphore("s_ffn"))
        with ExitStack() as moe:
            W = ExpertWeights(nc, moe, a)
            place(nc, a, W, Wgu[0], s_ffn, L, mask, m8, slot8, w8, blk_tok, endb, blk_tab, tab_dram)
            experts(nc, h_dram, y_dram, W, Wgu[0], low_bits, s_ffn, blk_tok, endb, blk_tab, ident)
        Wdn = as_float32r_too(nc, ctx, "ffn_d", [P, FC, D])
        finish(nc, a, out, y_dram, X, spare, slot8, w8, Wgu, Wdn, low_bits, s_ffn, ident)


def lay_out(i):
    f = {k: np.ascontiguousarray(v) for k, v in i.items()}
    chunks = lambda wT: np.ascontiguousarray(wT.reshape(-1, P, wT.shape[-1]).transpose(1, 0, 2))
    tok = f["ctx_2048"].reshape(NT, P, DC, P)
    mem = f["ctx_2048"].reshape(B, S, DC, P)
    gu = np.concatenate([f["L0_ffn_w_gate"], f["L0_ffn_w_up"]], axis=2)
    return {
        "x": f["x"].reshape(T, D),
        "ctxT": np.ascontiguousarray(tok.transpose(0, 3, 2, 1)),
        "attn_wT": np.stack([chunks(f["L0_xattn_" + n + "_w"].T) for n in ("q", "k_img", "v_img", "o")]),
        "rows": np.stack([f["L0_xattn_" + n] for n in ("q_b", "norm_q_w", "k_img_b", "norm_k_img_w", "v_img_b", "o_b")]),
        "router_wT": chunks(f["L0_ffn_gate_weight"].T),
        "exp_gu": np.ascontiguousarray(gu.reshape(E, DC, P, 2 * I).transpose(0, 2, 1, 3)),
        "exp_d": np.ascontiguousarray(f["L0_ffn_w_down"].reshape(E, 2, IH, D).transpose(0, 2, 1, 3)),
        "memT": np.ascontiguousarray(mem.transpose(3, 0, 2, 1)),
        "mem": chunks(f["ctx_2048"].reshape(T, D)),
        "mask": f["mask_BxS2_bk0"],
        "ffn_gT": chunks(f["L1_ffn_gate_w"].T),
        "ffn_uT": chunks(f["L1_ffn_up_w"].T),
        "ffn_dT": chunks(f["L1_ffn_down_w"].T),
        "gate_s": np.ascontiguousarray(f["L1_ffn_gate_s"].reshape(FC, P).T),
        "up_s": np.ascontiguousarray(f["L1_ffn_up_s"].reshape(FC, P).T),
        "down_s": f["L1_ffn_down_s"],
    }


def kernel(**inputs):
    import concourse.bacc as bacc
    from concourse.bass_utils import run_bass_kernel_spmd

    arrays = lay_out(inputs)
    nc = bacc.Bacc("TRN2", target_bir_lowering=False, num_devices=1)
    a = {n: nc.dram_tensor("in_" + n, v.shape, mybir.dt.from_np(v.dtype), kind="ExternalInput").ap() for n, v in arrays.items()}
    out = nc.dram_tensor("out", (T, D), F32, kind="ExternalOutput").ap()
    build(nc, a, out)
    got = run_bass_kernel_spmd(nc, [{"in_" + n: v for n, v in arrays.items()}], core_ids=[0])
    return got.results[0]["out"].reshape(B, S, D)
```
